# Optimizing a Trainium2 kernel written in Bass

```python
import numpy as np
import jax
import jax.numpy as jnp

def _softmax(x, axis=-1):
    return jax.nn.softmax(x, axis=axis)

def _gelu(x):
    return jax.nn.gelu(x, approximate=True)

def _silu(x):
    return jax.nn.silu(x)

def _sigmoid(x):
    return jax.nn.sigmoid(x)

def _layernorm(x, axis=-1, eps=1e-05):
    m = jnp.mean(x, axis=axis, keepdims=True)
    v = jnp.var(x, axis=axis, keepdims=True)
    return (x - m) / jnp.sqrt(v + eps)

def _scatter_add(tgt, idx, src, axis=0):
    return tgt.at[idx].add(src)

def _segment_sum(src, seg, n):
    return jax.ops.segment_sum(src, seg, n)
kernel_name = 'mk_gps_d1_gnn_r8_3a47c1'

def setup_inputs(seed: int=0):
    np.random.seed(seed)
    _w = jnp.asarray

    def _rec_inputs():
        import jax
        import jax.numpy as jnp
        _gk = jax.random.key(seed)
        x = -0.0002117 + 1 * jax.random.normal(jax.random.fold_in(_gk, 1), (6250, 256), jnp.float32)
        src = jax.random.randint(jax.random.fold_in(_gk, 2), (200000,), 0, 6250, jnp.int32)
        dst = jnp.minimum((6250 * jax.random.uniform(jax.random.fold_in(_gk, 3), (200000,)) ** 2.0).astype(jnp.int32), 49999)
        _o = jnp.argsort(dst, stable=True)
        src = src[_o]
        dst = dst[_o]
        return (x, src, dst)
    x, src, dst = _rec_inputs()

    def _L0_gnn_setup():
        import jax, jax.numpy as jnp
        import numpy as np
        N_NODES = 12500
        N_EDGES = 200000
        D_IN = 256
        HEADS = 8
        D_HEAD = 32
        NEG_SLOPE = 0.2
        BN_EPS = 1e-05
        key = jax.random.key(seed)
        ks = jax.random.split(key, 8)
        x = jax.random.normal(ks[0], (N_NODES, D_IN), dtype=jnp.float32)
        edge_index = jax.random.randint(ks[1], (2, N_EDGES), 0, N_NODES, dtype=jnp.int32)
        W = jax.random.normal(ks[2], (D_IN, HEADS * D_HEAD), dtype=jnp.float32) / np.sqrt(D_IN)
        att_src = jax.random.normal(ks[3], (HEADS, D_HEAD), dtype=jnp.float32) / np.sqrt(D_HEAD)
        att_dst = jax.random.normal(ks[4], (HEADS, D_HEAD), dtype=jnp.float32) / np.sqrt(D_HEAD)
        bias = jax.random.normal(ks[5], (HEADS * D_HEAD,), dtype=jnp.float32) * 0.01
        gamma = jnp.ones((HEADS * D_HEAD,), dtype=jnp.float32)
        beta = jnp.zeros((HEADS * D_HEAD,), dtype=jnp.float32)
        return {'x': x, 'edge_index': edge_index, 'W': W, 'att_src': att_src, 'att_dst': att_dst, 'bias': bias, 'gamma': gamma, 'beta': beta}
    _L0_gnn_all = _L0_gnn_setup()
    _L0_gnn_in = {k: v for k, v in _L0_gnn_all.items() if k in ('W', 'att_src', 'att_dst', 'bias', 'gamma', 'beta')}
    del _L0_gnn_all

    def _L0_mix_setup():
        import jax, jax.numpy as jnp
        import numpy as np
        EMB, HEADS, DEPTH, SEQ, BATCH = (256, 8, 4, 1024, 4)
        DH = EMB // HEADS
        FF = 4 * EMB
        EPS = 1e-05

        def _layernorm(x, g, b):
            mu = x.mean(-1, keepdims=True)
            var = ((x - mu) ** 2).mean(-1, keepdims=True)
            return (x - mu) * jax.lax.rsqrt(var + EPS) * g + b

        def _linear_attn(x, Wq, Wk, Wv, Wo, bo):
            b, n, dm = x.shape
            split = lambda t: t.reshape(b, n, HEADS, DH).transpose(0, 2, 1, 3)
            scale = DH ** (-0.25)
            q = jax.nn.softmax(split(x @ Wq) * scale, axis=-1)
            k = jax.nn.softmax(split(x @ Wk) * scale, axis=-2)
            v = split(x @ Wv)
            context = jnp.einsum('bhnd,bhne->bhde', k, v)
            out = jnp.einsum('bhnd,bhde->bhne', q, context)
            out = out.transpose(0, 2, 1, 3).reshape(b, n, dm)
            return out @ Wo + bo

        def _forward(x, Wq, Wk, Wv, Wo, bo, ln1_g, ln1_b, W1, b1, W2, b2, ln2_g, ln2_b):
            for i in range(DEPTH):
                h = _layernorm(x, ln1_g[i], ln1_b[i])
                x = x + _linear_attn(h, Wq[i], Wk[i], Wv[i], Wo[i], bo[i])
                h = _layernorm(x, ln2_g[i], ln2_b[i])
                x = x + (jax.nn.gelu(h @ W1[i] + b1[i], approximate=False) @ W2[i] + b2[i])
            return x
        key = jax.random.key(seed)
        ks = jax.random.split(key, 8)
        w = lambda k, shape: jax.random.normal(k, shape, dtype=jnp.float32) * 0.02
        D = DEPTH
        return {'x': jax.random.normal(ks[0], (BATCH, SEQ, EMB), dtype=jnp.float32), 'Wq': w(ks[1], (D, EMB, EMB)), 'Wk': w(ks[2], (D, EMB, EMB)), 'Wv': w(ks[3], (D, EMB, EMB)), 'Wo': w(ks[4], (D, EMB, EMB)), 'bo': jnp.zeros((D, EMB), jnp.float32), 'ln1_g': jnp.ones((D, EMB), jnp.float32), 'ln1_b': jnp.zeros((D, EMB), jnp.float32), 'W1': w(ks[5], (D, EMB, FF)), 'b1': jnp.zeros((D, FF), jnp.float32), 'W2': w(ks[6], (D, FF, EMB)), 'b2': jnp.zeros((D, EMB), jnp.float32), 'ln2_g': jnp.ones((D, EMB), jnp.float32), 'ln2_b': jnp.zeros((D, EMB), jnp.float32)}
    _L0_mix_all = _L0_mix_setup()
    _L0_mix_in = {k: v for k, v in _L0_mix_all.items() if k in ('Wq', 'Wk', 'Wv', 'Wo', 'bo', 'ln1_g', 'ln1_b', 'W1', 'b1', 'W2', 'b2', 'ln2_g', 'ln2_b')}
    del _L0_mix_all

    def _L0_ffn_setup():
        import math
        import jax, jax.numpy as jnp
        import numpy as np
        CAPACITY_FACTOR = 1.25
        key = jax.random.key(seed)
        ks = jax.random.split(key, 5)
        B, L, D, F, E = (8, 1024, 256, 1024, 8)
        h = jax.random.normal(ks[0], (B, L, D), dtype=jnp.float32)
        gate_w = jax.random.normal(ks[1], (D, E), dtype=jnp.float32) * 0.02
        gate_b = jnp.zeros((E,), dtype=jnp.float32)
        w1 = jax.random.normal(ks[2], (E, D, F), dtype=jnp.float32) * (1.0 / math.sqrt(D))
        b1 = jnp.zeros((E, F), dtype=jnp.float32)
        w2 = jax.random.normal(ks[3], (E, F, D), dtype=jnp.float32) * (1.0 / math.sqrt(F))
        b2 = jnp.zeros((E, D), dtype=jnp.float32)
        return {'h': h, 'gate_w': gate_w, 'gate_b': gate_b, 'w1': w1, 'b1': b1, 'w2': w2, 'b2': b2}
    _L0_ffn_all = _L0_ffn_setup()
    _L0_ffn_in = {k: v for k, v in _L0_ffn_all.items() if k in ('gate_w', 'gate_b', 'w1', 'b1', 'w2', 'b2')}
    del _L0_ffn_all
    return {'x': x, 'src': src, 'dst': dst, 'L0_gnn_W': _L0_gnn_in['W'], 'L0_gnn_att_src': _L0_gnn_in['att_src'], 'L0_gnn_att_dst': _L0_gnn_in['att_dst'], 'L0_gnn_bias': _L0_gnn_in['bias'], 'L0_gnn_gamma': _L0_gnn_in['gamma'], 'L0_gnn_beta': _L0_gnn_in['beta'], 'L0_mix_Wq': _L0_mix_in['Wq'], 'L0_mix_Wk': _L0_mix_in['Wk'], 'L0_mix_Wv': _L0_mix_in['Wv'], 'L0_mix_Wo': _L0_mix_in['Wo'], 'L0_mix_bo': _L0_mix_in['bo'], 'L0_mix_ln1_g': _L0_mix_in['ln1_g'], 'L0_mix_ln1_b': _L0_mix_in['ln1_b'], 'L0_mix_W1': _L0_mix_in['W1'], 'L0_mix_b1': _L0_mix_in['b1'], 'L0_mix_W2': _L0_mix_in['W2'], 'L0_mix_b2': _L0_mix_in['b2'], 'L0_mix_ln2_g': _L0_mix_in['ln2_g'], 'L0_mix_ln2_b': _L0_mix_in['ln2_b'], 'L0_ffn_gate_w': _L0_ffn_in['gate_w'], 'L0_ffn_gate_b': _L0_ffn_in['gate_b'], 'L0_ffn_w1': _L0_ffn_in['w1'], 'L0_ffn_b1': _L0_ffn_in['b1'], 'L0_ffn_w2': _L0_ffn_in['w2'], 'L0_ffn_b2': _L0_ffn_in['b2']}

def reference(x, src, dst, L0_gnn_W, L0_gnn_att_src, L0_gnn_att_dst, L0_gnn_bias, L0_gnn_gamma, L0_gnn_beta, L0_mix_Wq, L0_mix_Wk, L0_mix_Wv, L0_mix_Wo, L0_mix_bo, L0_mix_ln1_g, L0_mix_ln1_b, L0_mix_W1, L0_mix_b1, L0_mix_W2, L0_mix_b2, L0_mix_ln2_g, L0_mix_ln2_b, L0_ffn_gate_w, L0_ffn_gate_b, L0_ffn_w1, L0_ffn_b1, L0_ffn_w2, L0_ffn_b2):
    import jax
    import jax.numpy as jnp

    def _L0_gnn_ref(x, edge_index, W, att_src, att_dst, bias, gamma, beta):
        import jax, jax.numpy as jnp
        import numpy as np
        N_NODES = 12500
        N_EDGES = 200000
        D_IN = 256
        HEADS = 8
        D_HEAD = 32
        NEG_SLOPE = 0.2
        BN_EPS = 1e-05
        N = x.shape[0]
        H, D = att_src.shape
        xh = (x @ W).reshape(N, H, D)
        a_src = jnp.einsum('nhd,hd->nh', xh, att_src)
        a_dst = jnp.einsum('nhd,hd->nh', xh, att_dst)
        loops = jnp.arange(N, dtype=edge_index.dtype)
        src = jnp.concatenate([edge_index[0], loops])
        dst = jnp.concatenate([edge_index[1], loops])
        e = jax.nn.leaky_relu(a_src[src] + a_dst[dst], NEG_SLOPE)
        m = jax.ops.segment_max(e, dst, num_segments=N)
        e = jnp.exp(e - m[dst])
        denom = jax.ops.segment_sum(e, dst, num_segments=N)
        alpha = e / denom[dst]
        msg = xh[src] * alpha[:, :, None]
        out = jax.ops.segment_sum(msg, dst, num_segments=N).reshape(N, H * D) + bias
        mean = jnp.mean(out, axis=0)
        var = jnp.var(out, axis=0)
        out = (out - mean) * jax.lax.rsqrt(var + BN_EPS) * gamma + beta
        return out + x

    def _L0_mix_ref(x, Wq, Wk, Wv, Wo, bo, ln1_g, ln1_b, W1, b1, W2, b2, ln2_g, ln2_b):
        import jax, jax.numpy as jnp
        import numpy as np
        EMB, HEADS, DEPTH, SEQ, BATCH = (256, 8, 4, 1024, 4)
        DH = EMB // HEADS
        FF = 4 * EMB
        EPS = 1e-05

        def _layernorm(x, g, b):
            mu = x.mean(-1, keepdims=True)
            var = ((x - mu) ** 2).mean(-1, keepdims=True)
            return (x - mu) * jax.lax.rsqrt(var + EPS) * g + b

        def _linear_attn(x, Wq, Wk, Wv, Wo, bo):
            b, n, dm = x.shape
            split = lambda t: t.reshape(b, n, HEADS, DH).transpose(0, 2, 1, 3)
            scale = DH ** (-0.25)
            q = jax.nn.softmax(split(x @ Wq) * scale, axis=-1)
            k = jax.nn.softmax(split(x @ Wk) * scale, axis=-2)
            v = split(x @ Wv)
            context = jnp.einsum('bhnd,bhne->bhde', k, v)
            out = jnp.einsum('bhnd,bhde->bhne', q, context)
            out = out.transpose(0, 2, 1, 3).reshape(b, n, dm)
            return out @ Wo + bo

        def _forward(x, Wq, Wk, Wv, Wo, bo, ln1_g, ln1_b, W1, b1, W2, b2, ln2_g, ln2_b):
            for i in range(DEPTH):
                h = _layernorm(x, ln1_g[i], ln1_b[i])
                x = x + _linear_attn(h, Wq[i], Wk[i], Wv[i], Wo[i], bo[i])
                h = _layernorm(x, ln2_g[i], ln2_b[i])
                x = x + (jax.nn.gelu(h @ W1[i] + b1[i], approximate=False) @ W2[i] + b2[i])
            return x
        return _forward(x, Wq, Wk, Wv, Wo, bo, ln1_g, ln1_b, W1, b1, W2, b2, ln2_g, ln2_b)

    def _L0_ffn_ref(h, gate_w, gate_b, w1, b1, w2, b2):
        import math
        import jax, jax.numpy as jnp
        import numpy as np
        CAPACITY_FACTOR = 1.25
        B, L, D = h.shape
        E = gate_w.shape[1]
        T = B * L
        C = max(1, math.ceil(CAPACITY_FACTOR * T / E))
        x = h.reshape(T, D)
        logits = x @ gate_w + gate_b
        probs = jax.nn.softmax(logits, axis=-1)
        idx = jnp.argmax(probs, axis=-1)
        prb = jnp.take_along_axis(probs, idx[:, None], axis=1)[:, 0]
        one_hot = jax.nn.one_hot(idx, E, dtype=jnp.float32)
        pos = (jnp.cumsum(one_hot, axis=0) * one_hot).sum(-1).astype(jnp.int32) - 1
        kept = pos < C
        pos_safe = jnp.where(kept, pos, C)
        buf = jnp.zeros((E, C, D), dtype=h.dtype).at[idx, pos_safe].set(x, mode='drop')
        hmid = jax.nn.relu(jnp.einsum('ecd,edf->ecf', buf, w1) + b1[:, None, :])
        ybuf = jnp.einsum('ecf,efd->ecd', hmid, w2) + b2[:, None, :]
        pos_g = jnp.minimum(pos, C - 1)
        y_tok = ybuf[idx, pos_g] * (prb * kept)[:, None]
        y = y_tok.reshape(B, L, D)
        y = jnp.nan_to_num(y, nan=0.0, posinf=10000.0, neginf=-10000.0)
        return y
    edge_index = jnp.stack([src, dst])
    xn = _layernorm(x, axis=-1)
    x = x + _L0_gnn_ref(xn, edge_index, L0_gnn_W, L0_gnn_att_src, L0_gnn_att_dst, L0_gnn_bias, L0_gnn_gamma, L0_gnn_beta) + _L0_mix_ref(xn[None], L0_mix_Wq, L0_mix_Wk, L0_mix_Wv, L0_mix_Wo, L0_mix_bo, L0_mix_ln1_g, L0_mix_ln1_b, L0_mix_W1, L0_mix_b1, L0_mix_W2, L0_mix_b2, L0_mix_ln2_g, L0_mix_ln2_b)[0]
    x = x + _L0_ffn_ref(_layernorm(x, axis=-1)[None], L0_ffn_gate_w, L0_ffn_gate_b, L0_ffn_w1, L0_ffn_b1, L0_ffn_w2, L0_ffn_b2)[0]
    return x

_drawn_inputs = setup_inputs


def setup_inputs(seed=0):
    import zlib

    import numpy as np

    out = dict(_drawn_inputs(seed))
    spreads = {'L0_gnn_gamma': (1.0, 0.2),
     'L0_gnn_beta': (0.0, 0.428),
     'L0_mix_bo': (0.0, 0.1),
     'L0_mix_ln1_g': (1.0, 0.6),
     'L0_mix_ln1_b': (0.0, 0.8),
     'L0_mix_b1': (0.0, 0.32),
     'L0_mix_b2': (0.0, 0.1),
     'L0_mix_ln2_g': (1.0, 0.6),
     'L0_mix_ln2_b': (0.0, 0.8),
     'L0_ffn_gate_b': (0.0, 0.271),
     'L0_ffn_b1': (0.0, 2.0),
     'L0_ffn_b2': (0.0, 2.0)}
    factors = {'L0_gnn_bias': 64.0,
     'L0_mix_Wq': 8.0,
     'L0_mix_Wk': 8.0,
     'L0_mix_Wv': 4.176,
     'L0_mix_Wo': 3.938,
     'L0_ffn_gate_w': 3.172,
     'L0_ffn_w1': 4.245,
     'L0_ffn_w2': 2.887}
    for name, (base, spread) in spreads.items():
        noise = np.random.default_rng([zlib.crc32(name.encode()), seed]).standard_normal(out[name].shape)
        drawn = base * np.exp(spread * noise) if base else spread * noise
        out[name] = jnp.asarray(drawn.astype(out[name].dtype))
    for name, factor in factors.items():
        out[name] = (out[name] * factor).astype(out[name].dtype)
    return out
```

```python
from contextlib import ExitStack

import concourse.bass as bass
from concourse import mybir

F32 = mybir.dt.float32
BF16 = mybir.dt.bfloat16
I32 = mybir.dt.int32
U32 = mybir.dt.uint32
U16 = mybir.dt.uint16
ALU = mybir.AluOpType
ACT = mybir.ActivationFunctionType
AX = mybir.AxisListType

P = 125
D = 256
KC = D // 128
HEADS = 8
DH = D // HEADS
EPS = 1e-5
FAR = -1.0e30
ds = bass.ds


class Kit:

    def __init__(self, nc, ctx, stage):
        self.nc, self.ctx, self.stage, self.sems, self.unraised = nc, ctx, stage, [], []
        ctx.callback(self.clear)

    def start(self):
        engines = (self.nc.sync, self.nc.scalar, self.nc.vector, self.nc.tensor, self.nc.gpsimd)
        for i, sem in enumerate(self.sems):
            if not any(sem is s for s in self.unraised):
                engines[i % len(engines)].sem_inc(sem, 1)
        self.nc.all_engine_barrier()
        return self.ctx.enter_context(self.nc.Block())

    def clear(self):
        if self.sems:
            self.nc.clear_and_free_semaphores(self.sems)
            self.nc.all_engine_barrier()

    def sb(self, name, shape, dt=F32):
        return self.ctx.enter_context(self.nc.sbuf_tensor(f"{self.stage}_{name}", shape, dt))

    def ps(self, name, shape, dt=F32):
        return self.ctx.enter_context(self.nc.psum_tensor(f"{self.stage}_{name}", shape, dt))

    def sem(self, name):
        self.sems.append(self.nc.alloc_semaphore(f"{self.stage}_{name}"))
        return self.sems[-1]

    def gather_sem(self, name):
        self.unraised.append(self.sem(name))
        return self.sems[-1]


def seen(count):
    return count + 1


class Chain:

    def __init__(self, eng, sem):
        self.eng, self.sem, self.base, self.n = eng, sem, 0, 0

    def at(self, base):
        self.base, self.n = base, 0

    def step(self, ins):
        ins.then_inc(self.sem, 1)
        self.n += 1

    def after(self):
        self.eng.wait_ge(self.sem, seen(self.base + self.n))

    def link(self, ins):
        self.step(ins)
        self.after()



def rsqrt_eps(dve, chain, out, var, tmp):
    v, t = tmp
    chain.link(dve.tensor_scalar(v, var, EPS, None, ALU.add))
    chain.link(dve.tensor_scalar(t.bitcast(I32), v.bitcast(I32), 1, None, ALU.arith_shift_right))
    chain.link(dve.tensor_scalar(out.bitcast(I32), t.bitcast(I32), -1.0, float(0x5F3759DF), ALU.mult, ALU.add))
    for _ in range(3):
        chain.link(dve.tensor_tensor(t, out, out, ALU.mult))
        chain.link(dve.tensor_tensor(t, t, v, ALU.mult))
        chain.link(dve.tensor_scalar(t, t, -0.5, 1.5, ALU.mult, ALU.add))
        if _ < 2:
            chain.link(dve.tensor_tensor(out, out, t, ALU.mult))
    chain.link(dve.tensor_tensor(out, out, t, ALU.mult))


RSQRT_STEPS = 15


AGGREGATE_STEPS = 6


def aggregate_stats(dve, chain, mean, var, stats, size):
    even, odd, dev_even, dev_odd = stats[:, :, 1], stats[:, :, 4], stats[:, :, 2], stats[:, :, 5]
    chain.step(dve.tensor_tensor(mean, even, odd, ALU.add))
    chain.step(dve.tensor_tensor(var, even, odd, ALU.subtract))
    chain.link(dve.tensor_tensor(dev_even, dev_even, dev_odd, ALU.add))
    chain.step(dve.tensor_scalar(mean, mean, 0.5, None, ALU.mult))
    chain.link(dve.scalar_tensor_tensor(out=var, in0=var, scalar=0.25, in1=var, op0=ALU.mult, op1=ALU.mult))
    chain.link(dve.scalar_tensor_tensor(out=var, in0=dev_even, scalar=1.0 / size, in1=var, op0=ALU.mult, op1=ALU.add))


def wait_apart(eng, sem, value, passed):
    eng.wait_ge(sem, value)
    eng.sem_inc(passed, 1)


def row(vec, parts):
    return vec.rearrange("(a n) -> a n", a=1).broadcast_to([parts, vec.shape[0]])


def prepare(nc, io, dram, keep, NT):
    with ExitStack() as ctx:
        k = Kit(nc, ctx, "prep")
        x_all = k.sb("x_all", [P, NT, D])
        x_twice = k.sb("x_twice", [P, NT, D])
        stats = k.sb("stats", [P, NT, 6])
        mean, var = k.sb("mean", [P, NT, 1]), k.sb("var", [P, NT])
        rstd = k.sb("rstd", [P, NT, 1])
        rtmp = k.sb("rtmp", [P, 2, NT])
        w = k.sb("w", [128, KC, D + 2 * HEADS])
        att = k.sb("att", [128, 2, D])
        w_att = k.sb("w_att", [128, KC, 2, D])
        xn_tile = k.sb("xn_tile", [P, 2, D])
        xnT = k.sb("xnT", [128, 2, KC, P])
        table = k.sb("table", [P, NT, D + 2 * HEADS])
        ps_t = [k.ps(f"ps_t{b}", [128, KC, P]) for b in range(2)]
        ps_h = [k.ps(f"ps_h{b}", [P, 512]) for b in range(2)]
        x_loaded, w_loaded = k.sem("x_loaded"), k.sem("w_loaded")
        ident_zero, ident_ready = k.sem("ident_zero"), k.sem("ident_ready")
        dve_done = k.sem("dve_done")
        w_ready = k.sem("w_ready")
        xn_ready = k.sem("xn_ready")
        xn_copied = [k.sem(f"xn_copied{b}") for b in range(2)]
        xnT_in_psum = [k.sem(f"xnT_in_psum{b}") for b in range(2)]
        xnT_ready = [k.sem(f"xnT_ready{b}") for b in range(2)]
        xh_in_psum = [k.sem(f"xh_in_psum{b}") for b in range(2)]
        xh_ready = [k.sem(f"xh_ready{b}") for b in range(2)]
        ad_kept, x_copied, sum_ready = k.sem("ad_kept"), k.sem("x_copied"), k.sem("sum_ready")
        stored, edges_copied, pad_ready = k.sem("stored"), k.sem("edges_copied"), k.sem("pad_ready")
        pad = k.sb("pad", [1, 512], I32)
        block = k.start()

        @block.sync
        def _(sp):
            sp.dma_start(x_all[:], io["x"].rearrange("(t p) d -> p t d", p=P)).then_inc(x_loaded, 16)
            sp.dma_start(w[:, :, 0:D], io["L0_gnn_W"].rearrange("(k p) d -> p k d", p=128)).then_inc(w_loaded, 16)
            for i, name in enumerate(("L0_gnn_att_src", "L0_gnn_att_dst")):
                sp.dma_start(att[:, i, :], row(io[name].rearrange("h d -> (h d)"), 128)).then_inc(w_loaded, 16)
            E = io["src"].shape[0]
            sp.wait_ge(pad_ready, seen(1))
            sp.dma_start(dram["dst_pad"][0:E].rearrange("(p c) -> p c", p=P), io["dst"].rearrange("(p c) -> p c", p=P)).then_inc(edges_copied, 16)
            sp.dma_start(dram["dst_pad"][E:E + 512].rearrange("(a c) -> a c", a=1), pad[:]).then_inc(edges_copied, 16)
            sp.wait_ge(xn_ready, seen(NT))
            sp.dma_start(dram["res"][0].rearrange("(t p) d -> p t d", p=P), x_all[:]).then_inc(stored, 16)
            for b in range(2):
                sp.wait_ge(xh_ready[b], seen(NT // 2))
            sp.wait_ge(sum_ready, seen(1))
            sp.dma_start(dram["x_plus_xn"].rearrange("(t p) d -> p t d", p=P), x_twice[:]).then_inc(stored, 16)
            sp.dma_start(dram["node_rows"].rearrange("(t p) d -> p t d", p=P), table[:, :, 0:D + HEADS]).then_inc(stored, 16)
            sp.wait_ge(stored, seen(48))
            sp.dma_start(dram["edge_rows"][E:E + 512, :], dram["node_rows"][0:512, :]).then_inc(stored, 16)
            sp.wait_ge(stored, seen(64))
            sp.wait_ge(edges_copied, seen(32))

        @block.gpsimd
        def _(pool):
            pool.memset(pad[:], 1 << 14).then_inc(pad_ready, 1)
            pool.memset(keep["ident"][:], 0.0).then_inc(ident_zero, 1)
            pool.wait_ge(ident_zero, seen(1))
            pool.affine_select(out=keep["ident"][:], in_=keep["ident"][:], compare_op=ALU.not_equal, fill=1.0,
                               base=0, pattern=[[-1, 128]], channel_multiplier=1).then_inc(ident_ready, 1)

        @block.vector
        def _(dve):
            chain = Chain(dve, dve_done)
            dve.wait_ge(w_loaded, seen(48))
            chain.link(dve.tensor_tensor(w_att[:, :, 0, :], w[:, :, 0:D], att[:, 0:1, :].broadcast_to([128, KC, D]), ALU.mult))
            chain.link(dve.tensor_tensor(w_att[:, :, 1, :], w[:, :, 0:D], att[:, 1:2, :].broadcast_to([128, KC, D]), ALU.mult))
            for kc in range(KC):
                dve.tensor_reduce(w[:, kc, D:D + 2 * HEADS], w_att[:, kc].rearrange("p a (h e) -> p (a h) e", e=DH),
                                  AX.X, ALU.add).then_inc(w_ready, 1)
            dve.wait_ge(x_loaded, seen(16))
            dve.tensor_copy(x_twice[:], x_all[:]).then_inc(x_copied, 1)
            base = chain.n
            with dve.Fori(0, NT, 1) as t:
                dve.bn_stats(stats[:, ds(t, 1), :], x_all[:, ds(t, 1), :]).then_inc(dve_done, 1)
            dve.wait_ge(dve_done, seen(base + NT))
            chain.at(base + NT)
            aggregate_stats(dve, chain, mean[:, :, 0], var[:], stats, D)
            rsqrt_eps(dve, chain, rstd[:, :, 0], var[:], (rtmp[:, 0, :], rtmp[:, 1, :]))
            with dve.Fori(0, NT, 1) as t:
                dve.tensor_scalar(x_all[:, ds(t, 1), :], x_all[:, ds(t, 1), :], mean[:, ds(t, 1), 0], rstd[:, ds(t, 1), 0],
                                  ALU.subtract, ALU.mult).then_inc(xn_ready, 1)
            dve.wait_ge(x_copied, seen(1))
            dve.wait_ge(xn_ready, seen(NT))
            dve.tensor_tensor(x_twice[:], x_twice[:], x_all[:], ALU.add).then_inc(sum_ready, 1)
            with dve.Fori(0, NT // 2, 1) as g:
                for b in range(2):
                    dve.wait_ge(xh_in_psum[b], seen(g + 1))
                    dve.tensor_copy(table[:, ds(2 * g + b, 1), :], ps_h[b][:, None, 0:D + 2 * HEADS]).then_inc(xh_ready[b], 1)
            for b in range(2):
                dve.wait_ge(xh_ready[b], seen(NT // 2))
            dve.tensor_copy(keep["a_node"][:], table[:, :, D:D + 2 * HEADS]).then_inc(ad_kept, 1)

        @block.tensor
        def _(pe):
            pe.wait_ge(ident_ready, seen(1))
            pe.wait_ge(w_ready, seen(KC))
            with pe.Fori(0, NT // 2, 1) as g:
                for b in range(2):
                    pe.wait_ge(xn_copied[b], seen(g + 1))
                    pe.wait_ge(xnT_ready[b], seen(g))
                    for kc in range(KC):
                        last = pe.transpose(ps_t[b][:, kc, :], xn_tile[:, b, kc * 128:(kc + 1) * 128],
                                            keep["ident"][0:P, 0:P])
                    last.then_inc(xnT_in_psum[b], 1)
                for b in range(2):
                    pe.wait_ge(xnT_ready[b], seen(g + 1))
                    pe.wait_ge(xh_ready[b], seen(g))
                    for kc in range(KC):
                        last = pe.matmul(ps_h[b][:, 0:D + 2 * HEADS], xnT[:, b, kc, :], w[:, kc, :],
                                         start=(kc == 0), stop=(kc == KC - 1))
                    last.then_inc(xh_in_psum[b], 1)

        @block.scalar
        def _(act):
            with act.Fori(0, NT // 2, 1) as g:
                for b in range(2):
                    act.wait_ge(xn_ready, seen(2 * g + b + 1))
                    act.wait_ge(xnT_in_psum[b], seen(g))
                    act.activation(xn_tile[:, b, :], x_all[:, ds(2 * g + b, 1), :], ACT.Copy).then_inc(xn_copied[b], 1)
                for b in range(2):
                    act.wait_ge(xnT_in_psum[b], seen(g + 1))
                    act.wait_ge(xh_in_psum[b], seen(g))
                    act.activation(xnT[:, b], ps_t[b][:], ACT.Copy).then_inc(xnT_ready[b], 1)




class Group:

    def __init__(self, i, j, k, layer, n_groups):
        self.i = i
        self.b = k % 2
        count = lambda k: layer * (n_groups // 2 + (k % 2 == 0) * (n_groups % 2)) + (k // 2) + j
        self.m = count(k)
        self.m_before = count(k - 1)


def pipeline(eng, layer, n_groups, steps):
    depth = max(lag for lag, _ in steps)

    def turn(k, j):
        for lag, f in steps:
            g = k - lag
            if isinstance(j, int) and not 0 <= g < n_groups:
                continue
            f(Group(g + 2 * j, j, g, layer, n_groups))

    pairs = (n_groups - depth) // 2
    for k in range(depth):
        turn(k, 0)
    with eng.Fori(0, pairs, 1) as j:
        turn(depth, j)
        turn(depth + 1, j)
    for k in range(depth + 2 * pairs, n_groups + depth):
        turn(k, 0)


def mix(nc, io, dram, keep, NT):
    N = io["x"].shape[0]
    L, _, FF = io["L0_mix_W1"].shape
    NG = NT // 2
    T2 = 2 * P
    FC = FF // 128
    SCALE = float(DH) ** -0.25
    uses = (NG // 2 + NG % 2, NG // 2)
    E_LOCAL = dram["src"].shape[1]

    with ExitStack() as ctx:
        k = Kit(nc, ctx, "mix")
        X = k.sb("X", [P, NT, D])
        big = k.sb("big", [128, NT, D])
        kT_all = big[:].rearrange("p t d -> p (t d)")[:, 0:KC * N].rearrange("p (k n) -> p k n", k=KC)
        extra = big[0:P]
        wq, wk, wv, wo = (k.sb(n, [128, KC, D]) for n in ("wq", "wk", "wv", "wo"))
        w1 = k.sb("w1", [128, KC, FF])
        w2 = k.sb("w2", [128, FC, D])
        ln = k.sb("ln", [128, 4, KC])
        bo, b2 = k.sb("bo", [P, 1, D]), k.sb("b2", [P, 1, D])
        b1 = k.sb("b1", [128, FC])
        stats = k.sb("stats", [P, NT, 6])
        mean, var = k.sb("mean", [P, NT, 1]), k.sb("var", [P, NT])
        rstd = k.sb("rstd", [P, NT, 1])
        rtmp = k.sb("rtmp", [P, 2, NT])
        xhat = k.sb("xhat", [P, 2, 2, D])
        hT = k.sb("hT", [128, 2, KC, T2])
        hL = k.sb("hL", [128, 2, KC, T2])
        kexp = k.sb("kexp", [128, 2, KC, T2])
        kt = k.sb("kt", [P, 2, 2, D])
        vt = k.sb("vt", [P, 2, 2, D])
        kmaxs, ksums = k.sb("kmaxs", [128, KC, NG]), k.sb("ksums", [128, KC, NG])
        kmax, kbias = k.sb("kmax", [128, KC]), k.sb("kbias", [128, KC])
        ksum, krec = k.sb("ksum", [128, KC]), k.sb("krec", [128, KC])
        out_ready = k.sem("out_ready")
        passed_sp, passed_dve, passed_pool = k.sem("passed_sp"), k.sem("passed_dve"), k.sem("passed_pool")
        zeros = k.sb("zeros", [P, 128])
        same_head = k.sb("same_head", [128, 4, DH])
        ctxT = k.sb("ctxT", [128, KC, 128])
        wm = k.sb("wm", [128, KC, D])
        qmax = k.sb("qmax", [P, 2 * HEADS])
        qsum, qrec = k.sb("qsum", [P, 2 * HEADS]), k.sb("qrec", [P, 2 * HEADS])
        qs = kt
        qe = vt
        qT = kexp
        uT = k.sb("uT", [128, FC, T2])
        ps = [k.ps(f"ps{i}", [128, 512]) for i in range(8)]

        def tok(bank):
            return bank[0:P, :].rearrange("p (t d) -> p t d", t=2)

        def feat(bank):
            return bank[:, 0:KC * T2].rearrange("p (k n) -> p k n", k=KC)

        pair = lambda name: [k.sem(f"{name}{b}") for b in range(2)]
        x_loaded = k.sem("x_loaded")
        wa_loaded, wb_loaded = k.sem("wa_loaded"), k.sem("wb_loaded")
        dve_done, stats0_done = k.sem("dve_done"), k.sem("stats0_done")
        shift_done, norm_done, res1_done, res2_done = (k.sem(n) for n in ("shift_done", "norm_done", "res1_done", "res2_done"))
        const_ready = k.sem("const_ready")
        xhat_ready, xT_in_psum, hT_ready, h_stored = pair("xhat_ready"), pair("xT_in_psum"), pair("hT_ready"), pair("h_stored")
        k_in_psum, kmax_taken, k_copied = pair("k_in_psum"), pair("kmax_taken"), pair("k_copied")
        kbias_ready = k.sem("kbias_ready")
        h_loaded, kexp_ready, kx_in_psum, k_ready = pair("h_loaded"), pair("kexp_ready"), pair("kx_in_psum"), pair("k_ready")
        v_in_psum, v_ready, ctx_done = pair("v_in_psum"), pair("v_ready"), pair("ctx_done")
        ctx_ready, wm_in_psum, wm_ready = k.sem("ctx_ready"), k.sem("wm_in_psum"), k.sem("wm_ready")
        h_loaded2, q_in_psum, q_shifted, q_exped, q_ready = (pair(n) for n in ("h_loaded2_", "q_in_psum", "q_shifted", "q_exped", "q_ready"))
        qT_in_psum, qT_ready, attn_in_psum, attn_taken = pair("qT_in_psum"), pair("qT_ready"), pair("attn_in_psum"), pair("attn_taken")
        xhat2_ready, x1T_in_psum, h2T_ready = pair("xhat2_ready"), pair("x1T_in_psum"), pair("h2T_ready")
        up_in_psum, gelu_done = ([k.sem(f"{n}{f}") for f in range(FC // 2)] for n in ("up_in_psum", "gelu_done"))
        down_in_psum, down_taken = pair("down_in_psum"), pair("down_taken")
        bias_added = k.sem("bias_added")
        mix_stored = k.sem("mix_stored")
        ie = k.sb("src_idx", [P, E_LOCAL], U32)
        GC = 8
        idx_tile = k.sb("idx_tile", [P, 2, GC], U32)
        got = k.sb("got", [P, 2, GC, D + HEADS])
        got_a = k.sb("got_a", [P, 2, GC, HEADS])
        got_a_ready = pair("got_a_ready")
        src_loaded, idx_copied, gathered, got_stored = k.sem("src_loaded"), pair("idx_copied"), *([k.gather_sem(f"{n}{b}") for b in range(2)] for n in ("gathered", "got_stored"))
        block = k.start()

        @block.sync
        def _(sp):
            sp.dma_start(ie[:], dram["src"]).then_inc(src_loaded, 16)
            sp.dma_start(X[:], dram["res"][0].rearrange("(t p) d -> p t d", p=P)).then_inc(x_loaded, 16)
            with sp.Fori(0, L, 1) as l:
                wait_apart(sp, res2_done, seen(l * (NG * 2)), passed_sp)
                for tile, name in ((wk, "Wk"), (wv, "Wv"), (wq, "Wq"), (wo, "Wo")):
                    sp.dma_start(tile[:], io[f"L0_mix_{name}"][ds(l, 1)].rearrange("l (k p) n -> p (l k) n", p=128)).then_inc(wa_loaded, 16)
                for i, name in enumerate(("ln1_g", "ln1_b", "ln2_g", "ln2_b")):
                    sp.dma_start(ln[:, i, :], io[f"L0_mix_{name}"][ds(l, 1)].rearrange("l (k p) -> p (l k)", p=128),
                                 allow_slow_non_contiguous=True).then_inc(wa_loaded, 16)
                sp.dma_start(bo[:], io["L0_mix_bo"][ds(l, 1)][None].broadcast_to([P, 1, D])).then_inc(wa_loaded, 16)
                sp.dma_start(w1[:], io["L0_mix_W1"][ds(l, 1)].rearrange("l (k p) n -> p (l k) n", p=128)).then_inc(wb_loaded, 16)
                sp.dma_start(w2[:], io["L0_mix_W2"][ds(l, 1)].rearrange("l (k p) n -> p (l k) n", p=128)).then_inc(wb_loaded, 16)
                sp.dma_start(b2[:], io["L0_mix_b2"][ds(l, 1)][None].broadcast_to([P, 1, D])).then_inc(wb_loaded, 16)
                sp.dma_start(b1[:], io["L0_mix_b1"][ds(l, 1)].rearrange("l (k p) -> p (l k)", p=128),
                             allow_slow_non_contiguous=True).then_inc(wb_loaded, 16)

                def store_h(g):
                    wait_apart(sp, hT_ready[g.b], seen(g.m + 1), passed_sp)
                    sp.dma_start(dram["hT"][ds(g.i, 1)].rearrange("g p k n -> p (g k) n"), hT[:, g.b]).then_inc(h_stored[g.b], 16)

                pipeline(sp, l, NG, [(0, store_h)])
                for b in range(2):
                    wait_apart(sp, h_stored[b], seen((l + 1) * (16 * uses[b])), passed_sp)

                def load_h(g):
                    wait_apart(sp, v_in_psum[g.b], seen(g.m), passed_sp)
                    wait_apart(sp, q_in_psum[g.b], seen(l * uses[g.b]), passed_sp)
                    sp.dma_start(hL[:, g.b], dram["hT"][ds(g.i, 1)].rearrange("g p k n -> p (g k) n")).then_inc(h_loaded[g.b], 16)

                pipeline(sp, l, NG, [(0, load_h)])

                def load_h2(g):
                    wait_apart(sp, q_in_psum[g.b], seen(g.m), passed_sp)
                    wait_apart(sp, v_in_psum[g.b], seen((l + 1) * uses[g.b]), passed_sp)
                    sp.dma_start(hL[:, g.b], dram["hT"][ds(g.i, 1)].rearrange("g p k n -> p (g k) n")).then_inc(h_loaded2[g.b], 16)

                pipeline(sp, l, NG, [(0, load_h2)])
            sp.wait_ge(kbias_ready, seen(L))
            for b in range(2):
                sp.wait_ge(kexp_ready[b], seen(L * uses[b]))
            sp.dma_start(extra, dram["x_plus_xn"].rearrange("(t p) d -> p t d", p=P)).then_inc(x_loaded, 16)
            sp.wait_ge(out_ready, seen(1))
            sp.dma_start(dram["mix_out"].rearrange("(t p) d -> p t d", p=P), X[:]).then_inc(mix_stored, 16)
            sp.wait_ge(mix_stored, seen(16))

        @block.gpsimd
        def _(pool):
            pool.memset(zeros[:], 0.0).then_inc(const_ready, 1)
            pool.memset(same_head[:], 1.0).then_inc(const_ready, 1)
            pool.wait_ge(const_ready, seen(2))
            pool.affine_select(out=same_head[:], in_=same_head[:], compare_op=ALU.is_ge, fill=0.0,
                               base=0, pattern=[[-DH, 4], [0, DH]], channel_multiplier=1).then_inc(const_ready, 1)
            pool.wait_ge(const_ready, seen(3))
            pool.affine_select(out=same_head[:], in_=same_head[:], compare_op=ALU.is_ge, fill=0.0,
                               base=DH - 1, pattern=[[DH, 4], [0, DH]], channel_multiplier=-1).then_inc(const_ready, 1)
            edge_rows = dram["edge_rows"][0:P * E_LOCAL, :].rearrange("(p c) w -> p c w", p=P)
            pool.wait_ge(src_loaded, seen(16))

            def gather(r, b):
                if not isinstance(r, int):
                    pool.wait_ge(gathered[b], r * (16 * GC))
                    pool.wait_ge(got_stored[b], r * 32)
                pool.tensor_copy(idx_tile[:, b, :], ie[:, ds((2 * r + b) * GC, GC)]).then_inc(idx_copied[b], 1)
                if isinstance(r, int):
                    pool.wait_ge(idx_copied[b], seen(r + 1))
                else:
                    wait_apart(pool, idx_copied[b], seen(r + 1), passed_pool)
                for c in range(GC):
                    pool.indirect_dma_start(got[:, b, c, :], None, dram["node_rows"],
                                            bass.IndirectOffsetOnAxis(ap=idx_tile[:, b, c:c + 1], axis=0)).then_inc(gathered[b], 16)

            def store(r, b):
                pool.wait_ge(gathered[b], (r + 1) * (16 * GC))
                pool.dma_start(edge_rows[:, ds((2 * r + b) * GC, GC), :], got[:, b]).then_inc(got_stored[b], 16)
                pool.tensor_copy(got_a[:, b], got[:, b, :, D:]).then_inc(got_a_ready[b], 1)
                if isinstance(r, int):
                    pool.wait_ge(got_a_ready[b], seen(r + 1))
                else:
                    wait_apart(pool, got_a_ready[b], seen(r + 1), passed_pool)
                pool.dma_start(dram["a_edge"][:, ds((2 * r + b) * (GC * HEADS), GC * HEADS)], got_a[:, b].rearrange("p c h -> p (c h)")).then_inc(got_stored[b], 16)

            gather(0, 0)
            gather(0, 1)
            store(0, 0)
            with pool.Fori(1, E_LOCAL // (2 * GC), 1) as r:
                gather(r, 0)
                store(r - 1, 1)
                gather(r, 1)
                store(r, 0)
            store(E_LOCAL // (2 * GC) - 1, 1)
            for b in range(2):
                pool.wait_ge(got_stored[b], E_LOCAL // (2 * GC) * 32)

        def layer_norm_stats(dve, chain, g):
            for t in range(2):
                chain.step(dve.bn_stats(stats[:, ds(2 * g.i + t, 1), :], X[:, ds(2 * g.i + t, 1), :]))

        @block.vector
        def _(dve):
            dve.wait_ge(x_loaded, seen(16))
            stats0 = Chain(dve, stats0_done)

            def first_stats(g):
                stats0.at(g.i * 2)
                layer_norm_stats(dve, stats0, g)

            pipeline(dve, 0, NG, [(0, first_stats)])
            dve.wait_ge(stats0_done, seen(2 * NG))
            chain = Chain(dve, dve_done)
            per_layer = 2 * (AGGREGATE_STEPS + RSQRT_STEPS) + 3
            with dve.Fori(0, L, 1) as l:
                chain.at(dve.snap(l * per_layer))
                dve.wait_ge(res2_done, seen(l * (2 * NG)))
                aggregate_stats(dve, chain, mean[:, :, 0], var[:], stats, D)
                rsqrt_eps(dve, chain, rstd[:, :, 0], var[:], (rtmp[:, 0, :], rtmp[:, 1, :]))

                def norm(ready, done):
                    def f(g):
                        dve.wait_ge(done[g.b], seen(g.m))
                        for t in range(2):
                            last = dve.tensor_scalar(xhat[:, g.b, t:t + 1, :], X[:, ds(2 * g.i + t, 1), :], mean[:, ds(2 * g.i + t, 1), 0],
                                                     rstd[:, ds(2 * g.i + t, 1), 0], ALU.subtract, ALU.mult)
                        last.then_inc(ready[g.b], 1)
                    return f

                def key_max(g):
                    dve.wait_ge(k_copied[g.b], seen(g.m + 1))
                    dve.tensor_reduce(kmaxs[:, :, ds(g.i, 1)], kT_all[:, :, ds(g.i * T2, T2)], AX.X, ALU.max).then_inc(kmax_taken[g.b], 1)

                for b in range(2):
                    dve.wait_ge(x1T_in_psum[b], seen(l * uses[b]))
                pipeline(dve, l, NG, [(0, norm(xhat_ready, xT_in_psum)), (1, key_max)])
                for b in range(2):
                    dve.wait_ge(kmax_taken[b], seen((l + 1) * uses[b]))
                chain.link(dve.tensor_reduce(kmax[:], kmaxs[:], AX.X, ALU.max))
                dve.tensor_scalar(kbias[:], kmax[:], -SCALE, None, ALU.mult).then_inc(kbias_ready, 1)

                def take_k(g):
                    dve.wait_ge(kx_in_psum[g.b], seen(g.m + 1))
                    dve.wait_ge(ctx_done[g.b], seen(g.m))
                    dve.tensor_copy(kt[:, g.b], tok(ps[g.b])).then_inc(k_ready[g.b], 1)

                for b in range(2):
                    wait_apart(dve, q_exped[b], seen(l * uses[b]), passed_dve)
                pipeline(dve, l, NG, [(0, take_k)])
                for b in range(2):
                    dve.wait_ge(ctx_done[b], seen((l + 1) * uses[b]))
                for kc in range(KC):
                    last = dve.tensor_tensor(ctxT[:, kc, :], ps[4][:, kc * 128:(kc + 1) * 128],
                                             same_head[:].rearrange("p a b -> p (a b)"), ALU.mult)
                last.then_inc(ctx_ready, 1)
                chain.link(dve.tensor_reduce(ksum[:], ksums[:], AX.X, ALU.add))
                chain.link(dve.reciprocal(krec[:], ksum[:]))
                dve.wait_ge(wm_in_psum, seen(l + 1))
                for kc in range(KC):
                    last = dve.tensor_scalar(wm[:, kc, :], ps[5][:, kc * D:(kc + 1) * D], krec[:, kc:kc + 1], None, ALU.mult)
                last.then_inc(wm_ready, 1)

                def per_head(ap):
                    return ap.rearrange("p t (h e) -> p (t h) e", e=DH)

                def shift(g):
                    c = Chain(dve, shift_done)
                    c.at(dve.snap(l * NG + g.i))
                    dve.wait_ge(q_in_psum[g.b], seen(g.m + 1))
                    c.link(dve.tensor_reduce(qmax[:], per_head(tok(ps[g.b])), AX.X, ALU.max))
                    dve.wait_ge(q_exped[g.b], seen(g.m))
                    dve.tensor_tensor(per_head(qs[:, g.b]), per_head(tok(ps[g.b])), qmax[:, :, None].broadcast_to([P, 2 * HEADS, DH]),
                                      ALU.subtract).then_inc(q_shifted[g.b], 1)

                def normalise(g):
                    c = Chain(dve, norm_done)
                    c.at(dve.snap((l * NG + g.i) * 2))
                    dve.wait_ge(q_exped[g.b], seen(g.m + 1))
                    c.link(dve.tensor_reduce(qsum[:], per_head(qe[:, g.b]), AX.X, ALU.add))
                    c.link(dve.reciprocal(qrec[:], qsum[:]))
                    dve.tensor_tensor(per_head(qe[:, g.b]), per_head(qe[:, g.b]), qrec[:, :, None].broadcast_to([P, 2 * HEADS, DH]),
                                      ALU.mult).then_inc(q_ready[g.b], 1)

                def residual(banks, ready, taken, bias, sem):
                    def f(g):
                        c = Chain(dve, sem)
                        c.at(0)
                        rows = X[:, ds(2 * g.i, 2), :]
                        dve.wait_ge(ready[g.b], seen(g.m + 1))
                        dve.tensor_tensor(rows, tok(ps[banks + g.b]), rows, ALU.add).then_inc(taken[g.b], 1)
                        dve.wait_ge(taken[g.b], seen(g.m + 1))
                        dve.tensor_tensor(rows, rows, bias[:].broadcast_to([P, 2, D]), ALU.add).then_inc(bias_added, 1)
                        wait_apart(dve, bias_added, seen((l * 2 + (sem is res2_done)) * NG + g.i + 1), passed_dve)
                        layer_norm_stats(dve, c, g)
                    return f

                dve.wait_ge(wa_loaded, seen((l + 1) * (16 * 9)))
                pipeline(dve, l, NG, [(1, normalise), (0, shift), (2, residual(6, attn_in_psum, attn_taken, bo, res1_done))])

                dve.wait_ge(res1_done, seen((l + 1) * (2 * NG)))
                aggregate_stats(dve, chain, mean[:, :, 0], var[:], stats, D)
                rsqrt_eps(dve, chain, rstd[:, :, 0], var[:], (rtmp[:, 0, :], rtmp[:, 1, :]))
                for b in range(2):
                    dve.wait_ge(xT_in_psum[b], seen((l + 1) * uses[b]))
                dve.wait_ge(wb_loaded, seen((l + 1) * (16 * 4)))
                pipeline(dve, l, NG, [(0, norm(xhat2_ready, x1T_in_psum)), (1, residual(6, down_in_psum, down_taken, b2, res2_done))])
            dve.wait_ge(x_loaded, seen(32))
            dve.wait_ge(res2_done, seen(L * NG * 2))
            dve.tensor_tensor(X[:], X[:], extra, ALU.add).then_inc(out_ready, 1)

        @block.tensor
        def _(pe):
            ident = keep["ident"]
            pe.wait_ge(const_ready, seen(4))
            with pe.Fori(0, L, 1) as l:
                def all_of(sems, layers):
                    for b in range(2):
                        pe.wait_ge(sems[b], seen(layers * uses[b]))

                def to_features(bank, src):
                    for kc in range(KC):
                        for t in range(2):
                            last = pe.transpose(feat(bank)[:, kc, t * P:(t + 1) * P], src[:, t, kc * 128:(kc + 1) * 128], ident[0:P, 0:P])
                    return last

                def by_node(bank, lhs, w, first=True, last_half=True):
                    for t in range(2):
                        for kc in range(KC):
                            last = pe.matmul(tok(bank)[:, t, :], lhs[:, kc, t * P:(t + 1) * P], w[:, kc, :], start=(kc == 0), stop=(kc == KC - 1))
                    return last

                all_of(h2T_ready, l)
                for f in range(FC // 2):
                    pe.wait_ge(gelu_done[f], seen(l * NG))
                pe.wait_ge(wa_loaded, seen((l + 1) * (16 * 9)))

                def x_transposes(g):
                    pe.wait_ge(xhat_ready[g.b], seen(g.m + 1))
                    pe.wait_ge(hT_ready[g.b], seen(g.m))
                    to_features(ps[g.b], xhat[:, g.b]).then_inc(xT_in_psum[g.b], 1)

                def keys(g):
                    pe.wait_ge(hT_ready[g.b], seen(g.m + 1))
                    pe.wait_ge(k_copied[g.b], seen(g.m))
                    for dc in range(KC):
                        for kc in range(KC):
                            last = pe.matmul(feat(ps[2 + g.b])[:, dc, :], wk[:, kc, dc * 128:(dc + 1) * 128], hT[:, g.b, kc, :],
                                             start=(kc == 0), stop=(kc == KC - 1))
                    last.then_inc(k_in_psum[g.b], 1)

                pipeline(pe, l, NG, [(0, x_transposes), (1, keys)])

                all_of(hT_ready, l + 1)
                all_of(k_copied, l + 1)
                for kc in range(KC):
                    pe.matmul(ps[4][:, kc * 128:(kc + 1) * 128], zeros[:], zeros[:], start=(kc == 0), stop=False, skip_group_check=True)

                def kv(g):
                    pe.wait_ge(kexp_ready[g.b], seen(g.m + 1))
                    pe.wait_ge(k_ready[g.b], seen(g.m))
                    for t in range(2):
                        for kc in range(KC):
                            last = pe.transpose(tok(ps[g.b])[:, t, kc * 128:(kc + 1) * 128], kexp[:, g.b, kc, t * P:(t + 1) * P], ident[:])
                    last.then_inc(kx_in_psum[g.b], 1)
                    pe.wait_ge(h_loaded[g.b], seen((g.m + 1) * 16))
                    pe.wait_ge(v_ready[g.b], seen(g.m))
                    by_node(ps[2 + g.b], hL[:, g.b], wv).then_inc(v_in_psum[g.b], 1)

                def context(g):
                    pe.wait_ge(k_ready[g.b], seen(g.m + 1))
                    pe.wait_ge(v_ready[g.b], seen(g.m + 1))
                    for t in range(2):
                        for kc in range(KC):
                            half = slice(kc * 128, (kc + 1) * 128)
                            last = pe.matmul(ps[4][:, half], vt[:, g.b, t, half], kt[:, g.b, t, half], start=False, stop=False, skip_group_check=True)
                    last.then_inc(ctx_done[g.b], 1)

                pipeline(pe, l, NG, [(0, kv), (1, context)])
                pe.wait_ge(ctx_ready, seen(l + 1))
                for kc in range(KC):
                    last = pe.matmul(ps[5][:, kc * D:(kc + 1) * D], ctxT[:, kc, :], wo[:, kc, :], start=True, stop=True)
                last.then_inc(wm_in_psum, 1)

                all_of(k_ready, l + 1)
                all_of(v_ready, l + 1)
                all_of(down_taken, l)

                def q_transposes(g):
                    pe.wait_ge(q_ready[g.b], seen(g.m + 1))
                    pe.wait_ge(qT_ready[g.b], seen(g.m))
                    to_features(ps[2 + g.b], qe[:, g.b]).then_inc(qT_in_psum[g.b], 1)

                def queries(g):
                    pe.wait_ge(h_loaded2[g.b], seen((g.m + 1) * 16))
                    pe.wait_ge(q_shifted[g.b], seen(g.m))
                    by_node(ps[g.b], hL[:, g.b], wq).then_inc(q_in_psum[g.b], 1)

                def attend(g):
                    pe.wait_ge(qT_ready[g.b], seen(g.m + 1))
                    pe.wait_ge(attn_taken[g.b], seen(g.m))
                    pe.wait_ge(wm_ready, seen(l + 1))
                    by_node(ps[6 + g.b], qT[:, g.b], wm).then_inc(attn_in_psum[g.b], 1)

                pipeline(pe, l, NG, [(2, q_transposes), (0, queries), (2, attend)])

                all_of(q_shifted, l + 1)
                all_of(qT_ready, l + 1)
                all_of(attn_taken, l + 1)
                pe.wait_ge(wb_loaded, seen((l + 1) * (16 * 4)))

                def x1_transposes(g):
                    pe.wait_ge(xhat2_ready[g.b], seen(g.m + 1))
                    pe.wait_ge(h2T_ready[g.b], seen(g.m))
                    to_features(ps[g.b], xhat[:, g.b]).then_inc(x1T_in_psum[g.b], 1)

                def down(g):
                    pe.wait_ge(down_taken[g.b], seen(g.m))
                    for f in range(FC // 2):
                        pe.wait_ge(gelu_done[f], seen(pe.snap(l * NG + g.i + 1)))
                    for t in range(2):
                        for f in range(FC):
                            last = pe.matmul(tok(ps[6 + g.b])[:, t, :], uT[:, f, t * P:(t + 1) * P], w2[:, f, :], start=(f == 0), stop=(f == FC - 1))
                    last.then_inc(down_in_psum[g.b], 1)

                def up(g):
                    pe.wait_ge(h2T_ready[g.b], seen(g.m + 1))
                    n = pe.snap(l * NG + g.i)
                    for f in range(FC):
                        if f % 2 == 0:
                            pe.wait_ge(gelu_done[f // 2], seen(n))
                        for kc in range(KC):
                            last = pe.matmul(feat(ps[2 + f // 2])[:, f % 2, :], w1[:, kc, f * 128:(f + 1) * 128], hT[:, g.b, kc, :],
                                             start=(kc == 0), stop=(kc == KC - 1))
                        if f % 2:
                            last.then_inc(up_in_psum[f // 2], 1)

                pipeline(pe, l, NG, [(0, x1_transposes), (1, down), (0, up)])

        @block.scalar
        def _(act):
            with act.Fori(0, L, 1) as l:
                def all_of(sems, layers):
                    for b in range(2):
                        act.wait_ge(sems[b], seen(layers * uses[b]))

                act.wait_ge(wa_loaded, seen((l + 1) * (16 * 9)))
                for f in range(FC // 2):
                    act.wait_ge(up_in_psum[f], seen(l * NG))

                def take_hT(which, in_psum, done, ready):
                    def f(g):
                        act.wait_ge(in_psum[g.b], seen(g.m + 1))
                        done(g)
                        for kc in range(KC):
                            last = act.activation(hT[:, g.b, kc, :], feat(ps[g.b])[:, kc, :], ACT.Identity,
                                                  bias=ln[:, which + 1, kc:kc + 1], scale=ln[:, which, kc:kc + 1])
                        last.then_inc(ready[g.b], 1)
                    return f

                def hT_stored(g):
                    act.wait_ge(k_in_psum[g.b], seen(g.m))
                    act.wait_ge(h_stored[g.b], seen(g.m * 16))

                def copy_k(g):
                    act.wait_ge(k_in_psum[g.b], seen(g.m + 1))
                    act.activation(kT_all[:, :, ds(g.i * T2, T2)], feat(ps[2 + g.b]), ACT.Copy).then_inc(k_copied[g.b], 1)

                pipeline(act, l, NG, [(0, take_hT(0, xT_in_psum, hT_stored, hT_ready)), (1, copy_k)])

                all_of(attn_in_psum, l)
                all_of(qT_in_psum, l)
                all_of(k_copied, l + 1)
                act.wait_ge(kbias_ready, seen(l + 1))

                def exp_k(g):
                    act.wait_ge(kx_in_psum[g.b], seen(g.m))
                    for kc in range(KC):
                        last = act.activation(kexp[:, g.b, kc, None, :], kT_all[:, kc:kc + 1, ds(g.i * T2, T2)], ACT.Exp, bias=kbias[:, kc:kc + 1], scale=SCALE,
                                              accum_out=ksums[:, kc, ds(g.i, 1)])
                    last.then_inc(kexp_ready[g.b], 1)

                def take_v(g):
                    act.wait_ge(v_in_psum[g.b], seen(g.m + 1))
                    act.wait_ge(ctx_done[g.b], seen(g.m))
                    act.activation(vt[:, g.b], tok(ps[2 + g.b]), ACT.Copy).then_inc(v_ready[g.b], 1)

                pipeline(act, l, NG, [(0, exp_k), (1, take_v)])

                all_of(ctx_done, l + 1)
                all_of(kx_in_psum, l + 1)

                def take_qT(g):
                    act.wait_ge(qT_in_psum[g.b], seen(g.m + 1))
                    act.wait_ge(attn_in_psum[g.b], seen(g.m))
                    act.activation(qT[:, g.b], feat(ps[2 + g.b]), ACT.Copy).then_inc(qT_ready[g.b], 1)

                def exp_q(g):
                    act.wait_ge(q_shifted[g.b], seen(g.m + 1))
                    act.wait_ge(qT_in_psum[g.b], seen(g.m))
                    act.activation(qe[:, g.b], qs[:, g.b], ACT.Exp, scale=SCALE).then_inc(q_exped[g.b], 1)

                pipeline(act, l, NG, [(2, take_qT), (0, exp_q)])

                all_of(k_in_psum, l + 1)
                for b in range(2):
                    act.wait_ge(h_stored[b], seen((l + 1) * (16 * uses[b])))
                act.wait_ge(wb_loaded, seen((l + 1) * (16 * 4)))
                all_of(down_in_psum, l)

                def h2T_used(g):
                    pass

                def gelu(g):
                    n = act.snap(l * NG + g.i)
                    act.wait_ge(down_in_psum[1 - g.b], seen(g.m_before + 1))
                    for f in range(FC // 2):
                        act.wait_ge(up_in_psum[f], seen(n + 1))
                        for h in range(2):
                            last = act.activation(uT[:, 2 * f + h, :], feat(ps[2 + f])[:, h, :], ACT.Gelu, bias=b1[:, 2 * f + h:2 * f + h + 1])
                        last.then_inc(gelu_done[f], 1)

                pipeline(act, l, NG, [(0, take_hT(2, x1T_in_psum, h2T_used, h2T_ready)), (0, gelu)])


def segments(nc, io, dram, keep, NT, plan_steps):
    N = io["x"].shape[0]
    E = io["src"].shape[0]
    EL = E // P
    CH = 500
    NC = E // CH
    SP_ = 110
    SC = plan_steps // SP_
    with ExitStack() as ctx:
        k = Kit(nc, ctx, "seg")
        AE = k.sb("AE", [P, EL, HEADS])
        dst = k.sb("dst", [P, EL], I32)
        pen = k.sb("pen", [P, EL])
        endT, carryT = k.sb("endT", [HEADS, P]), k.sb("carryT", [HEADS, P])
        firsts, lasts = k.sb("firsts", [HEADS, P], I32), k.sb("lasts", [HEADS, P], I32)
        joins, whole, pen8 = k.sb("joins", [HEADS, P]), k.sb("whole", [HEADS, P]), k.sb("pen8", [HEADS, P])
        start_row = k.sb("start_row", [1, NC], I32)
        starts = k.sb("starts", [P, NC], I32)
        junk = k.sb("junk", [P, CH])
        node = k.sb("node", [P, NT])
        count1, count2 = k.sb("count1", [P, NT]), k.sb("count2", [P, NT])
        chunk_f, chunk_i = k.sb("chunk_f", [P, NT]), k.sb("chunk_i", [P, NT], U32)
        rows = k.sb("rows", [P, NT, CH], I32)
        r0, r1 = k.sb("r0", [P, NT]), k.sb("r1", [P, NT])
        end_f = k.sb("end_f", [P, 1])
        last_f, last_i = k.sb("last_f", [P, NT]), k.sb("last_i", [P, NT], U32)
        part_f, part_i = k.sb("part_f", [P, NT]), k.sb("part_i", [P, NT], U32)
        bounds = k.sb("bounds", [P, P - 1])
        m_scan, m_carry = k.sb("m_scan", [P, NT, HEADS]), k.sb("m_carry", [P, NT, HEADS])
        spans, empty = k.sb("spans", [P, NT]), k.sb("empty", [P, NT])
        pair_v = k.sb("pair_v", [P, NT, 2 * HEADS])
        blk = k.sb("blk", [1, NT + 1])
        blk_i = k.sb("blk_i", [1, NT], I32)
        blk_row = k.sb("blk_row", [1, 3, NT])
        blk_all = k.sb("blk_all", [SP_, 3 * NT])
        step = k.sb("step", [SP_, SC])
        hit = k.sb("hit", [SP_, SC, NT])
        st_b, st_e, st_f = k.sb("st_b", [SP_, SC]), k.sb("st_e", [SP_, SC]), k.sb("st_f", [SP_, SC])
        plan = k.sb("plan", [SP_, 2, SC], I32)
        ones_row, zero_row = k.sb("ones_row", [1, NT]), k.sb("zero_row", [1, NT])
        n = {name: k.sem(name) for name in (
            "edges_loaded", "ends_loaded", "starts_loaded", "starts_spread", "iotas_ready", "done", "scanned", "scan_stored", "ends_ready",
            "carry_ready", "carry_stored", "chunks_ready", "rowptr_ready", "rowptr_stored", "rowptr_loaded",
            "last_ready", "blk_ready", "blk_spread", "plan_ready", "plan_stored", "plan_loaded")}
        for name in ("rows_gathered", "m_gathered"):
            n[name] = k.gather_sem(name)
        block = k.start()

        @block.sync
        def _(sp):
            sp.dma_start(start_row[:], io["dst"].rearrange("(a c e) -> a c e", a=1, e=CH)[:, :, 0],
                         allow_slow_non_contiguous=True).then_inc(n["starts_loaded"], 16)
            sp.dma_start(dst[:], io["dst"].rearrange("(p c) -> p c", p=P)).then_inc(n["edges_loaded"], 16)
            sp.dma_start(AE[:], dram["a_edge"].rearrange("p (c h) -> p c h", h=HEADS)).then_inc(n["edges_loaded"], 16)
            for tile, c in ((firsts, 0), (lasts, EL - 1)):
                sp.dma_start(tile[:], io["dst"].rearrange("(a p c) -> a p c", a=1, p=P)[:, :, c].broadcast_to([HEADS, P]),
                             allow_slow_non_contiguous=True).then_inc(n["ends_loaded"], 16)
            sp.wait_ge(n["rowptr_ready"], seen(1))
            sp.dma_start(dram["rowptr"][0:N].rearrange("(t p) -> p t", p=P), r0[:], allow_slow_non_contiguous=True).then_inc(n["rowptr_stored"], 16)
            sp.dma_start(dram["rowptr"][N:N + 1].rearrange("(a b) -> a b", a=1), end_f[0:1, :]).then_inc(n["rowptr_stored"], 16)
            sp.wait_ge(n["rowptr_stored"], seen(32))
            sp.dma_start(r1[:], dram["rowptr"][1:N + 1].rearrange("(t p) -> p t", p=P), allow_slow_non_contiguous=True).then_inc(n["rowptr_loaded"], 16)
            sp.dma_start(blk[:, 0:NT], dram["rowptr"][0:N].rearrange("(a t p) -> a t p", a=1, p=P)[:, :, 0],
                         allow_slow_non_contiguous=True).then_inc(n["rowptr_loaded"], 16)
            sp.dma_start(blk[:, NT:NT + 1], dram["rowptr"][N:N + 1].rearrange("(a b) -> a b", a=1)).then_inc(n["rowptr_loaded"], 16)
            sp.wait_ge(n["scanned"], seen(HEADS))
            sp.dma_start(dram["scan"].rearrange("(p c) h -> p c h", p=P), AE[:]).then_inc(n["scan_stored"], 16)
            sp.wait_ge(n["scan_stored"], seen(16))
            sp.dma_start(endT[:], dram["scan"].rearrange("(p c) h -> h p c", p=P)[:, :, EL - 1],
                         allow_slow_non_contiguous=True).then_inc(n["ends_ready"], 16)
            sp.wait_ge(n["carry_ready"], seen(1))
            sp.dma_start(dram["carry"].rearrange("p h -> h p"), carryT[:], allow_slow_non_contiguous=True).then_inc(n["carry_stored"], 16)
            sp.wait_ge(n["plan_ready"], seen(2))
            sp.dma_start(dram["plan"].rearrange("w (p s) -> p w s", s=SC), plan[:]).then_inc(n["plan_stored"], 16)
            sp.wait_ge(n["plan_stored"], seen(16))
            for q in range(4):
                sp.dma_start(keep["plan"][q:q + 1, :, q:q + plan_steps], dram["plan"][None]).then_inc(n["plan_loaded"], 16)
            sp.wait_ge(n["plan_loaded"], seen(64))
            sp.wait_ge(n["carry_stored"], seen(16))

        @block.gpsimd
        def _(pool):
            pool.iota(node[:], pattern=[[P, NT]], base=0, channel_multiplier=1, allow_small_or_imprecise_dtypes=True).then_inc(n["iotas_ready"], 1)
            pool.iota(bounds[:], pattern=[[EL, P - 1]], base=EL, channel_multiplier=0, allow_small_or_imprecise_dtypes=True).then_inc(n["iotas_ready"], 1)
            pool.iota(step[:], pattern=[[1, SC]], base=0, channel_multiplier=SC, allow_small_or_imprecise_dtypes=True).then_inc(n["iotas_ready"], 1)
            pool.iota(blk_row[:, 2, :], pattern=[[1, NT]], base=0, channel_multiplier=0, allow_small_or_imprecise_dtypes=True).then_inc(n["iotas_ready"], 1)
            pool.memset(end_f[:], float(E)).then_inc(n["iotas_ready"], 1)
            pool.memset(zero_row[:], 0.0).then_inc(n["iotas_ready"], 1)
            pool.wait_ge(n["starts_loaded"], seen(16))
            pool.partition_broadcast(starts[:], start_row[:], channels=P).then_inc(n["starts_spread"], 1)
            pool.wait_ge(n["chunks_ready"], seen(1))
            for t in range(NT):
                pool.indirect_dma_start(rows[:, t, :], None, io["dst"].rearrange("(c e) -> c e", e=CH),
                                        bass.IndirectOffsetOnAxis(ap=chunk_i[:, t:t + 1], axis=0)).then_inc(n["rows_gathered"], 16)
            pool.wait_ge(n["blk_ready"], seen(1))
            pool.wait_ge(n["iotas_ready"], seen(6))
            pool.partition_broadcast(blk_all[:], blk_row[:].rearrange("a b c -> a (b c)"), channels=SP_).then_inc(n["blk_spread"], 1)
            pool.wait_ge(n["last_ready"], seen(2))
            pool.wait_ge(n["scan_stored"], seen(16))
            pool.wait_ge(n["carry_stored"], seen(16))
            for t in range(NT):
                pool.indirect_dma_start(m_scan[:, t, :], None, dram["scan"],
                                        bass.IndirectOffsetOnAxis(ap=last_i[:, t:t + 1], axis=0)).then_inc(n["m_gathered"], 16)
            for t in range(NT):
                pool.indirect_dma_start(m_carry[:, t, :], None, dram["carry"],
                                        bass.IndirectOffsetOnAxis(ap=part_i[:, t:t + 1], axis=0)).then_inc(n["m_gathered"], 16)

        @block.vector
        def _(dve):
            c = Chain(dve, n["done"])
            link = c.link
            link(dve.memset(keep["plan"][:], 0))
            dve.wait_ge(n["iotas_ready"], seen(6))
            dve.wait_ge(n["starts_spread"], seen(1))
            for t in range(NT):
                link(dve.tensor_scalar(junk[:, 0:NC], starts[:], node[:, t:t + 1], 0.0, ALU.is_lt, ALU.add, accum_out=count1[:, t:t + 1]))
            link(dve.tensor_scalar(chunk_f[:], count1[:], -1.0, 0.0, ALU.add, ALU.max))
            dve.tensor_copy(chunk_i[:], chunk_f[:]).then_inc(n["chunks_ready"], 1)
            dve.wait_ge(n["edges_loaded"], seen(32))
            dve.wait_ge(n["ends_loaded"], seen(32))
            link(dve.memset(pen[:, 0:1], FAR))
            link(dve.tensor_tensor(pen[:, 1:EL], dst[:, 1:EL], dst[:, 0:EL - 1], ALU.is_equal))
            link(dve.tensor_scalar(pen[:, 1:EL], pen[:, 1:EL], -1.0, -FAR, ALU.add, ALU.mult))
            for h in range(HEADS):
                dve.tensor_tensor_scan(AE[:, :, h], pen[:], AE[:, :, h], FAR, ALU.add, ALU.max).then_inc(n["scanned"], 1)
            dve.wait_ge(n["rows_gathered"], 16 * NT)
            for t in range(NT):
                link(dve.tensor_scalar(junk[:], rows[:, t, :], node[:, t:t + 1], 0.0, ALU.is_lt, ALU.add, accum_out=count2[:, t:t + 1]))
            dve.scalar_tensor_tensor(out=r0[:], in0=chunk_f[:], scalar=float(CH), in1=count2[:], op0=ALU.mult, op1=ALU.add).then_inc(n["rowptr_ready"], 1)
            link(dve.tensor_tensor(joins[:, 1:P], firsts[:, 1:P], lasts[:, 0:P - 1], ALU.is_equal))
            link(dve.tensor_tensor(whole[:], firsts[:], lasts[:], ALU.is_equal))
            link(dve.tensor_tensor(pen8[:, 1:P], joins[:, 1:P], whole[:, 0:P - 1], ALU.mult))
            link(dve.tensor_scalar(pen8[:, 1:P], pen8[:, 1:P], -1.0, -FAR, ALU.add, ALU.mult))
            link(dve.tensor_scalar(joins[:, 1:P], joins[:, 1:P], -1.0, -FAR, ALU.add, ALU.mult))
            dve.wait_ge(n["ends_ready"], seen(16))
            link(dve.tensor_tensor(joins[:, 1:P], joins[:, 1:P], endT[:, 0:P - 1], ALU.add))
            link(dve.memset(carryT[:, 0:1], FAR))
            dve.tensor_tensor_scan(carryT[:, 1:P], pen8[:, 1:P], joins[:, 1:P], FAR, ALU.add, ALU.max).then_inc(n["carry_ready"], 1)
            dve.wait_ge(n["rowptr_loaded"], seen(48))
            link(dve.tensor_tensor(blk_row[:, 1, :], blk[:, 1:NT + 1], blk[:, 0:NT], ALU.subtract))
            link(dve.tensor_scalar(blk_i[:], blk_row[:, 1, :], 511.0, None, ALU.add))
            link(dve.tensor_scalar(blk_i[:], blk_i[:], 9, None, ALU.arith_shift_right))
            link(dve.tensor_copy(blk_row[:, 1, :], blk_i[:]))
            link(dve.tensor_tensor_scan(blk_row[:, 0, :], blk_row[:, 1, :], zero_row[:], 0.0, ALU.add, ALU.add))
            link(dve.tensor_tensor(blk_row[:, 1, :], blk_row[:, 0, :], blk_row[:, 1, :], ALU.subtract))
            dve.scalar_tensor_tensor(out=blk_row[:, 1, :], in0=blk_row[:, 1, :], scalar=-512.0, in1=blk[:, 0:NT],
                                     op0=ALU.mult, op1=ALU.add).then_inc(n["blk_ready"], 1)
            dve.wait_ge(n["blk_spread"], seen(1))

            def over(i):
                return blk_all[:, None, i * NT:(i + 1) * NT].broadcast_to([SP_, SC, NT])

            link(dve.tensor_tensor(hit[:], over(0), step[:, :, None].broadcast_to([SP_, SC, NT]), ALU.is_le))
            link(dve.tensor_reduce(st_b[:], hit[:], AX.X, ALU.add))
            link(dve.tensor_tensor(hit[:], over(2), st_b[:, :, None].broadcast_to([SP_, SC, NT]), ALU.is_equal))
            link(dve.tensor_tensor(hit[:], hit[:], over(1), ALU.mult))
            link(dve.tensor_reduce(st_e[:], hit[:], AX.X, ALU.add))
            link(dve.scalar_tensor_tensor(out=st_e[:], in0=step[:], scalar=512.0, in1=st_e[:], op0=ALU.mult, op1=ALU.add))
            link(dve.tensor_scalar(st_f[:], st_b[:], float(NT), float(E), ALU.is_ge, ALU.mult))
            link(dve.tensor_tensor(st_e[:], st_e[:], st_f[:], ALU.add))
            dve.tensor_scalar(plan[:, 0, :], st_b[:], float(NT - 1), None, ALU.min).then_inc(n["plan_ready"], 1)
            dve.tensor_scalar(plan[:, 1, :], st_e[:], float(E), None, ALU.min).then_inc(n["plan_ready"], 1)
            link(dve.tensor_scalar(last_f[:], r1[:], -1.0, 0.0, ALU.add, ALU.max))
            dve.tensor_copy(last_i[:], last_f[:]).then_inc(n["last_ready"], 1)
            flat = rows[:].rearrange("p a b -> p (a b)").bitcast(F32)[:, 0:NT * (P - 1)].rearrange("p (t k) -> p t k", t=NT)
            link(dve.tensor_tensor(flat, bounds[:, None, :].broadcast_to([P, NT, P - 1]), last_f[:, :, None].broadcast_to([P, NT, P - 1]), ALU.is_le))
            link(dve.tensor_reduce(part_f[:], flat, AX.X, ALU.add))
            dve.tensor_copy(part_i[:], part_f[:]).then_inc(n["last_ready"], 1)
            link(dve.tensor_scalar(part_f[:], part_f[:], float(EL), None, ALU.mult))
            link(dve.tensor_tensor(spans[:], r0[:], part_f[:], ALU.is_lt))
            link(dve.tensor_scalar(spans[:], spans[:], -1.0, -FAR, ALU.add, ALU.mult))
            link(dve.tensor_tensor(empty[:], r0[:], r1[:], ALU.is_equal))
            link(dve.tensor_scalar(empty[:], empty[:], FAR, None, ALU.mult))
            dve.wait_ge(n["m_gathered"], 16 * 2 * NT)

            def wide(ap):
                return ap[:, :, None].broadcast_to([P, NT, HEADS])

            a_node = keep["a_node"]
            link(dve.tensor_tensor(m_carry[:], m_carry[:], wide(spans), ALU.add))
            link(dve.tensor_tensor(m_scan[:], m_scan[:], m_carry[:], ALU.max))
            link(dve.tensor_tensor(m_scan[:], m_scan[:], wide(empty), ALU.add))
            link(dve.tensor_tensor(m_scan[:], m_scan[:], a_node[:, :, 0:HEADS], ALU.max))
            link(dve.tensor_tensor(m_scan[:], m_scan[:], a_node[:, :, HEADS:], ALU.add))
            link(dve.scalar_tensor_tensor(out=pair_v[:, :, HEADS:], in0=m_scan[:], scalar=0.2, in1=m_scan[:], op0=ALU.mult, op1=ALU.max))
            link(dve.tensor_copy(keep["m_node"][:], pair_v[:, :, HEADS:]))
            link(dve.tensor_copy(pair_v[:, :, 0:HEADS], a_node[:, :, HEADS:]))
            parts = keep["pair_parts"]
            for i in range(3):
                link(dve.tensor_copy(parts[:, :, i, :], pair_v[:]))
                if i < 2:
                    link(dve.tensor_tensor(pair_v[:], pair_v[:], parts[:, :, i, :], ALU.subtract))


def aggregate(nc, io, dram, keep, NT, plan_steps):
    W = D + HEADS
    R = 4
    with ExitStack() as ctx:
        k = Kit(nc, ctx, "agg")
        node_ids = k.sb("node_ids", [128, NT * P], U16)
        acc = k.sb("acc", [P, NT, W])
        dst4 = k.sb("dst4", [128, R, 4], I32)
        feats = k.sb("feats", [128, R, 4, W])
        msg = k.sb("msg", [128, R, 4, W])
        sel = k.sb("sel", [128, R, 4, P])
        sel_bf = k.sb("sel_bf", [128, R, 4, P], BF16)
        selT = k.sb("selT", [P, R, 4, 128], BF16)
        z = k.sb("z", [128, 4, HEADS])
        ident_bf = k.sb("ident_bf", [128, 128], BF16)
        ps_selT = [k.ps(f"ps_selT{b}", [P, 8, 128], BF16)[:, 0:4, :] for b in range(2)]
        ps_pair = [k.ps(f"ps_pair{b}", [128, 4, 128])[:, :, 0:2 * HEADS] for b in range(2)]
        ps_sum = [k.ps(f"ps_sum{b}", [P, 512]) for b in range(R)]
        ring = lambda name: [k.sem(f"{name}{b}") for b in range(R)]
        passed_sp, passed_pool = k.sem("passed_sp"), k.sem("passed_pool")
        iota_ready, zeros_ready, z_done, acc_stored = k.sem("iota_ready"), k.sem("zeros_ready"), k.sem("z_done"), k.sem("acc_stored")
        ident_ready, dst_loaded, rows_loaded = k.sem("ident_ready"), ring("dst_loaded"), ring("rows_loaded")
        sel_bf_ready, sel_ready, selT_in_psum, selT_ready, pair_in_psum = ring("sel_bf_ready"), ring("sel_ready"), ring("selT_in_psum"), ring("selT_ready"), ring("pair_in_psum")
        z_ready, p_ready, msg_ready, sum_in_psum, sum_added = ring("z_ready"), ring("p_ready"), ring("msg_ready"), ring("sum_in_psum"), ring("sum_added")
        block = k.start()
        plan = keep["plan"]
        TURNS = plan_steps // R

        BLOCK, FIRST = 0, 1
        limits = (NT - 1, io["src"].shape[0])

        def before(sems, r, b, back):
            return sems[(b - back) % R], seen(r + 1 + (b - back) // R)

        def in_turns(eng, parts):
            depth = max(lag for lag, _, _ in parts)
            first = -(-depth // R) * R
            regs = [[eng.alloc_register(name=f"{k.stage}_{f.__name__}{b}") for b in range(R)] if field is not None else None for _, f, field in parts]

            def turns(i, j, n):
                for (lag, _, field), to in zip(parts, regs):
                    if field is not None:
                        q = lag % R
                        eng.load(to, plan[q:q + 1, field, ds(R * j + max(i - lag + q, 0), R)])
                for b in range(n):
                    for (lag, f, field), to in zip(parts, regs):
                        step = i + b - lag
                        if not isinstance(j, int) or 0 <= step < plan_steps:
                            value = () if field is None else (eng.snap(to[b], min_val=0, max_val=limits[field]),)
                            f(j + step // R, step % R, *value)

            for i in range(0, first, R):
                turns(i, 0, R)
            with eng.Fori(0, (plan_steps - first) // R, 1) as j:
                turns(first, j, R)
            for i in range(plan_steps, plan_steps + depth, R):
                turns(i, 0, min(R, plan_steps + depth - i))

        @block.sync
        def _(sp):
            def load_dst(r, b, first):
                wait_apart(sp, sel_bf_ready[b], seen(r), passed_sp)
                sp.dma_start(dst4[:, b, :], dram["dst_pad"][ds(first, 512)].rearrange("(p c) -> p c", c=4)).then_inc(dst_loaded[b], 16)

            def load_rows(r, b, first):
                wait_apart(sp, msg_ready[b], seen(r), passed_sp)
                sp.dma_start(feats[:, b], dram["edge_rows"][ds(first, 512), :].rearrange("(p c) w -> p c w", c=4)).then_inc(rows_loaded[b], 16)

            in_turns(sp, [(0, load_dst, FIRST), (3, load_rows, FIRST)])
            for b in range(R):
                sp.wait_ge(sum_added[b], seen(TURNS))
            sp.dma_start(dram["acc"].rearrange("(t p) w -> p t w", p=P), acc[:]).then_inc(acc_stored, 16)
            sp.wait_ge(acc_stored, seen(16))

        @block.gpsimd
        def _(pool):
            pool.iota(node_ids[:], pattern=[[1, NT * P]], base=0, channel_multiplier=0, allow_small_or_imprecise_dtypes=True).then_inc(iota_ready, 1)
            def sel_copy(r, b):
                wait_apart(pool, sum_in_psum[b], seen(r), passed_pool)
                wait_apart(pool, sel_bf_ready[b], seen(r + 1), passed_pool)
                pool.tensor_copy(sel[:, b], sel_bf[:, b]).then_inc(sel_ready[b], 1)

            in_turns(pool, [(0, sel_copy, None)])

        @block.vector
        def _(dve):
            dve.memset(acc[:], 0.0).then_inc(zeros_ready, 1)
            dve.tensor_copy(ident_bf[:], keep["ident"][:]).then_inc(ident_ready, 1)
            dve.wait_ge(iota_ready, seen(1))
            dve.wait_ge(zeros_ready, seen(1))

            def one_hot(r, b, n):
                dve.wait_ge(dst_loaded[b], seen((r + 1) * 16))
                dve.wait_ge(sel_ready[b], seen(r))
                dve.wait_ge(selT_in_psum[b], seen(r))
                dve.tensor_tensor(sel_bf[:, b], node_ids[:, None, ds(n * P, P)].broadcast_to([128, 4, P]),
                                  dst4[:, b, :, None].broadcast_to([128, 4, P]), ALU.is_equal).then_inc(sel_bf_ready[b], 1)

            def logits(r, b):
                base = dve.snap((R * r + b) * 3)
                dve.wait_ge(rows_loaded[b], seen((r + 1) * 16))
                dve.wait_ge(pair_in_psum[b], seen(r + 1))
                dve.tensor_tensor(z[:], feats[:, b, :, D:W], ps_pair[b % 2][:, :, 0:HEADS], ALU.add).then_inc(z_done, 1)
                dve.wait_ge(z_done, seen(base + 1))
                dve.scalar_tensor_tensor(out=z[:], in0=z[:], scalar=0.2, in1=z[:], op0=ALU.mult, op1=ALU.max).then_inc(z_done, 1)
                dve.wait_ge(z_done, seen(base + 2))
                dve.tensor_tensor(z[:], z[:], ps_pair[b % 2][:, :, HEADS:], ALU.subtract).then_inc(z_done, 1)
                dve.wait_ge(z_done, seen(base + 3))
                dve.wait_ge(sum_in_psum[b], seen(r))
                dve.tensor_scalar(msg[:, b, :, D:W], z[:], 0.0, None, ALU.min).then_inc(z_ready[b], 1)

            def messages(r, b):
                dve.wait_ge(p_ready[b], seen(r + 1))
                dve.tensor_tensor(msg[:, b, :, 0:D].rearrange("p c (h e) -> p c h e", e=DH), feats[:, b, :, 0:D].rearrange("p c (h e) -> p c h e", e=DH),
                                  msg[:, b, :, D:W, None].broadcast_to([128, 4, HEADS, DH]), ALU.mult).then_inc(msg_ready[b], 1)

            def add(r, b, n):
                dve.wait_ge(sum_in_psum[b], seen(r + 1))
                dve.wait_ge(*before(sum_added, r, b, 1))
                rows = acc[:, ds(n, 1), :]
                dve.tensor_tensor(rows, ps_sum[b][:, None, 0:W], rows, ALU.add).then_inc(sum_added[b], 1)

            in_turns(dve, [(3, logits, None), (0, one_hot, BLOCK), (5, add, BLOCK), (3, messages, None)])

        @block.tensor
        def _(pe):
            def transposes(r, b):
                pe.wait_ge(sel_bf_ready[b], seen(r + 1))
                pe.wait_ge(*before(selT_ready, r, b, 2))
                for c in range(4):
                    last = pe.transpose(ps_selT[b % 2][:, c, :], sel_bf[:, b, c, :], ident_bf[:])
                last.then_inc(selT_in_psum[b], 1)

            def expand(r, b, n):
                pe.wait_ge(selT_ready[b], seen(r + 1))
                pe.wait_ge(*before(z_ready, r, b, 2))
                for c in range(4):
                    for i in range(3):
                        last = pe.matmul(ps_pair[b % 2][:, c, :], selT[:, b, c, :], keep["pair_parts"][:, ds(n, 1), i, :], start=(i == 0), stop=(i == 2))
                last.then_inc(pair_in_psum[b], 1)

            def product(r, b):
                pe.wait_ge(sel_ready[b], seen(r + 1))
                pe.wait_ge(msg_ready[b], seen(r + 1))
                pe.wait_ge(sum_added[b], seen(r))
                for c in range(4):
                    last = pe.matmul(ps_sum[b][:, 0:W], sel[:, b, c, :], msg[:, b, c, :], start=(c == 0), stop=(c == 3))
                last.then_inc(sum_in_psum[b], 1)

            pe.wait_ge(ident_ready, seen(1))
            in_turns(pe, [(2, expand, BLOCK), (1, transposes, None), (4, product, None)])

        @block.scalar
        def _(act):
            def turn_selT(r, b):
                act.wait_ge(selT_in_psum[b], seen(r + 1))
                act.wait_ge(pair_in_psum[b], seen(r))
                act.activation(selT[:, b], ps_selT[b % 2][:], ACT.Copy).then_inc(selT_ready[b], 1)

            def exps(r, b):
                act.wait_ge(z_ready[b], seen(r + 1))
                act.activation(msg[:, b, :, D:W], msg[:, b, :, D:W], ACT.Exp).then_inc(p_ready[b], 1)

            act.preload_act_table(ACT.Exp)
            in_turns(act, [(3, exps, None), (1, turn_selT, None)])


def combine_and_route(nc, io, dram, keep, NT, CAP, SLOTS):
    N = io["x"].shape[0]
    W = D + HEADS
    NX = io["L0_ffn_gate_w"].shape[1]
    BIG = float(1 << 20)
    PIECES = -(-NX * SLOTS * D // (128 * 2048))
    with ExitStack() as ctx:
        k = Kit(nc, ctx, "comb")
        acc = k.sb("acc", [P, NT, W])
        rows = k.sb("rows", [P, NT, W])
        base = k.sb("base", [P, NT, D])
        z, p_self, den = k.sb("z", [P, NT, HEADS]), k.sb("p_self", [P, NT, HEADS]), k.sb("den", [P, NT, HEADS])
        vecs = k.sb("vecs", [P, 3, D])
        mean, gain, vtmp = k.sb("mean", [P, D]), k.sb("gain", [P, D]), k.sb("vtmp", [P, 2, D])
        ones = k.sb("ones", [P, P])
        upper = k.sb("upper", [P, P])
        gate_w, gate_b = k.sb("gate_w", [128, KC, NX]), k.sb("gate_b", [P, 1, NX])
        stats, ln_mean, ln_var, rstd, rtmp = k.sb("stats", [P, NT, 6]), k.sb("ln_mean", [P, NT, 1]), k.sb("ln_var", [P, NT]), k.sb("rstd", [P, NT, 1]), k.sb("rtmp", [P, 2, NT])
        h_tile, hT = k.sb("h_tile", [P, 2, D]), k.sb("hT", [128, 2, KC, P])
        zero_rows = k.sb("zero_rows", [128, 2048])
        logits, e, hot = k.sb("logits", [P, NT, NX]), k.sb("e", [P, NT, NX]), k.sb("hot", [P, NT, NX])
        expert_no = k.sb("expert_no", [P, 1, NX])
        total, upto = k.sb("total", [P, NT, NX]), k.sb("upto", [P, NT, NX])
        ones_row = k.sb("ones_row", [P, NT])
        col = {c: k.sb(f"col_{c}", [P, NT]) for c in ("top", "sum", "rec", "pick", "pos", "kept", "late", "slot")}
        slot_i = k.sb("slot_i", [P, NT], U32)
        ps_sum, ps_sq = k.ps("ps_sum", [P, 512]), k.ps("ps_sq", [P, 512])
        ps_t = [k.ps(f"ps_t{b}", [128, 4, 128])[:, 0:KC, 0:P] for b in range(2)]
        ps_gate, ps_pos, ps_tot = k.ps("ps_gate", [P, 512]), k.ps("ps_pos", [P, 512]), k.ps("ps_tot", [P, 512])
        n = {name: k.sem(name) for name in (
            "acc_loaded", "rows_loaded", "base_loaded", "vecs_loaded", "consts", "done", "z_ready", "p_ready", "out_ready", "sum_in_psum",
            "centred", "squared", "sq_in_psum", "x1_ready", "x1_stored", "stat_done", "h_ready", "gate_in_psum", "e_in", "e_out",
            "hot_ready", "pos_in_psum", "slot_ready", "zeroed")}
        n["scattered"] = k.gather_sem("scattered")
        pair = lambda name: [k.sem(f"{name}{b}") for b in range(2)]
        h_copied, hT_in_psum, hT_ready, gate_done = pair("h_copied"), pair("hT_in_psum"), pair("hT_ready"), pair("gate_done")
        block = k.start()

        @block.sync
        def _(sp):
            sp.dma_start(acc[:], dram["acc"].rearrange("(t p) w -> p t w", p=P)).then_inc(n["acc_loaded"], 16)
            sp.dma_start(rows[:], dram["node_rows"].rearrange("(t p) w -> p t w", p=P)).then_inc(n["rows_loaded"], 16)
            sp.dma_start(base[:], dram["mix_out"].rearrange("(t p) d -> p t d", p=P)).then_inc(n["base_loaded"], 16)
            for i, name in enumerate(("L0_gnn_bias", "L0_gnn_gamma", "L0_gnn_beta")):
                sp.dma_start(vecs[:, i, :], row(io[name], P)).then_inc(n["vecs_loaded"], 16)
            sp.dma_start(gate_w[:], io["L0_ffn_gate_w"].rearrange("(k p) n -> p k n", p=128)).then_inc(n["vecs_loaded"], 16)
            sp.dma_start(gate_b[:, 0, :], row(io["L0_ffn_gate_b"], P)).then_inc(n["vecs_loaded"], 16)
            sp.wait_ge(n["consts"], seen(6))
            flat = dram["buf"].rearrange("s d -> (s d)")
            size = NX * SLOTS * D
            piece = 128 * 2048
            done, pieces = 0, 0
            while done < size:
                width = min(piece, size - done) // 128
                sp.dma_start(flat[done:done + 128 * width].rearrange("(p c) -> p c", p=128), zero_rows[:, 0:width]).then_inc(n["zeroed"], 16)
                done += 128 * width
                pieces += 1
            assert done == size and pieces == PIECES
            sp.wait_ge(n["x1_ready"], seen(1))
            sp.dma_start(dram["x1"].rearrange("(t p) d -> p t d", p=P), acc[:, :, 0:D]).then_inc(n["x1_stored"], 16)
            sp.wait_ge(n["x1_stored"], seen(16))

        @block.gpsimd
        def _(pool):
            pool.memset(ones[:], 1.0).then_inc(n["consts"], 1)
            pool.memset(upper[:], 1.0).then_inc(n["consts"], 1)
            pool.memset(zero_rows[:], 0.0).then_inc(n["consts"], 1)
            pool.memset(ones_row[:], 1.0).then_inc(n["consts"], 1)
            pool.iota(expert_no[:, 0, :], pattern=[[1, NX]], base=0, channel_multiplier=0, allow_small_or_imprecise_dtypes=True).then_inc(n["consts"], 1)
            pool.wait_ge(n["consts"], seen(5))
            pool.affine_select(out=upper[:], in_=upper[:], compare_op=ALU.is_ge, fill=0.0, base=0, pattern=[[1, P]],
                               channel_multiplier=-1).then_inc(n["consts"], 1)
            pool.wait_ge(n["zeroed"], seen(PIECES * 16))
            pool.wait_ge(n["h_ready"], seen(NT))
            pool.wait_ge(n["slot_ready"], seen(1))
            for t in range(NT):
                pool.indirect_dma_start(dram["buf"], bass.IndirectOffsetOnAxis(ap=slot_i[:, t:t + 1], axis=0), rows[:, t, 0:D], None,
                                        bounds_check=NX * SLOTS - 1, oob_is_err=False).then_inc(n["scattered"], 16)
            pool.wait_ge(n["scattered"], NT * 16)

        @block.vector
        def _(dve):
            c = Chain(dve, n["done"])
            link = c.link
            tt, ts, stt = dve.tensor_tensor, dve.tensor_scalar, dve.scalar_tensor_tensor
            a_node, m_node = keep["a_node"], keep["m_node"]

            def heads(ap):
                return ap.rearrange("p t (h e) -> p t h e", e=DH)

            def by_head(ap):
                return ap[:, :, :, None].broadcast_to([P, NT, HEADS, DH])

            def by_row(ap):
                return ap[:, None, :].broadcast_to([P, NT, D])

            dve.wait_ge(n["consts"], seen(6))
            link(tt(z[:], a_node[:, :, 0:HEADS], a_node[:, :, HEADS:], ALU.add))
            link(stt(out=z[:], in0=z[:], scalar=0.2, in1=z[:], op0=ALU.mult, op1=ALU.max))
            tt(z[:], z[:], m_node[:], ALU.subtract).then_inc(n["z_ready"], 1)
            dve.wait_ge(n["p_ready"], seen(1))
            dve.wait_ge(n["rows_loaded"], seen(16))
            dve.wait_ge(n["acc_loaded"], seen(16))
            link(tt(heads(rows[:, :, 0:D]), heads(rows[:, :, 0:D]), by_head(p_self[:]), ALU.mult))
            link(tt(acc[:, :, 0:D], acc[:, :, 0:D], rows[:, :, 0:D], ALU.add))
            link(tt(den[:], acc[:, :, D:W], p_self[:], ALU.add))
            link(dve.reciprocal(den[:], den[:]))
            link(tt(heads(acc[:, :, 0:D]), heads(acc[:, :, 0:D]), by_head(den[:]), ALU.mult))
            dve.wait_ge(n["vecs_loaded"], seen(16 * 5))
            tt(acc[:, :, 0:D], acc[:, :, 0:D], by_row(vecs[:, 0, :]), ALU.add).then_inc(n["out_ready"], 1)
            dve.wait_ge(n["base_loaded"], seen(16))
            link(tt(base[:], base[:], by_row(vecs[:, 2, :]), ALU.add))
            dve.wait_ge(n["sum_in_psum"], seen(1))
            link(ts(mean[:], ps_sum[:, 0:D], 1.0 / N, None, ALU.mult))
            dve.wait_ge(n["out_ready"], seen(1))
            tt(acc[:, :, 0:D], acc[:, :, 0:D], by_row(mean[:]), ALU.subtract).then_inc(n["centred"], 1)
            dve.wait_ge(n["sq_in_psum"], seen(1))
            link(ts(gain[:], ps_sq[:, 0:D], 1.0 / N, None, ALU.mult))
            rsqrt_eps(dve, c, mean[:], gain[:], (vtmp[:, 0, :], vtmp[:, 1, :]))
            link(tt(gain[:], mean[:], vecs[:, 1, :], ALU.mult))
            dve.wait_ge(n["centred"], seen(1))
            link(tt(acc[:, :, 0:D], acc[:, :, 0:D], by_row(gain[:]), ALU.mult))
            tt(acc[:, :, 0:D], acc[:, :, 0:D], base[:], ALU.add).then_inc(n["x1_ready"], 1)
            dve.wait_ge(n["x1_ready"], seen(1))
            with dve.Fori(0, NT, 1) as t:
                dve.bn_stats(stats[:, ds(t, 1), :], acc[:, ds(t, 1), 0:D]).then_inc(n["stat_done"], 1)
            dve.wait_ge(n["stat_done"], seen(NT))
            aggregate_stats(dve, c, ln_mean[:, :, 0], ln_var[:], stats, D)
            rsqrt_eps(dve, c, rstd[:, :, 0], ln_var[:], (rtmp[:, 0, :], rtmp[:, 1, :]))
            with dve.Fori(0, NT, 1) as t:
                ts(rows[:, ds(t, 1), 0:D], acc[:, ds(t, 1), 0:D], ln_mean[:, ds(t, 1), 0], rstd[:, ds(t, 1), 0],
                   ALU.subtract, ALU.mult).then_inc(n["h_ready"], 1)
            for b in range(2):
                dve.wait_ge(gate_done[b], seen(NT // 2))

            def by_token(ap):
                return ap[:, :, None].broadcast_to([P, NT, NX])

            link(tt(logits[:], ps_gate[:, 0:NT * NX].rearrange("p (t x) -> p t x", x=NX), gate_b[:].broadcast_to([P, NT, NX]), ALU.add))
            link(dve.tensor_reduce(col["top"][:], logits[:], AX.X, ALU.max))
            tt(logits[:], logits[:], by_token(col["top"]), ALU.subtract).then_inc(n["e_in"], 1)
            dve.wait_ge(n["e_out"], seen(1))
            link(dve.tensor_reduce(col["sum"][:], e[:], AX.X, ALU.add))
            link(dve.tensor_reduce(col["top"][:], e[:], AX.X, ALU.max))
            link(dve.reciprocal(col["rec"][:], col["sum"][:]))
            link(tt(hot[:], e[:], by_token(col["top"]), ALU.is_lt))
            link(stt(out=hot[:], in0=hot[:], scalar=float(NX), in1=expert_no[:].broadcast_to([P, NT, NX]), op0=ALU.mult, op1=ALU.add))
            link(dve.tensor_reduce(col["pick"][:], hot[:], AX.X, ALU.min))
            tt(hot[:], expert_no[:].broadcast_to([P, NT, NX]), by_token(col["pick"]), ALU.is_equal).then_inc(n["hot_ready"], 1)
            link(tt(col["rec"][:], col["rec"][:], col["top"][:], ALU.mult))
            dve.wait_ge(n["pos_in_psum"], seen(1))
            link(dve.tensor_copy(total[:], ps_tot[:, 0:NT * NX].rearrange("p (t x) -> p t x", x=NX)))
            for x in range(NX):
                c.step(dve.tensor_tensor_scan(upto[:, :, x], ones_row[:], total[:, :, x], 0.0, ALU.mult, ALU.add))
            c.after()
            link(tt(upto[:], upto[:], total[:], ALU.subtract))
            link(tt(upto[:], upto[:], ps_pos[:, 0:NT * NX].rearrange("p (t x) -> p t x", x=NX), ALU.add))
            dve.wait_ge(n["hot_ready"], seen(1))
            link(tt(upto[:], upto[:], hot[:], ALU.mult))
            link(dve.tensor_reduce(col["pos"][:], upto[:], AX.X, ALU.add))
            link(ts(col["pos"][:], col["pos"][:], -1.0, None, ALU.add))
            link(ts(col["kept"][:], col["pos"][:], float(CAP), None, ALU.is_lt))
            link(ts(col["late"][:], col["pos"][:], float(CAP), BIG, ALU.is_ge, ALU.mult))
            link(ts(col["slot"][:], col["pick"][:], float(SLOTS), None, ALU.mult))
            link(tt(col["pos"][:], col["pos"][:], col["late"][:], ALU.add))
            link(tt(col["late"][:], col["slot"][:], col["pos"][:], ALU.add))
            dve.tensor_copy(slot_i[:], col["late"][:]).then_inc(n["slot_ready"], 1)
            link(ts(col["pos"][:], col["pos"][:], float(CAP - 1), None, ALU.min))
            link(tt(col["slot"][:], col["slot"][:], col["pos"][:], ALU.add))
            link(dve.tensor_copy(keep["slot"][:], col["slot"][:]))
            link(tt(keep["weight"][:], col["rec"][:], col["kept"][:], ALU.mult))

        @block.tensor
        def _(pe):
            pe.wait_ge(n["consts"], seen(6))
            pe.wait_ge(n["vecs_loaded"], seen(16 * 5))
            for ready, what, bank, done in (("out_ready", acc, ps_sum, "sum_in_psum"), ("squared", rows, ps_sq, "sq_in_psum")):
                pe.wait_ge(n[ready], seen(1))
                pe.matmul(bank[:, 0:D], ones[:], what[:, 0, 0:D], start=True, stop=False)
                with pe.Fori(1, NT - 1, 1) as t:
                    pe.matmul(bank[:, 0:D], ones[:], what[:, ds(t, 1), 0:D], start=False, stop=False, skip_group_check=True)
                pe.matmul(bank[:, 0:D], ones[:], what[:, NT - 1, 0:D], start=False, stop=True).then_inc(n[done], 1)
            with pe.Fori(0, NT // 2, 1) as g:
                for b in range(2):
                    pe.wait_ge(h_copied[b], seen(g + 1))
                    pe.wait_ge(hT_ready[b], seen(g))
                    for kc in range(KC):
                        last = pe.transpose(ps_t[b][:, kc, :], h_tile[:, b, kc * 128:(kc + 1) * 128], keep["ident"][0:P, 0:P])
                    last.then_inc(hT_in_psum[b], 1)
                for b in range(2):
                    pe.wait_ge(hT_ready[b], seen(g + 1))
                    for kc in range(KC):
                        last = pe.matmul(ps_gate[:, ds((2 * g + b) * NX, NX)], hT[:, b, kc, :], gate_w[:, kc, :], start=(kc == 0), stop=(kc == KC - 1))
                    last.then_inc(gate_done[b], 1)
            pe.wait_ge(n["hot_ready"], seen(1))
            flat = hot[:].rearrange("p t x -> p (t x)")
            pe.matmul(ps_pos[:, 0:NT * NX], upper[:], flat, start=True, stop=True)
            pe.matmul(ps_tot[:, 0:NT * NX], ones[:], flat, start=True, stop=True).then_inc(n["pos_in_psum"], 1)

        @block.scalar
        def _(act):
            act.wait_ge(n["z_ready"], seen(1))
            act.activation(p_self[:], z[:], ACT.Exp).then_inc(n["p_ready"], 1)
            act.wait_ge(n["centred"], seen(1))
            act.activation(rows[:, :, 0:D], acc[:, :, 0:D], ACT.Square).then_inc(n["squared"], 1)
            with act.Fori(0, NT // 2, 1) as g:
                for b in range(2):
                    act.wait_ge(n["h_ready"], seen(2 * g + b + 1))
                    act.wait_ge(hT_in_psum[b], seen(g))
                    act.activation(h_tile[:, b, None, :], rows[:, ds(2 * g + b, 1), 0:D], ACT.Copy).then_inc(h_copied[b], 1)
                for b in range(2):
                    act.wait_ge(hT_in_psum[b], seen(g + 1))
                    act.wait_ge(gate_done[b], seen(g))
                    act.activation(hT[:, b], ps_t[b], ACT.Copy).then_inc(hT_ready[b], 1)
            act.wait_ge(n["e_in"], seen(1))
            act.activation(e[:], logits[:], ACT.Exp).then_inc(n["e_out"], 1)


def experts(nc, io, dram, keep, TILE, SLOTS):
    NX, _, FF = io["L0_ffn_w1"].shape
    FC = FF // 128
    T2 = 2 * TILE
    CX = SLOTS // T2
    assert NX % 2 == 0 and CX % 2 == 0 and CX * T2 == SLOTS
    TURN = 2 * CX
    with ExitStack() as ctx:
        k = Kit(nc, ctx, "exp")
        w1, w2 = k.sb("w1", [128, 2, KC, FF]), k.sb("w2", [128, 2, FC, D])
        b1, b2 = k.sb("b1", [128, 2, FC]), k.sb("b2", [TILE, 2, 1, D])
        tok, tokT = k.sb("tok", [TILE, 2, 2, D]), k.sb("tokT", [128, 2, KC, T2])
        uT = k.sb("uT", [128, FC, T2])
        y = k.sb("y", [TILE, 2, 2, D])
        ps_t = [k.ps(f"ps_t{b}", [128, 512])[:, 0:KC * T2].rearrange("p (k n) -> p k n", k=KC) for b in range(2)]
        ps_u = [k.ps(f"ps_u{f}", [128, 512])[:, 0:KC * T2].rearrange("p (k n) -> p k n", k=2) for f in range(FC // 2)]
        ps_y = [k.ps(f"ps_y{b}", [128, 512])[0:TILE].rearrange("p (t d) -> p t d", t=2) for b in range(2)]
        pair = lambda name: [k.sem(f"{name}{b}") for b in range(2)]
        w_loaded, tok_loaded, tokT_in_psum, tokT_ready = pair("w_loaded"), pair("tok_loaded"), pair("tokT_in_psum"), pair("tokT_ready")
        u_in_psum, relu_done = ([k.sem(f"{n}{f}") for f in range(FC // 2)] for n in ("u_in_psum", "relu_done"))
        y_in_psum, y_ready, y_stored = pair("y_in_psum"), pair("y_ready"), pair("y_stored")
        block = k.start()
        buf = dram["buf"].rearrange("(c t p) d -> c p t d", t=2, p=TILE)
        ybuf = dram["ybuf"].rearrange("(c t p) d -> c p t d", t=2, p=TILE)

        class Chunk:

            def __init__(self, i, r):
                self.k, self.r = i, r
                self.i = TURN * r + i
                self.b, self.m = i % 2, (TURN // 2) * r + i // 2
                self.m_before = (TURN // 2) * r + (i - 1) // 2
                self.wb, self.wm = (i // CX) % 2, r + i // TURN

        def run(*steps):
            def turn(i, r):
                for lag, f in steps:
                    if r is None and not 0 <= i - lag < NX * CX:
                        continue
                    f(Chunk(i - lag, 0 if r is None else r))
            return turn

        def loop(eng, *steps):
            turn = run(*steps)
            turn(0, None)
            with eng.Fori(0, NX // 2 - 1, 1) as r:
                for i in range(1, TURN + 1):
                    turn(i, r)
            for i in range(NX * CX - TURN + 1, NX * CX + 1):
                turn(i, None)

        @block.sync
        def _(sp):
            def load_weights(x, slot, before):
                for b in range(2):
                    sp.wait_ge(y_ready[b], seen(before))
                one = ds(x, 1)
                sp.dma_start(w1[:, slot], io["L0_ffn_w1"][one].rearrange("x (k p) n -> p (x k) n", p=128)).then_inc(w_loaded[slot], 16)
                sp.dma_start(w2[:, slot], io["L0_ffn_w2"][one].rearrange("x (k p) n -> p (x k) n", p=128)).then_inc(w_loaded[slot], 16)
                sp.dma_start(b1[:, slot], io["L0_ffn_b1"][one].rearrange("x (k p) -> p (x k)", p=128),
                             allow_slow_non_contiguous=True).then_inc(w_loaded[slot], 16)
                sp.dma_start(b2[:, slot], io["L0_ffn_b2"][one][None].broadcast_to([TILE, 1, D])).then_inc(w_loaded[slot], 16)

            def load(c):
                if c.k == 0:
                    load_weights(0, 0, 0)
                if c.k % CX == 2 and c.k // CX != NX - 1:
                    e = c.k // CX
                    load_weights(e + 1 + 2 * c.r, (e + 1) % 2, e * (CX // 2) + CX * c.r)
                sp.wait_ge(tokT_in_psum[c.b], seen(c.m))
                sp.dma_start(tok[:, c.b], buf[ds(c.i, 1)].rearrange("c p t d -> p (c t) d")).then_inc(tok_loaded[c.b], 16)

            def store(c):
                sp.wait_ge(y_ready[c.b], seen(c.m + 1))
                sp.dma_start(ybuf[ds(c.i, 1)].rearrange("c p t d -> p (c t) d"), y[:, c.b]).then_inc(y_stored[c.b], 16)

            loop(sp, (0, load), (1, store))
            for b in range(2):
                sp.wait_ge(y_stored[b], seen(NX * CX // 2 * 16))

        @block.vector
        def _(dve):
            def take(c):
                dve.wait_ge(y_in_psum[c.b], seen(c.m + 1))
                dve.wait_ge(y_stored[c.b], seen(c.m * 16))
                dve.tensor_tensor(y[:, c.b], ps_y[c.b], b2[:, c.wb].broadcast_to([TILE, 2, D]), ALU.add).then_inc(y_ready[c.b], 1)

            loop(dve, (1, take))

        @block.tensor
        def _(pe):
            def transposes(c):
                pe.wait_ge(tok_loaded[c.b], seen((c.m + 1) * 16))
                pe.wait_ge(tokT_ready[c.b], seen(c.m))
                for kc in range(KC):
                    for t in range(2):
                        last = pe.transpose(ps_t[c.b][:, kc, t * TILE:(t + 1) * TILE], tok[:, c.b, t, kc * 128:(kc + 1) * 128], keep["ident"][0:TILE, 0:TILE])
                last.then_inc(tokT_in_psum[c.b], 1)

            def down(c):
                pe.wait_ge(y_ready[c.b], seen(c.m))
                for f in range(FC // 2):
                    pe.wait_ge(relu_done[f], seen(c.i + 1))
                for t in range(2):
                    for f in range(FC):
                        last = pe.matmul(ps_y[c.b][:, t, :], uT[:, f, t * TILE:(t + 1) * TILE], w2[:, c.wb, f, :], start=(f == 0), stop=(f == FC - 1))
                last.then_inc(y_in_psum[c.b], 1)

            def up(c):
                pe.wait_ge(w_loaded[c.wb], seen((c.wm + 1) * 64))
                pe.wait_ge(tokT_ready[c.b], seen(c.m + 1))
                for f in range(FC):
                    if f % 2 == 0:
                        pe.wait_ge(relu_done[f // 2], seen(c.i))
                    for kc in range(KC):
                        last = pe.matmul(ps_u[f // 2][:, f % 2, :], w1[:, c.wb, kc, f * 128:(f + 1) * 128], tokT[:, c.b, kc, :],
                                         start=(kc == 0), stop=(kc == KC - 1))
                    if f % 2:
                        last.then_inc(u_in_psum[f // 2], 1)

            loop(pe, (0, transposes), (1, down), (0, up))

        @block.scalar
        def _(act):
            def take_T(c):
                act.wait_ge(tokT_in_psum[c.b], seen(c.m + 1))
                act.activation(tokT[:, c.b], ps_t[c.b], ACT.Copy).then_inc(tokT_ready[c.b], 1)

            def relu(c):
                act.wait_ge(w_loaded[c.wb], seen((c.wm + 1) * 64))
                act.wait_ge(y_in_psum[1 - c.b], seen(c.m_before + 1))
                for f in range(FC // 2):
                    act.wait_ge(u_in_psum[f], seen(c.i + 1))
                    for h in range(2):
                        last = act.activation(uT[:, 2 * f + h, :], ps_u[f][:, h, :], ACT.Relu, bias=b1[:, c.wb, 2 * f + h:2 * f + h + 1])
                    last.then_inc(relu_done[f], 1)

            loop(act, (0, take_T), (0, relu))


def collect(nc, io, dram, keep, NT, out):
    LARGEST = 3.4028234663852886e38
    with ExitStack() as ctx:
        k = Kit(nc, ctx, "coll")
        x1, got = k.sb("x1", [P, NT, D]), k.sb("got", [P, NT, D])
        bound, real, finite, clean = (k.sb(n, [P, 2, D], dt) for n, dt in (("bound", F32), ("real", F32), ("finite", F32), ("clean", F32)))
        n = {name: k.sem(name) for name in ("x1_loaded", "stored")}
        gathered = [k.gather_sem(f"gathered{i}") for i in range(NT // 2)]
        done = k.sem("done")
        ready = k.sem("ready")
        block = k.start()
        x1_v = dram["x1"].rearrange("(t p) d -> p t d", p=P)
        out_v = out.rearrange("(t p) d -> p t d", p=P)

        @block.sync
        def _(sp):
            sp.dma_start(x1[:], x1_v).then_inc(n["x1_loaded"], 16)
            with sp.Fori(0, NT // 2, 1) as g:
                sp.wait_ge(ready, seen(g + 1))
                sp.dma_start(out_v[:, ds(2 * g, 2), :], x1[:, ds(2 * g, 2), :]).then_inc(n["stored"], 16)
            sp.wait_ge(n["stored"], seen(NT // 2 * 16))

        @block.gpsimd
        def _(pool):
            for t in range(NT):
                pool.indirect_dma_start(got[:, t, :], None, dram["ybuf"], bass.IndirectOffsetOnAxis(ap=keep["slot"][:, t:t + 1], axis=0)).then_inc(gathered[t // 2], 16)

        @block.vector
        def _(dve):
            c = Chain(dve, done)
            link = c.link
            dve.wait_ge(n["x1_loaded"], seen(16))
            for g in range(NT // 2):
                rows = got[:, 2 * g:2 * g + 2, :]
                dve.wait_ge(gathered[g], 32)
                link(dve.tensor_tensor(rows, rows, keep["weight"][:, 2 * g:2 * g + 2, None].broadcast_to([P, 2, D]), ALU.mult))
                c.step(dve.tensor_scalar(bound[:], rows, 1.0e4, -1.0e4, ALU.min, ALU.max))
                c.step(dve.tensor_tensor(real[:], rows, rows, ALU.is_equal))
                c.step(dve.tensor_scalar(finite[:], rows, 0.0, 0.0, ALU.mult, ALU.is_equal))
                link(dve.memset(clean[:], 0.0))
                link(dve.copy_predicated(clean[:], real[:].bitcast(U32), bound[:]))
                link(dve.copy_predicated(clean[:], finite[:].bitcast(U32), rows))
                link(dve.tensor_tensor(x1[:, 2 * g:2 * g + 2, :], x1[:, 2 * g:2 * g + 2, :], clean[:], ALU.add))
                dve.sem_inc(ready, 1)


def graph_block_kernel(nc, io, out):
    N = io["x"].shape[0]
    NT = N // P
    E = io["src"].shape[0]
    depth = io["L0_mix_Wq"].shape[0]
    NX = io["L0_ffn_gate_w"].shape[1]
    CAP = max(1, -(-5 * N // (4 * NX)))
    TILE = -(-CAP // 8)
    SLOTS = 8 * TILE
    plan_steps = -(-(E // 512 + NT) // 110) * 110

    def scratch(name, shape, dt=F32):
        return nc.dram_tensor(name, shape, dt, kind="Internal").ap()

    dram = {
        "src": io["src"].bitcast(U32).rearrange("(p c) -> p c", p=P),
        "res": scratch("res_dram", (1, N, D)),
        "mix_out": scratch("mix_dram", (N, D)),
        "node_rows": scratch("node_rows_dram", (N, D + HEADS)),
        "a_edge": scratch("a_edge_dram", (P, E // P * HEADS)),
        "scan": scratch("scan_dram", (E, HEADS)),
        "carry": scratch("carry_dram", (P, HEADS)),
        "rowptr": scratch("rowptr_dram", (N + 1,)),
        "plan": scratch("plan_dram", (2, plan_steps), I32),
        "edge_rows": scratch("edge_rows_dram", (E + 512, D + HEADS)),
        "dst_pad": scratch("dst_pad_dram", (E + 512,), I32),
        "acc": scratch("acc_dram", (N, D + HEADS)),
        "x_plus_xn": scratch("x_plus_xn_dram", (N, D)),
        "x1": scratch("x1_dram", (N, D)),
        "buf": scratch("buf_dram", (NX * SLOTS, D)),
        "ybuf": scratch("ybuf_dram", (NX * SLOTS, D)),
        "hT": scratch("hT_dram", (NT // 2, 128, KC, 2 * P)),
    }
    with ExitStack() as ctx:
        k = Kit(nc, ctx, "keep")
        keep = {
            "ident": k.sb("ident", [128, 128]),
            "a_node": k.sb("a_node", [P, NT, 2 * HEADS]),
            "m_node": k.sb("m_node", [P, NT, HEADS]),
            "pair_parts": k.sb("pair_parts", [P, NT, 3, 2 * HEADS], BF16),
            "plan": k.sb("plan", [4, 2, plan_steps + 8], I32),
            "slot": k.sb("slot", [P, NT], U32),
            "weight": k.sb("weight", [P, NT]),
        }
        prepare(nc, io, dram, keep, NT)
        mix(nc, io, dram, keep, NT)
        segments(nc, io, dram, keep, NT, plan_steps)
        aggregate(nc, io, dram, keep, NT, plan_steps)
        combine_and_route(nc, io, dram, keep, NT, CAP, SLOTS)
        experts(nc, io, dram, keep, TILE, SLOTS)
        collect(nc, io, dram, keep, NT, out)


def kernel(**inputs):
    import numpy as _np
    import concourse.bacc as _bacc
    from concourse import mybir as _mybir
    from concourse.bass_utils import run_bass_kernel_spmd as _run

    nc = _bacc.Bacc("TRN2", target_bir_lowering=False, num_devices=1)
    arrays, args = {}, {}
    for name, a in inputs.items():
        a = _np.ascontiguousarray(a)
        arrays[f"in_{name}_dram"] = a
        args[name] = nc.dram_tensor(f"in_{name}_dram", a.shape, _mybir.dt.from_np(a.dtype), kind="ExternalInput").ap()
    out = nc.dram_tensor("out_0_dram", inputs["x"].shape, _mybir.dt.float32, kind="ExternalOutput").ap()
    graph_block_kernel(nc, args, out)
    r = _run(nc, [arrays], core_ids=[0])
    return r.results[0]["out_0_dram"]
```

```python
import math
from contextlib import ExitStack

import concourse.bass as bass
from concourse import mybir

F32 = mybir.dt.float32
BF16 = mybir.dt.bfloat16
I32 = mybir.dt.int32
U32 = mybir.dt.uint32
U16 = mybir.dt.uint16
F32R = mybir.dt.float32r
ALU = mybir.AluOpType
ACT = mybir.ActivationFunctionType
AX = mybir.AxisListType

P = 125
D = 256
KC = D // 128
HEADS = 8
DH = D // HEADS
EPS = 1e-5
FAR = -1.0e30
ds = bass.ds


class Kit:

    def __init__(self, nc, ctx, stage):
        self.nc, self.ctx, self.stage, self.sems, self.unraised = nc, ctx, stage, [], []
        ctx.callback(self.clear)

    def start(self):
        engines = (self.nc.sync, self.nc.scalar, self.nc.vector, self.nc.tensor, self.nc.gpsimd)
        for i, sem in enumerate(self.sems):
            if not any(sem is s for s in self.unraised):
                engines[i % len(engines)].sem_inc(sem, 1)
        self.nc.all_engine_barrier()
        return self.ctx.enter_context(self.nc.Block())

    def clear(self):
        if self.sems:
            self.nc.clear_and_free_semaphores(self.sems)
            self.nc.all_engine_barrier()

    def sb(self, name, shape, dt=F32):
        return self.ctx.enter_context(self.nc.sbuf_tensor(f"{self.stage}_{name}", shape, dt))

    def share(self, *groups):
        sizes = [sum(shape if name is None else 4 * math.prod(shape[1:]) for name, shape in group) for group in groups]
        made = []
        for group, size in zip(groups, sizes):
            whole = [*group, (None, max(sizes) - size)]
            with ExitStack() as part:
                ctx = part if group is not groups[-1] else self.ctx
                took = [ctx.enter_context(self.nc.sbuf_tensor(f"{self.stage}_{name or f'gap{len(made)}_{i}'}", shape if name else [128, shape // 4], F32))
                        for i, (name, shape) in enumerate(whole) if name or shape]
                made.append([t for t, (name, _) in zip(took, [x for x in whole if x[0] or x[1]]) if name])
        return made

    def ps(self, name, shape, dt=F32):
        return self.ctx.enter_context(self.nc.psum_tensor(f"{self.stage}_{name}", shape, dt))

    def sem(self, name):
        self.sems.append(self.nc.alloc_semaphore(f"{self.stage}_{name}"))
        return self.sems[-1]

    def gather_sem(self, name):
        self.unraised.append(self.sem(name))
        return self.sems[-1]


def seen(count):
    return count + 1


class Chain:

    def __init__(self, eng, sem):
        self.eng, self.sem, self.base, self.n = eng, sem, 0, 0

    def at(self, base):
        self.base, self.n = base, 0

    def step(self, ins):
        ins.then_inc(self.sem, 1)
        self.n += 1

    def after(self):
        self.eng.wait_ge(self.sem, seen(self.base + self.n))

    def link(self, ins):
        self.step(ins)
        self.after()



def rsqrt_eps(dve, chain, out, var, tmp):
    v, t = tmp
    chain.link(dve.tensor_scalar(v, var, EPS, None, ALU.add))
    chain.link(dve.tensor_scalar(t.bitcast(I32), v.bitcast(I32), 1, None, ALU.arith_shift_right))
    chain.link(dve.tensor_scalar(out.bitcast(I32), t.bitcast(I32), -1.0, float(0x5F3759DF), ALU.mult, ALU.add))
    for _ in range(3):
        chain.link(dve.tensor_tensor(t, out, out, ALU.mult))
        chain.link(dve.tensor_tensor(t, t, v, ALU.mult))
        chain.link(dve.tensor_scalar(t, t, -0.5, 1.5, ALU.mult, ALU.add))
        if _ < 2:
            chain.link(dve.tensor_tensor(out, out, t, ALU.mult))
    chain.link(dve.tensor_tensor(out, out, t, ALU.mult))


RSQRT_STEPS = 15


AGGREGATE_STEPS = 6


def aggregate_stats(dve, chain, mean, var, stats, size):
    even, odd, dev_even, dev_odd = stats[:, :, 1], stats[:, :, 4], stats[:, :, 2], stats[:, :, 5]
    chain.step(dve.tensor_tensor(mean, even, odd, ALU.add))
    chain.step(dve.tensor_tensor(var, even, odd, ALU.subtract))
    chain.link(dve.tensor_tensor(dev_even, dev_even, dev_odd, ALU.add))
    chain.step(dve.tensor_scalar(mean, mean, 0.5, None, ALU.mult))
    chain.link(dve.scalar_tensor_tensor(out=var, in0=var, scalar=0.25, in1=var, op0=ALU.mult, op1=ALU.mult))
    chain.link(dve.scalar_tensor_tensor(out=var, in0=dev_even, scalar=1.0 / size, in1=var, op0=ALU.mult, op1=ALU.add))


def wait_apart(eng, sem, value, passed):
    eng.wait_ge(sem, value)
    eng.sem_inc(passed, 1)


def split_high(dve, high, whole):
    return dve.tensor_copy(high.bitcast(F32R), whole)


def split_rest(dve, rest, whole, high):
    return dve.tensor_tensor(rest.bitcast(F32R), whole, high, ALU.subtract)


def product_of_parts(pe, out, lhs, rhs, start, stop):
    order = ((0, 0), (0, 1), (1, 0))
    for i, (a, b) in enumerate(order):
        last = pe.matmul(out, lhs[a].bitcast(F32R), rhs[b].bitcast(F32R), start=start and i == 0, stop=stop and i == len(order) - 1)
    return last


def row(vec, parts):
    return vec.rearrange("(a n) -> a n", a=1).broadcast_to([parts, vec.shape[0]])


def prepare(nc, io, dram, keep, NT):
    with ExitStack() as ctx:
        k = Kit(nc, ctx, "prep")
        x_all = k.sb("x_all", [P, NT, D])
        x_twice = k.sb("x_twice", [P, NT, D])
        stats = k.sb("stats", [P, NT, 6])
        mean, var = k.sb("mean", [P, NT, 1]), k.sb("var", [P, NT])
        rstd = k.sb("rstd", [P, NT, 1])
        rtmp = k.sb("rtmp", [P, 2, NT])
        w = k.sb("w", [128, KC, D + 2 * HEADS])
        att = k.sb("att", [128, 2, D])
        w_att = k.sb("w_att", [128, KC, 2, D])
        xn_tile = k.sb("xn_tile", [P, 2, D])
        xnT = k.sb("xnT", [128, 2, KC, P])
        table = k.sb("table", [P, NT, D + 2 * HEADS])
        ps_t = [k.ps(f"ps_t{b}", [128, KC, P]) for b in range(2)]
        ps_h = [k.ps(f"ps_h{b}", [P, 512]) for b in range(2)]
        x_loaded, w_loaded = k.sem("x_loaded"), k.sem("w_loaded")
        ident_zero, ident_ready = k.sem("ident_zero"), k.sem("ident_ready")
        dve_done = k.sem("dve_done")
        w_ready = k.sem("w_ready")
        xn_ready = k.sem("xn_ready")
        xn_copied = [k.sem(f"xn_copied{b}") for b in range(2)]
        xnT_in_psum = [k.sem(f"xnT_in_psum{b}") for b in range(2)]
        xnT_ready = [k.sem(f"xnT_ready{b}") for b in range(2)]
        xh_in_psum = [k.sem(f"xh_in_psum{b}") for b in range(2)]
        xh_ready = [k.sem(f"xh_ready{b}") for b in range(2)]
        ad_kept, x_copied, sum_ready = k.sem("ad_kept"), k.sem("x_copied"), k.sem("sum_ready")
        stored, edges_copied, pad_ready = k.sem("stored"), k.sem("edges_copied"), k.sem("pad_ready")
        pad = k.sb("pad", [1, 512], U16)
        E = io["src"].shape[0]
        dst, dst_short = k.sb("dst", [P, E // P], I32), k.sb("dst_short", [P, E // P], U16)
        dst_loaded, dst_ready = k.sem("dst_loaded"), k.sem("dst_ready")
        block = k.start()

        @block.sync
        def _(sp):
            sp.dma_start(x_all[:], io["x"].rearrange("(t p) d -> p t d", p=P)).then_inc(x_loaded, 16)
            sp.dma_start(w[:, :, 0:D], io["L0_gnn_W"].rearrange("(k p) d -> p k d", p=128)).then_inc(w_loaded, 16)
            for i, name in enumerate(("L0_gnn_att_src", "L0_gnn_att_dst")):
                sp.dma_start(att[:, i, :], row(io[name].rearrange("h d -> (h d)"), 128)).then_inc(w_loaded, 16)
            sp.dma_start(dst[:], io["dst"].rearrange("(p c) -> p c", p=P)).then_inc(dst_loaded, 16)
            sp.wait_ge(dst_ready, seen(1))
            sp.dma_start(dram["dst_pad"][0:E].rearrange("(p c) -> p c", p=P), dst_short[:]).then_inc(edges_copied, 16)
            sp.wait_ge(pad_ready, seen(1))
            sp.dma_start(dram["dst_pad"][E:E + 512].rearrange("(a c) -> a c", a=1), pad[:]).then_inc(edges_copied, 16)
            sp.wait_ge(xn_ready, seen(NT))
            sp.dma_start(dram["res"][0].rearrange("(t p) d -> p t d", p=P), x_all[:]).then_inc(stored, 16)
            for b in range(2):
                sp.wait_ge(xh_ready[b], seen(NT // 2))
            sp.wait_ge(sum_ready, seen(1))
            sp.dma_start(dram["x_plus_xn"].rearrange("(t p) d -> p t d", p=P), x_twice[:]).then_inc(stored, 16)
            sp.dma_start(dram["node_rows"].rearrange("(t p) d -> p t d", p=P), table[:, :, 0:D + HEADS]).then_inc(stored, 16)
            sp.wait_ge(stored, seen(48))
            sp.dma_start(dram["edge_rows"][E:E + 512, :], dram["node_rows"][0:512, :]).then_inc(stored, 16)
            sp.wait_ge(stored, seen(64))
            sp.wait_ge(edges_copied, seen(32))

        @block.gpsimd
        def _(pool):
            pool.memset(pad[:], 1 << 14).then_inc(pad_ready, 1)
            pool.memset(keep["ident"][:], 0.0).then_inc(ident_zero, 1)
            pool.wait_ge(ident_zero, seen(1))
            pool.affine_select(out=keep["ident"][:], in_=keep["ident"][:], compare_op=ALU.not_equal, fill=1.0,
                               base=0, pattern=[[-1, 128]], channel_multiplier=1).then_inc(ident_ready, 1)

        @block.vector
        def _(dve):
            chain = Chain(dve, dve_done)
            dve.wait_ge(dst_loaded, seen(16))
            dve.tensor_copy(dst_short[:], dst[:]).then_inc(dst_ready, 1)
            dve.wait_ge(w_loaded, seen(48))
            chain.link(dve.tensor_tensor(w_att[:, :, 0, :], w[:, :, 0:D], att[:, 0:1, :].broadcast_to([128, KC, D]), ALU.mult))
            chain.link(dve.tensor_tensor(w_att[:, :, 1, :], w[:, :, 0:D], att[:, 1:2, :].broadcast_to([128, KC, D]), ALU.mult))
            for kc in range(KC):
                dve.tensor_reduce(w[:, kc, D:D + 2 * HEADS], w_att[:, kc].rearrange("p a (h e) -> p (a h) e", e=DH),
                                  AX.X, ALU.add).then_inc(w_ready, 1)
            dve.wait_ge(x_loaded, seen(16))
            dve.tensor_copy(x_twice[:], x_all[:]).then_inc(x_copied, 1)
            base = chain.n
            with dve.Fori(0, NT, 1) as t:
                dve.bn_stats(stats[:, ds(t, 1), :], x_all[:, ds(t, 1), :]).then_inc(dve_done, 1)
            dve.wait_ge(dve_done, seen(base + NT))
            chain.at(base + NT)
            aggregate_stats(dve, chain, mean[:, :, 0], var[:], stats, D)
            rsqrt_eps(dve, chain, rstd[:, :, 0], var[:], (rtmp[:, 0, :], rtmp[:, 1, :]))
            with dve.Fori(0, NT, 1) as t:
                dve.tensor_scalar(x_all[:, ds(t, 1), :], x_all[:, ds(t, 1), :], mean[:, ds(t, 1), 0], rstd[:, ds(t, 1), 0],
                                  ALU.subtract, ALU.mult).then_inc(xn_ready, 1)
            dve.wait_ge(x_copied, seen(1))
            dve.wait_ge(xn_ready, seen(NT))
            dve.tensor_tensor(x_twice[:], x_twice[:], x_all[:], ALU.add).then_inc(sum_ready, 1)
            with dve.Fori(0, NT // 2, 1) as g:
                for b in range(2):
                    dve.wait_ge(xh_in_psum[b], seen(g + 1))
                    dve.tensor_copy(table[:, ds(2 * g + b, 1), :], ps_h[b][:, None, 0:D + 2 * HEADS]).then_inc(xh_ready[b], 1)
            for b in range(2):
                dve.wait_ge(xh_ready[b], seen(NT // 2))
            dve.tensor_copy(keep["a_node"][:], table[:, :, D:D + 2 * HEADS]).then_inc(ad_kept, 1)

        @block.tensor
        def _(pe):
            pe.wait_ge(ident_ready, seen(1))
            pe.wait_ge(w_ready, seen(KC))
            with pe.Fori(0, NT // 2, 1) as g:
                for b in range(2):
                    pe.wait_ge(xn_copied[b], seen(g + 1))
                    pe.wait_ge(xnT_ready[b], seen(g))
                    for kc in range(KC):
                        last = pe.transpose(ps_t[b][:, kc, :], xn_tile[:, b, kc * 128:(kc + 1) * 128],
                                            keep["ident"][0:P, 0:P])
                    last.then_inc(xnT_in_psum[b], 1)
                for b in range(2):
                    pe.wait_ge(xnT_ready[b], seen(g + 1))
                    pe.wait_ge(xh_ready[b], seen(g))
                    for kc in range(KC):
                        last = pe.matmul(ps_h[b][:, 0:D + 2 * HEADS], xnT[:, b, kc, :], w[:, kc, :],
                                         start=(kc == 0), stop=(kc == KC - 1))
                    last.then_inc(xh_in_psum[b], 1)

        @block.scalar
        def _(act):
            with act.Fori(0, NT // 2, 1) as g:
                for b in range(2):
                    act.wait_ge(xn_ready, seen(2 * g + b + 1))
                    act.wait_ge(xnT_in_psum[b], seen(g))
                    act.activation(xn_tile[:, b, :], x_all[:, ds(2 * g + b, 1), :], ACT.Copy).then_inc(xn_copied[b], 1)
                for b in range(2):
                    act.wait_ge(xnT_in_psum[b], seen(g + 1))
                    act.wait_ge(xh_in_psum[b], seen(g))
                    act.activation(xnT[:, b], ps_t[b][:], ACT.Copy).then_inc(xnT_ready[b], 1)




class Group:

    def __init__(self, i, j, k, layer, n_groups):
        self.i = i
        self.b = k % 2
        count = lambda k: layer * (n_groups // 2 + (k % 2 == 0) * (n_groups % 2)) + (k // 2) + j
        self.m = count(k)


def pipeline(eng, layer, n_groups, steps):
    depth = max(lag for lag, _ in steps)

    def turn(k, j):
        for lag, f in steps:
            g = k - lag
            if isinstance(j, int) and not 0 <= g < n_groups:
                continue
            f(Group(g + 2 * j, j, g, layer, n_groups))

    pairs = (n_groups - depth) // 2
    for k in range(depth):
        turn(k, 0)
    with eng.Fori(0, pairs, 1) as j:
        turn(depth, j)
        turn(depth + 1, j)
    for k in range(depth + 2 * pairs, n_groups + depth):
        turn(k, 0)


def mix(nc, io, dram, keep, NT):
    N = io["x"].shape[0]
    L, _, FF = io["L0_mix_W1"].shape
    NG = NT // 2
    T2 = 2 * P
    FC = FF // 128
    SCALE = float(DH) ** -0.25
    uses = (NG // 2 + NG % 2, NG // 2)
    E_LOCAL = dram["src"].shape[1]

    with ExitStack() as ctx:
        k = Kit(nc, ctx, "mix")
        X = k.sb("X", [P, NT, D])
        at_w1 = 4 * (NT * D - 4 * KC * FF - 2 * FC * T2)
        (big, w1, w2, hL), (w1_high, w1_rest, w2_high, w2_rest, uT_high, uT_rest, hT_rest) = k.share(
            [("big", [128, NT, D]), ("w1", [128, KC, FF]), ("w2", [128, FC, D]), ("hL", [128, 2, KC, T2])],
            [("w1_high", [128, KC, FF]), ("w1_rest", [128, KC, FF]), ("w2_high", [128, FC, D]), ("w2_rest", [128, FC, D]),
             ("uT_high", [128, 2, FC, T2]), (None, at_w1), ("uT_rest", [128, 2, FC, T2]), (None, 4 * (4 * KC * FF // 2 - 2 * FC * T2)),
             ("hT_rest", [128, 2, KC, T2])])
        kT_all = big[:].rearrange("p t d -> p (t d)")[:, 0:KC * N].rearrange("p (k n) -> p k n", k=KC)
        extra = big[0:P]
        wq, wk, wv, wo = (k.sb(n, [128, KC, D]) for n in ("wq", "wk", "wv", "wo"))
        ln = k.sb("ln", [128, 4, KC])
        bo, b2 = k.sb("bo", [128, 1, D]), k.sb("b2", [P, 1, D])
        b1 = k.sb("b1", [128, FC])
        stats = k.sb("stats", [P, NT, 6])
        mean, var = k.sb("mean", [P, NT, 1]), k.sb("var", [P, NT])
        rstd = k.sb("rstd", [P, NT, 1])
        rtmp = k.sb("rtmp", [P, 2, NT])
        xhat = k.sb("xhat", [P, 2, 2, D])
        hT = k.sb("hT", [128, 2, KC, T2])
        kexp = k.sb("kexp", [128, 2, KC, T2])
        kt = k.sb("kt", [P, 2, 2, D])
        vt = k.sb("vt", [P, 2, 2, D])
        kmaxs, ksums = k.sb("kmaxs", [128, KC, NG]), k.sb("ksums", [128, KC, NG])
        kmax, kbias = k.sb("kmax", [128, KC]), k.sb("kbias", [128, KC])
        ksum, krec = k.sb("ksum", [128, KC]), k.sb("krec", [128, KC])
        out_ready = k.sem("out_ready")
        passed_sp, passed_dve, passed_pool = k.sem("passed_sp"), k.sem("passed_dve"), k.sem("passed_pool")
        zeros = k.sb("zeros", [P, 128])
        same_head = k.sb("same_head", [128, 4, DH])
        ctxT = k.sb("ctxT", [128, KC, 128])
        wm = k.sb("wm", [128, KC, D])
        qmax = k.sb("qmax", [P, 2 * HEADS])
        qsum, qrec = k.sb("qsum", [P, 2 * HEADS]), k.sb("qrec", [P, 2 * HEADS])
        qs = kt
        qe = vt
        qT = kexp
        hT_high = k.sb("hT_high", [128, 2, KC, T2])
        u_raw = kexp
        ps = [k.ps(f"ps{i}", [128, 512]) for i in range(8)]

        def tok(bank):
            return bank[0:P, :].rearrange("p (t d) -> p t d", t=2)

        def feat(bank):
            return bank[:, 0:KC * T2].rearrange("p (k n) -> p k n", k=KC)

        pair = lambda name: [k.sem(f"{name}{b}") for b in range(2)]
        x_loaded = k.sem("x_loaded")
        wa_loaded, wb_loaded = k.sem("wa_loaded"), k.sem("wb_loaded")
        dve_done, stats0_done = k.sem("dve_done"), k.sem("stats0_done")
        res1_done, res2_done = k.sem("res1_done"), k.sem("res2_done")
        q_max_taken, q_summed, q_inverted = pair("q_max_taken"), pair("q_summed"), pair("q_inverted")
        const_ready = k.sem("const_ready")
        xhat_ready, xT_in_psum, hT_ready, h_stored = pair("xhat_ready"), pair("xT_in_psum"), pair("hT_ready"), pair("h_stored")
        k_in_psum, kmax_taken, k_copied = pair("k_in_psum"), pair("kmax_taken"), pair("k_copied")
        kbias_ready = k.sem("kbias_ready")
        h_loaded, kexp_ready, kx_in_psum, k_ready = pair("h_loaded"), pair("kexp_ready"), pair("kx_in_psum"), pair("k_ready")
        v_in_psum, v_ready, ctx_done = pair("v_in_psum"), pair("v_ready"), pair("ctx_done")
        ctx_ready, wm_in_psum, wm_ready = k.sem("ctx_ready"), k.sem("wm_in_psum"), k.sem("wm_ready")
        h_loaded2, q_in_psum, q_shifted, q_exped, q_ready = (pair(n) for n in ("h_loaded2_", "q_in_psum", "q_shifted", "q_exped", "q_ready"))
        qT_in_psum, qT_ready, attn_in_psum, attn_taken = pair("qT_in_psum"), pair("qT_ready"), pair("attn_in_psum"), pair("attn_taken")
        xhat2_ready, x1T_in_psum, h2T_ready = pair("xhat2_ready"), pair("x1T_in_psum"), pair("h2T_ready")
        up_in_psum, gelu_done = ([k.sem(f"{n}{f}") for f in range(FC // 2)] for n in ("up_in_psum", "gelu_done"))
        down_in_psum, down_taken = pair("down_in_psum"), pair("down_taken")
        bias_added = k.sem("bias_added")
        w_high_done, w_split = k.sem("w_high_done"), k.sem("w_split")
        h_high_done, h_split = pair("h_high_done"), pair("h_split")
        u_high_done, u_split = ([k.sem(f"{n}{f}") for f in range(FC // 2)] for n in ("u_high_done", "u_split"))
        mix_stored = k.sem("mix_stored")
        ie = k.sb("src_idx", [P, E_LOCAL], U32)
        GC = 8
        GB = 3
        idx_tile = k.sb("idx_tile", [P, GB, GC], U32)
        got = k.sb("got", [P, GB, GC, D + HEADS])
        got_a = k.sb("got_a", [P, GB, GC, HEADS])
        got_a_ready = k.sem("got_a_ready")
        src_loaded, idx_copied = k.sem("src_loaded"), [k.sem(f"idx_copied{b}") for b in range(GB)]
        gathered, got_stored = ([k.gather_sem(f"{n}{b}") for b in range(GB)] for n in ("gathered", "got_stored"))
        got_a_stored = k.gather_sem("got_a_stored")
        block = k.start()

        @block.sync
        def _(sp):
            sp.dma_start(ie[:], dram["src"]).then_inc(src_loaded, 16)
            sp.dma_start(X[:], dram["res"][0].rearrange("(t p) d -> p t d", p=P)).then_inc(x_loaded, 16)
            def load_first(l):
                for tile, name in ((wk, "Wk"), (wv, "Wv"), (wq, "Wq"), (wo, "Wo")):
                    sp.dma_start(tile[:], io[f"L0_mix_{name}"][ds(l, 1)].rearrange("l (k p) n -> p (l k) n", p=128)).then_inc(wa_loaded, 16)
                for i, name in enumerate(("ln1_g", "ln1_b")):
                    sp.dma_start(ln[:, i, :], io[f"L0_mix_{name}"][ds(l, 1)].rearrange("l (k p) -> p (l k)", p=128),
                                 allow_slow_non_contiguous=True).then_inc(wa_loaded, 16)
                sp.dma_start(bo[:], io["L0_mix_bo"][ds(l, 1)][None].broadcast_to([128, 1, D])).then_inc(wa_loaded, 16)

            def load_feed(l):
                for i, name in enumerate(("ln2_g", "ln2_b")):
                    sp.dma_start(ln[:, 2 + i, :], io[f"L0_mix_{name}"][ds(l, 1)].rearrange("l (k p) -> p (l k)", p=128),
                                 allow_slow_non_contiguous=True).then_inc(wb_loaded, 16)
                sp.dma_start(w1[:], io["L0_mix_W1"][ds(l, 1)].rearrange("l (k p) n -> p (l k) n", p=128)).then_inc(wb_loaded, 16)
                sp.dma_start(w2[:], io["L0_mix_W2"][ds(l, 1)].rearrange("l (k p) n -> p (l k) n", p=128)).then_inc(wb_loaded, 16)
                sp.dma_start(b2[:], io["L0_mix_b2"][ds(l, 1)][None].broadcast_to([P, 1, D])).then_inc(wb_loaded, 16)
                sp.dma_start(b1[:], io["L0_mix_b1"][ds(l, 1)].rearrange("l (k p) -> p (l k)", p=128),
                             allow_slow_non_contiguous=True).then_inc(wb_loaded, 16)

            def layer(l):
                wait_apart(sp, res2_done, seen(l * (NG * 2)), passed_sp)
                load_feed(l)

                def store_h(g):
                    wait_apart(sp, hT_ready[g.b], seen(g.m + 1), passed_sp)
                    sp.dma_start(dram["hT"][ds(g.i, 1)].rearrange("g p k n -> p (g k) n"), hT[:, g.b]).then_inc(h_stored[g.b], 16)

                pipeline(sp, l, NG, [(0, store_h)])
                for b in range(2):
                    wait_apart(sp, h_stored[b], seen((l + 1) * (16 * uses[b])), passed_sp)

                def load_h(g):
                    wait_apart(sp, v_in_psum[g.b], seen(g.m), passed_sp)
                    wait_apart(sp, q_in_psum[g.b], seen(l * uses[g.b]), passed_sp)
                    sp.dma_start(hL[:, g.b], dram["hT"][ds(g.i, 1)].rearrange("g p k n -> p (g k) n")).then_inc(h_loaded[g.b], 16)

                pipeline(sp, l, NG, [(0, load_h)])

                def load_h2(g):
                    wait_apart(sp, q_in_psum[g.b], seen(g.m), passed_sp)
                    wait_apart(sp, v_in_psum[g.b], seen((l + 1) * uses[g.b]), passed_sp)
                    sp.dma_start(hL[:, g.b], dram["hT"][ds(g.i, 1)].rearrange("g p k n -> p (g k) n")).then_inc(h_loaded2[g.b], 16)

                pipeline(sp, l, NG, [(0, load_h2)])

            load_first(0)
            with sp.Fori(0, L - 1, 1) as l:
                layer(l)
                for b in range(2):
                    wait_apart(sp, q_in_psum[b], seen((l + 1) * uses[b]), passed_sp)
                wait_apart(sp, wm_ready, seen(l + 1), passed_sp)
                load_first(l + 1)
            layer(L - 1)
            sp.wait_ge(kbias_ready, seen(L))
            for b in range(2):
                sp.wait_ge(kexp_ready[b], seen(L * uses[b]))
                sp.wait_ge(down_in_psum[b], seen(L * uses[b]))
            sp.dma_start(extra, dram["x_plus_xn"].rearrange("(t p) d -> p t d", p=P)).then_inc(x_loaded, 16)
            sp.wait_ge(out_ready, seen(1))
            sp.dma_start(dram["mix_out"].rearrange("(t p) d -> p t d", p=P), X[:]).then_inc(mix_stored, 16)
            sp.wait_ge(mix_stored, seen(16))

        @block.gpsimd
        def _(pool):
            pool.memset(zeros[:], 0.0).then_inc(const_ready, 1)
            pool.memset(same_head[:], 1.0).then_inc(const_ready, 1)
            pool.wait_ge(const_ready, seen(2))
            pool.affine_select(out=same_head[:], in_=same_head[:], compare_op=ALU.is_ge, fill=0.0,
                               base=0, pattern=[[-DH, 4], [0, DH]], channel_multiplier=1).then_inc(const_ready, 1)
            pool.wait_ge(const_ready, seen(3))
            pool.affine_select(out=same_head[:], in_=same_head[:], compare_op=ALU.is_ge, fill=0.0,
                               base=DH - 1, pattern=[[DH, 4], [0, DH]], channel_multiplier=-1).then_inc(const_ready, 1)
            edge_rows = dram["edge_rows"][0:P * E_LOCAL, :].rearrange("(p c) w -> p c w", p=P)
            pool.wait_ge(src_loaded, seen(16))

            fills = E_LOCAL // GC

            def gather(r, b):
                if not isinstance(r, int) or r > 0:
                    pool.wait_ge(gathered[b], r * (16 * GC))
                    pool.wait_ge(got_stored[b], r * 16)
                pool.tensor_copy(idx_tile[:, b, :], ie[:, ds((GB * r + b) * GC, GC)]).then_inc(idx_copied[b], 1)
                wait_apart(pool, idx_copied[b], seen(r + 1), passed_pool)
                for c in range(GC):
                    pool.indirect_dma_start(got[:, b, c, :], None, dram["node_rows"],
                                            bass.IndirectOffsetOnAxis(ap=idx_tile[:, b, c:c + 1], axis=0)).then_inc(gathered[b], 16)

            def store(r, b):
                if not isinstance(r, int) or r > 0:
                    pool.wait_ge(got_a_stored, r * 16)
                pool.wait_ge(gathered[b], (r + 1) * (16 * GC))
                pool.dma_start(edge_rows[:, ds((GB * r + b) * GC, GC), :], got[:, b]).then_inc(got_stored[b], 16)
                pool.tensor_copy(got_a[:, b], got[:, b, :, D:]).then_inc(got_a_ready, 1)

            def store_a(r, n):
                wait_apart(pool, got_a_ready, seen(GB * r + n), passed_pool)
                pool.dma_start(dram["a_edge"][:, ds(r * (GB * GC * HEADS), n * GC * HEADS)],
                               got_a[:, 0:n].rearrange("p b c h -> p (b c h)")).then_inc(got_a_stored, 16)

            gather(0, 0)
            gather(0, 1)
            store(0, 0)
            gather(0, 2)
            store(0, 1)
            with pool.Fori(1, fills // GB, 1) as r:
                gather(r, 0)
                store(r - 1, 2)
                store_a(r - 1, GB)
                gather(r, 1)
                store(r, 0)
                gather(r, 2)
                store(r, 1)
            turns, rest = fills // GB, fills % GB
            if rest:
                gather(turns, 0)
            store(turns - 1, 2)
            store_a(turns - 1, GB)
            for b in range(rest):
                if b:
                    gather(turns, b)
                store(turns, b)
            if rest:
                store_a(turns, rest)
            for b in range(GB):
                pool.wait_ge(got_stored[b], (turns + (b < rest)) * 16)
            pool.wait_ge(got_a_stored, (turns + (rest > 0)) * 16)

        def layer_norm_stats(dve, chain, g):
            for t in range(2):
                chain.step(dve.bn_stats(stats[:, ds(2 * g.i + t, 1), :], X[:, ds(2 * g.i + t, 1), :]))

        @block.vector
        def _(dve):
            dve.wait_ge(x_loaded, seen(16))
            stats0 = Chain(dve, stats0_done)

            def first_stats(g):
                stats0.at(g.i * 2)
                layer_norm_stats(dve, stats0, g)

            pipeline(dve, 0, NG, [(0, first_stats)])
            dve.wait_ge(stats0_done, seen(2 * NG))
            chain = Chain(dve, dve_done)
            per_layer = 2 * (AGGREGATE_STEPS + RSQRT_STEPS) + 6
            with dve.Fori(0, L, 1) as l:
                chain.at(dve.snap(l * per_layer))
                dve.wait_ge(res2_done, seen(l * (2 * NG)))
                aggregate_stats(dve, chain, mean[:, :, 0], var[:], stats, D)
                rsqrt_eps(dve, chain, rstd[:, :, 0], var[:], (rtmp[:, 0, :], rtmp[:, 1, :]))

                def norm(ready, done):
                    def f(g):
                        dve.wait_ge(done[g.b], seen(g.m))
                        for t in range(2):
                            last = dve.tensor_scalar(xhat[:, g.b, t:t + 1, :], X[:, ds(2 * g.i + t, 1), :], mean[:, ds(2 * g.i + t, 1), 0],
                                                     rstd[:, ds(2 * g.i + t, 1), 0], ALU.subtract, ALU.mult)
                        last.then_inc(ready[g.b], 1)
                    return f

                def key_max(g):
                    dve.wait_ge(k_copied[g.b], seen(g.m + 1))
                    dve.tensor_reduce(kmaxs[:, :, ds(g.i, 1)], kT_all[:, :, ds(g.i * T2, T2)], AX.X, ALU.max).then_inc(kmax_taken[g.b], 1)

                for b in range(2):
                    dve.wait_ge(x1T_in_psum[b], seen(l * uses[b]))
                pipeline(dve, l, NG, [(0, norm(xhat_ready, xT_in_psum)), (2, key_max)])
                for b in range(2):
                    dve.wait_ge(kmax_taken[b], seen((l + 1) * uses[b]))
                chain.link(dve.tensor_reduce(kmax[:], kmaxs[:], AX.X, ALU.max))
                dve.tensor_scalar(kbias[:], kmax[:], -SCALE, None, ALU.mult).then_inc(kbias_ready, 1)

                def take_k(g):
                    dve.wait_ge(kx_in_psum[g.b], seen(g.m + 1))
                    dve.wait_ge(ctx_done[g.b], seen(g.m))
                    dve.tensor_copy(kt[:, g.b], tok(ps[g.b])).then_inc(k_ready[g.b], 1)

                for b in range(2):
                    wait_apart(dve, q_exped[b], seen(l * uses[b]), passed_dve)
                pipeline(dve, l, NG, [(0, take_k)])
                for b in range(2):
                    dve.wait_ge(ctx_done[b], seen((l + 1) * uses[b]))
                for kc in range(KC):
                    last = dve.tensor_tensor(ctxT[:, kc, :], ps[4][:, kc * 128:(kc + 1) * 128],
                                             same_head[:].rearrange("p a b -> p (a b)"), ALU.mult)
                last.then_inc(ctx_ready, 1)
                chain.link(dve.tensor_reduce(ksum[:], ksums[:], AX.X, ALU.add))
                chain.link(dve.reciprocal(krec[:], ksum[:]))
                dve.wait_ge(wm_in_psum, seen(l + 1))
                for kc in range(KC):
                    chain.step(dve.tensor_scalar(wm[:, kc, :], ps[5][:, kc * D:(kc + 1) * D], krec[:, kc:kc + 1], None, ALU.mult))
                dve.wait_ge(wa_loaded, seen((l + 1) * (16 * 7)))
                chain.link(dve.tensor_scalar(bo[:], bo[:], 1.0 / HEADS, None, ALU.mult))
                dve.tensor_tensor(wm[:], wm[:], bo[:].broadcast_to([128, KC, D]), ALU.add).then_inc(wm_ready, 1)

                def per_head(ap):
                    return ap.rearrange("p t (h e) -> p (t h) e", e=DH)

                def largest(g):
                    dve.wait_ge(q_in_psum[g.b], seen(g.m + 1))
                    dve.tensor_reduce(qmax[:], per_head(tok(ps[g.b])), AX.X, ALU.max).then_inc(q_max_taken[g.b], 1)

                def shift(g):
                    dve.wait_ge(q_max_taken[g.b], seen(g.m + 1))
                    dve.wait_ge(q_exped[g.b], seen(g.m))
                    dve.tensor_tensor(per_head(qs[:, g.b]), per_head(tok(ps[g.b])), qmax[:, :, None].broadcast_to([P, 2 * HEADS, DH]),
                                      ALU.subtract).then_inc(q_shifted[g.b], 1)

                def total(g):
                    dve.wait_ge(q_exped[g.b], seen(g.m + 1))
                    dve.tensor_reduce(qsum[:], per_head(qe[:, g.b]), AX.X, ALU.add).then_inc(q_summed[g.b], 1)

                def invert(g):
                    dve.wait_ge(q_summed[g.b], seen(g.m + 1))
                    dve.reciprocal(qrec[:], qsum[:]).then_inc(q_inverted[g.b], 1)

                def normalise(g):
                    dve.wait_ge(q_inverted[g.b], seen(g.m + 1))
                    dve.tensor_tensor(per_head(qe[:, g.b]), per_head(qe[:, g.b]), qrec[:, :, None].broadcast_to([P, 2 * HEADS, DH]),
                                      ALU.mult).then_inc(q_ready[g.b], 1)

                def residual(banks, ready, taken, bias, sem):
                    def f(g):
                        c = Chain(dve, sem)
                        c.at(0)
                        rows = X[:, ds(2 * g.i, 2), :]
                        dve.wait_ge(ready[g.b], seen(g.m + 1))
                        dve.tensor_tensor(rows, tok(ps[banks + g.b]), rows, ALU.add).then_inc(taken[g.b], 1)
                        if bias is None:
                            wait_apart(dve, taken[g.b], seen(g.m + 1), passed_dve)
                        else:
                            dve.wait_ge(taken[g.b], seen(g.m + 1))
                            dve.tensor_tensor(rows, rows, bias[:].broadcast_to([P, 2, D]), ALU.add).then_inc(bias_added, 1)
                            wait_apart(dve, bias_added, seen(l * NG + g.i + 1), passed_dve)
                        layer_norm_stats(dve, c, g)
                    return f

                pipeline(dve, l, NG, [(1, total), (0, largest), (1, invert), (0, shift), (1, normalise), (2, residual(6, attn_in_psum, attn_taken, None, res1_done))])

                dve.wait_ge(res1_done, seen((l + 1) * (2 * NG)))
                aggregate_stats(dve, chain, mean[:, :, 0], var[:], stats, D)
                rsqrt_eps(dve, chain, rstd[:, :, 0], var[:], (rtmp[:, 0, :], rtmp[:, 1, :]))
                for b in range(2):
                    dve.wait_ge(xT_in_psum[b], seen((l + 1) * uses[b]))
                dve.wait_ge(wb_loaded, seen((l + 1) * (16 * 6)))
                split_high(dve, w1_high[:], w1[:]).then_inc(w_high_done, 1)
                split_high(dve, w2_high[:], w2[:]).then_inc(w_high_done, 1)
                for i, (rest, whole, high) in enumerate(((w1_rest, w1, w1_high), (w2_rest, w2, w2_high))):
                    dve.wait_ge(w_high_done, seen(2 * l + i + 1))
                    split_rest(dve, rest[:], whole[:], high[:]).then_inc(w_split, 1)
                dve.wait_ge(w_split, seen(2 * l + 2))

                def split_h(g):
                    dve.wait_ge(h2T_ready[g.b], seen(g.m + 1))
                    split_high(dve, hT_high[:, g.b], hT[:, g.b]).then_inc(h_high_done[g.b], 1)
                    dve.wait_ge(h_high_done[g.b], seen(g.m + 1))
                    split_rest(dve, hT_rest[:, g.b], hT[:, g.b], hT_high[:, g.b]).then_inc(h_split[g.b], 1)

                def split_u(g):
                    n = dve.snap(l * NG + g.i)

                    def high(f):
                        dve.wait_ge(gelu_done[f], seen(n + 1))
                        split_high(dve, uT_high[:, g.b, 2 * f:2 * f + 2], u_raw[:, f % 2]).then_inc(u_high_done[f], 1)

                    def rest(f):
                        dve.wait_ge(u_high_done[f], seen(n + 1))
                        pair_f = slice(2 * f, 2 * f + 2)
                        split_rest(dve, uT_rest[:, g.b, pair_f], u_raw[:, f % 2], uT_high[:, g.b, pair_f]).then_inc(u_split[f], 1)

                    dve.wait_ge(down_in_psum[g.b], seen(g.m))
                    high(0)
                    for f in range(1, FC // 2):
                        high(f)
                        rest(f - 1)
                    rest(FC // 2 - 1)

                pipeline(dve, l, NG, [(0, norm(xhat2_ready, x1T_in_psum)), (1, split_h), (4, residual(6, down_in_psum, down_taken, b2, res2_done)), (2, split_u)])
            dve.wait_ge(x_loaded, seen(32))
            dve.wait_ge(res2_done, seen(L * NG * 2))
            dve.tensor_tensor(X[:], X[:], extra, ALU.add).then_inc(out_ready, 1)

        @block.tensor
        def _(pe):
            ident = keep["ident"]
            pe.wait_ge(const_ready, seen(4))
            with pe.Fori(0, L, 1) as l:
                def all_of(sems, layers):
                    for b in range(2):
                        pe.wait_ge(sems[b], seen(layers * uses[b]))

                def to_features(bank, src):
                    for kc in range(KC):
                        for t in range(2):
                            last = pe.transpose(feat(bank)[:, kc, t * P:(t + 1) * P], src[:, t, kc * 128:(kc + 1) * 128], ident[0:P, 0:P])
                    return last

                def by_node(bank, lhs, w):
                    for t in range(2):
                        for kc in range(KC):
                            last = pe.matmul(tok(bank)[:, t, :], lhs[:, kc, t * P:(t + 1) * P], w[:, kc, :], start=(kc == 0), stop=(kc == KC - 1))
                    return last

                all_of(h2T_ready, l)
                for f in range(FC // 2):
                    pe.wait_ge(gelu_done[f], seen(l * NG))
                pe.wait_ge(wa_loaded, seen((l + 1) * (16 * 7)))

                def x_transposes(g):
                    pe.wait_ge(xhat_ready[g.b], seen(g.m + 1))
                    pe.wait_ge(hT_ready[g.b], seen(g.m))
                    to_features(ps[g.b], xhat[:, g.b]).then_inc(xT_in_psum[g.b], 1)

                def keys(g):
                    pe.wait_ge(hT_ready[g.b], seen(g.m + 1))
                    pe.wait_ge(k_copied[g.b], seen(g.m))
                    for dc in range(KC):
                        for kc in range(KC):
                            last = pe.matmul(feat(ps[2 + g.b])[:, dc, :], wk[:, kc, dc * 128:(dc + 1) * 128], hT[:, g.b, kc, :],
                                             start=(kc == 0), stop=(kc == KC - 1))
                    last.then_inc(k_in_psum[g.b], 1)

                pipeline(pe, l, NG, [(0, x_transposes), (1, keys)])

                all_of(hT_ready, l + 1)
                all_of(k_copied, l + 1)
                for kc in range(KC):
                    pe.matmul(ps[4][:, kc * 128:(kc + 1) * 128], zeros[:], zeros[:], start=(kc == 0), stop=False, skip_group_check=True)

                def kv(g):
                    pe.wait_ge(kexp_ready[g.b], seen(g.m + 1))
                    pe.wait_ge(k_ready[g.b], seen(g.m))
                    for t in range(2):
                        for kc in range(KC):
                            last = pe.transpose(tok(ps[g.b])[:, t, kc * 128:(kc + 1) * 128], kexp[:, g.b, kc, t * P:(t + 1) * P], ident[:])
                    last.then_inc(kx_in_psum[g.b], 1)
                    pe.wait_ge(h_loaded[g.b], seen((g.m + 1) * 16))
                    pe.wait_ge(v_ready[g.b], seen(g.m))
                    by_node(ps[2 + g.b], hL[:, g.b], wv).then_inc(v_in_psum[g.b], 1)

                def context(g):
                    pe.wait_ge(k_ready[g.b], seen(g.m + 1))
                    pe.wait_ge(v_ready[g.b], seen(g.m + 1))
                    for t in range(2):
                        for kc in range(KC):
                            half = slice(kc * 128, (kc + 1) * 128)
                            last = pe.matmul(ps[4][:, half], vt[:, g.b, t, half], kt[:, g.b, t, half], start=False, stop=False, skip_group_check=True)
                    last.then_inc(ctx_done[g.b], 1)

                pipeline(pe, l, NG, [(0, kv), (1, context)])
                pe.wait_ge(ctx_ready, seen(l + 1))
                for kc in range(KC):
                    last = pe.matmul(ps[5][:, kc * D:(kc + 1) * D], ctxT[:, kc, :], wo[:, kc, :], start=True, stop=True)
                last.then_inc(wm_in_psum, 1)

                all_of(k_ready, l + 1)
                all_of(v_ready, l + 1)
                all_of(down_taken, l)

                def q_transposes(g):
                    pe.wait_ge(q_ready[g.b], seen(g.m + 1))
                    pe.wait_ge(qT_ready[g.b], seen(g.m))
                    to_features(ps[2 + g.b], qe[:, g.b]).then_inc(qT_in_psum[g.b], 1)

                def queries(g):
                    pe.wait_ge(h_loaded2[g.b], seen((g.m + 1) * 16))
                    pe.wait_ge(q_shifted[g.b], seen(g.m))
                    by_node(ps[g.b], hL[:, g.b], wq).then_inc(q_in_psum[g.b], 1)

                def attend(g):
                    pe.wait_ge(qT_ready[g.b], seen(g.m + 1))
                    pe.wait_ge(attn_taken[g.b], seen(g.m))
                    pe.wait_ge(wm_ready, seen(l + 1))
                    by_node(ps[6 + g.b], qT[:, g.b], wm).then_inc(attn_in_psum[g.b], 1)

                pipeline(pe, l, NG, [(2, q_transposes), (0, queries), (2, attend)])

                all_of(q_shifted, l + 1)
                all_of(qT_ready, l + 1)
                all_of(attn_taken, l + 1)
                pe.wait_ge(wb_loaded, seen((l + 1) * (16 * 6)))

                def x1_transposes(g):
                    pe.wait_ge(xhat2_ready[g.b], seen(g.m + 1))
                    pe.wait_ge(h2T_ready[g.b], seen(g.m))
                    to_features(ps[g.b], xhat[:, g.b]).then_inc(x1T_in_psum[g.b], 1)

                def down(g):
                    pe.wait_ge(down_taken[g.b], seen(g.m))
                    n = pe.snap(l * NG + g.i)
                    for f in range(FC // 2):
                        pe.wait_ge(u_split[f], seen(n + 1))
                    for t in range(2):
                        for f in range(FC):
                            lhs = [u[:, g.b, f, t * P:(t + 1) * P] for u in (uT_high, uT_rest)]
                            last = product_of_parts(pe, tok(ps[6 + g.b])[:, t, :], lhs, (w2_high[:, f, :], w2_rest[:, f, :]), f == 0, f == FC - 1)
                    last.then_inc(down_in_psum[g.b], 1)

                def up(g):
                    pe.wait_ge(h_split[g.b], seen(g.m + 1))
                    n = pe.snap(l * NG + g.i)
                    for f in range(FC):
                        if f % 2 == 0:
                            pe.wait_ge(gelu_done[f // 2], seen(n))
                        for kc in range(KC):
                            lhs = [w[:, kc, f * 128:(f + 1) * 128] for w in (w1_high, w1_rest)]
                            last = product_of_parts(pe, feat(ps[2 + f // 2])[:, f % 2, :], lhs, (hT_high[:, g.b, kc, :], hT_rest[:, g.b, kc, :]),
                                                    kc == 0, kc == KC - 1)
                        if f % 2:
                            last.then_inc(up_in_psum[f // 2], 1)

                pe.wait_ge(w_split, seen((l + 1) * 2))
                pipeline(pe, l, NG, [(0, x1_transposes), (1, up), (2, down)])

        @block.scalar
        def _(act):
            with act.Fori(0, L, 1) as l:
                def all_of(sems, layers):
                    for b in range(2):
                        act.wait_ge(sems[b], seen(layers * uses[b]))

                act.wait_ge(wa_loaded, seen((l + 1) * (16 * 7)))
                for f in range(FC // 2):
                    act.wait_ge(up_in_psum[f], seen(l * NG))
                all_of(down_in_psum, l)

                def take_hT(which, in_psum, done, ready):
                    def f(g):
                        act.wait_ge(in_psum[g.b], seen(g.m + 1))
                        done(g)
                        for kc in range(KC):
                            last = act.activation(hT[:, g.b, kc, :], feat(ps[g.b])[:, kc, :], ACT.Identity,
                                                  bias=ln[:, which + 1, kc:kc + 1], scale=ln[:, which, kc:kc + 1])
                        last.then_inc(ready[g.b], 1)
                    return f

                def hT_stored(g):
                    act.wait_ge(k_in_psum[g.b], seen(g.m))
                    act.wait_ge(h_stored[g.b], seen(g.m * 16))

                def copy_k(g):
                    act.wait_ge(k_in_psum[g.b], seen(g.m + 1))
                    act.activation(kT_all[:, :, ds(g.i * T2, T2)], feat(ps[2 + g.b]), ACT.Copy).then_inc(k_copied[g.b], 1)

                pipeline(act, l, NG, [(0, take_hT(0, xT_in_psum, hT_stored, hT_ready)), (1, copy_k)])

                all_of(attn_in_psum, l)
                all_of(qT_in_psum, l)
                all_of(k_copied, l + 1)
                act.wait_ge(kbias_ready, seen(l + 1))

                def exp_k(g):
                    act.wait_ge(kx_in_psum[g.b], seen(g.m))
                    for kc in range(KC):
                        last = act.activation(kexp[:, g.b, kc, None, :], kT_all[:, kc:kc + 1, ds(g.i * T2, T2)], ACT.Exp, bias=kbias[:, kc:kc + 1], scale=SCALE,
                                              accum_out=ksums[:, kc, ds(g.i, 1)])
                    last.then_inc(kexp_ready[g.b], 1)

                def take_v(g):
                    act.wait_ge(v_in_psum[g.b], seen(g.m + 1))
                    act.wait_ge(ctx_done[g.b], seen(g.m))
                    act.activation(vt[:, g.b], tok(ps[2 + g.b]), ACT.Copy).then_inc(v_ready[g.b], 1)

                pipeline(act, l, NG, [(0, exp_k), (1, take_v)])

                all_of(ctx_done, l + 1)
                all_of(kx_in_psum, l + 1)

                def take_qT(g):
                    act.wait_ge(qT_in_psum[g.b], seen(g.m + 1))
                    act.wait_ge(attn_in_psum[g.b], seen(g.m))
                    act.activation(qT[:, g.b], feat(ps[2 + g.b]), ACT.Copy).then_inc(qT_ready[g.b], 1)

                def exp_q(g):
                    act.wait_ge(q_shifted[g.b], seen(g.m + 1))
                    act.wait_ge(qT_in_psum[g.b], seen(g.m))
                    act.activation(qe[:, g.b], qs[:, g.b], ACT.Exp, scale=SCALE).then_inc(q_exped[g.b], 1)

                pipeline(act, l, NG, [(2, take_qT), (0, exp_q)])

                all_of(k_in_psum, l + 1)
                for b in range(2):
                    act.wait_ge(h_stored[b], seen((l + 1) * (16 * uses[b])))
                act.wait_ge(wb_loaded, seen((l + 1) * (16 * 6)))
                all_of(down_in_psum, l)

                def h2T_used(g):
                    pass

                def gelu(g):
                    n = act.snap(l * NG + g.i)
                    for f in range(FC // 2):
                        act.wait_ge(up_in_psum[f], seen(n + 1))
                        act.wait_ge(u_split[(f + 2) % (FC // 2)], seen(n + (f >= 2)))
                        for h in range(2):
                            last = act.activation(u_raw[:, f % 2, h, :], feat(ps[2 + f])[:, h, :], ACT.Gelu, bias=b1[:, 2 * f + h:2 * f + h + 1])
                        last.then_inc(gelu_done[f], 1)

                pipeline(act, l, NG, [(0, take_hT(2, x1T_in_psum, h2T_used, h2T_ready)), (1, gelu)])


def segments(nc, io, dram, keep, NT, plan_steps):
    N = io["x"].shape[0]
    E = io["src"].shape[0]
    EL = E // P
    CH = 500
    NC = E // CH
    SP_ = 110
    SC = plan_steps // SP_
    with ExitStack() as ctx:
        k = Kit(nc, ctx, "seg")
        AE = k.sb("AE", [P, EL, HEADS])
        dst = k.sb("dst", [P, EL], I32)
        pen = k.sb("pen", [P, EL])
        endT, carryT = k.sb("endT", [HEADS, P]), k.sb("carryT", [HEADS, P])
        firsts, lasts = k.sb("firsts", [HEADS, P], I32), k.sb("lasts", [HEADS, P], I32)
        joins, whole, pen8 = k.sb("joins", [HEADS, P]), k.sb("whole", [HEADS, P]), k.sb("pen8", [HEADS, P])
        start_row = k.sb("start_row", [1, NC], I32)
        starts = k.sb("starts", [P, NC], I32)
        junk = k.sb("junk", [P, CH])
        node = k.sb("node", [P, NT])
        count1, count2 = k.sb("count1", [P, NT]), k.sb("count2", [P, NT])
        chunk_f, chunk_i = k.sb("chunk_f", [P, NT]), k.sb("chunk_i", [P, NT], U32)
        rows = k.sb("rows", [P, NT, CH], I32)
        r0, r1 = k.sb("r0", [P, NT]), k.sb("r1", [P, NT])
        end_f = k.sb("end_f", [P, 1])
        last_f, last_i = k.sb("last_f", [P, NT]), k.sb("last_i", [P, NT], U32)
        part_f, part_i = k.sb("part_f", [P, NT]), k.sb("part_i", [P, NT], U32)
        bounds = k.sb("bounds", [P, P - 1])
        m_scan, m_carry = k.sb("m_scan", [P, NT, HEADS]), k.sb("m_carry", [P, NT, HEADS])
        spans, empty = k.sb("spans", [P, NT]), k.sb("empty", [P, NT])
        pair_v = k.sb("pair_v", [P, NT, 2 * HEADS])
        blk = k.sb("blk", [1, NT + 1])
        blk_i = k.sb("blk_i", [1, NT], I32)
        blk_row = k.sb("blk_row", [1, 3, NT])
        blk_all = k.sb("blk_all", [SP_, 3 * NT])
        step = k.sb("step", [SP_, SC])
        hit = k.sb("hit", [SP_, SC, NT])
        st_b, st_e, st_f = k.sb("st_b", [SP_, SC]), k.sb("st_e", [SP_, SC]), k.sb("st_f", [SP_, SC])
        plan = k.sb("plan", [SP_, 2, SC], I32)
        zero_row = k.sb("zero_row", [1, NT])
        n = {name: k.sem(name) for name in (
            "edges_loaded", "ends_loaded", "starts_loaded", "starts_spread", "iotas_ready", "done", "scanned", "scan_stored", "ends_ready",
            "carry_ready", "carry_stored", "chunks_ready", "rowptr_ready", "rowptr_stored", "rowptr_loaded",
            "last_ready", "blk_ready", "blk_spread", "plan_ready", "plan_stored", "plan_loaded")}
        for name in ("rows_gathered", "m_gathered"):
            n[name] = k.gather_sem(name)
        block = k.start()

        @block.sync
        def _(sp):
            sp.dma_start(start_row[:], io["dst"].rearrange("(a c e) -> a c e", a=1, e=CH)[:, :, 0],
                         allow_slow_non_contiguous=True).then_inc(n["starts_loaded"], 16)
            sp.dma_start(dst[:], io["dst"].rearrange("(p c) -> p c", p=P)).then_inc(n["edges_loaded"], 16)
            sp.dma_start(AE[:], dram["a_edge"].rearrange("p (c h) -> p c h", h=HEADS)).then_inc(n["edges_loaded"], 16)
            for tile, c in ((firsts, 0), (lasts, EL - 1)):
                sp.dma_start(tile[:], io["dst"].rearrange("(a p c) -> a p c", a=1, p=P)[:, :, c].broadcast_to([HEADS, P]),
                             allow_slow_non_contiguous=True).then_inc(n["ends_loaded"], 16)
            sp.wait_ge(n["rowptr_ready"], seen(1))
            sp.dma_start(dram["rowptr"][0:N].rearrange("(t p) -> p t", p=P), r0[:], allow_slow_non_contiguous=True).then_inc(n["rowptr_stored"], 16)
            sp.dma_start(dram["rowptr"][N:N + 1].rearrange("(a b) -> a b", a=1), end_f[0:1, :]).then_inc(n["rowptr_stored"], 16)
            sp.wait_ge(n["rowptr_stored"], seen(32))
            sp.dma_start(r1[:], dram["rowptr"][1:N + 1].rearrange("(t p) -> p t", p=P), allow_slow_non_contiguous=True).then_inc(n["rowptr_loaded"], 16)
            sp.dma_start(blk[:, 0:NT], dram["rowptr"][0:N].rearrange("(a t p) -> a t p", a=1, p=P)[:, :, 0],
                         allow_slow_non_contiguous=True).then_inc(n["rowptr_loaded"], 16)
            sp.dma_start(blk[:, NT:NT + 1], dram["rowptr"][N:N + 1].rearrange("(a b) -> a b", a=1)).then_inc(n["rowptr_loaded"], 16)
            sp.wait_ge(n["scanned"], seen(HEADS))
            sp.dma_start(dram["scan"].rearrange("(p c) h -> p c h", p=P), AE[:]).then_inc(n["scan_stored"], 16)
            sp.wait_ge(n["scan_stored"], seen(16))
            sp.dma_start(endT[:], dram["scan"].rearrange("(p c) h -> h p c", p=P)[:, :, EL - 1],
                         allow_slow_non_contiguous=True).then_inc(n["ends_ready"], 16)
            sp.wait_ge(n["carry_ready"], seen(1))
            sp.dma_start(dram["carry"].rearrange("p h -> h p"), carryT[:], allow_slow_non_contiguous=True).then_inc(n["carry_stored"], 16)
            sp.wait_ge(n["plan_ready"], seen(2))
            sp.dma_start(dram["plan"].rearrange("w (p s) -> p w s", s=SC), plan[:]).then_inc(n["plan_stored"], 16)
            sp.wait_ge(n["plan_stored"], seen(16))
            for q in range(4):
                sp.dma_start(keep["plan"][q:q + 1, :, q:q + plan_steps], dram["plan"][None]).then_inc(n["plan_loaded"], 16)
            sp.wait_ge(n["plan_loaded"], seen(64))
            sp.wait_ge(n["carry_stored"], seen(16))

        @block.gpsimd
        def _(pool):
            pool.iota(node[:], pattern=[[P, NT]], base=0, channel_multiplier=1, allow_small_or_imprecise_dtypes=True).then_inc(n["iotas_ready"], 1)
            pool.iota(bounds[:], pattern=[[EL, P - 1]], base=EL, channel_multiplier=0, allow_small_or_imprecise_dtypes=True).then_inc(n["iotas_ready"], 1)
            pool.iota(step[:], pattern=[[1, SC]], base=0, channel_multiplier=SC, allow_small_or_imprecise_dtypes=True).then_inc(n["iotas_ready"], 1)
            pool.iota(blk_row[:, 2, :], pattern=[[1, NT]], base=0, channel_multiplier=0, allow_small_or_imprecise_dtypes=True).then_inc(n["iotas_ready"], 1)
            pool.memset(end_f[:], float(E)).then_inc(n["iotas_ready"], 1)
            pool.memset(zero_row[:], 0.0).then_inc(n["iotas_ready"], 1)
            pool.wait_ge(n["starts_loaded"], seen(16))
            pool.partition_broadcast(starts[:], start_row[:], channels=P).then_inc(n["starts_spread"], 1)
            pool.wait_ge(n["chunks_ready"], seen(1))
            for t in range(NT):
                pool.indirect_dma_start(rows[:, t, :], None, io["dst"].rearrange("(c e) -> c e", e=CH),
                                        bass.IndirectOffsetOnAxis(ap=chunk_i[:, t:t + 1], axis=0)).then_inc(n["rows_gathered"], 16)
            pool.wait_ge(n["blk_ready"], seen(1))
            pool.wait_ge(n["iotas_ready"], seen(6))
            pool.partition_broadcast(blk_all[:], blk_row[:].rearrange("a b c -> a (b c)"), channels=SP_).then_inc(n["blk_spread"], 1)
            pool.wait_ge(n["last_ready"], seen(2))
            pool.wait_ge(n["scan_stored"], seen(16))
            pool.wait_ge(n["carry_stored"], seen(16))
            for t in range(NT):
                pool.indirect_dma_start(m_scan[:, t, :], None, dram["scan"],
                                        bass.IndirectOffsetOnAxis(ap=last_i[:, t:t + 1], axis=0)).then_inc(n["m_gathered"], 16)
            for t in range(NT):
                pool.indirect_dma_start(m_carry[:, t, :], None, dram["carry"],
                                        bass.IndirectOffsetOnAxis(ap=part_i[:, t:t + 1], axis=0)).then_inc(n["m_gathered"], 16)

        @block.vector
        def _(dve):
            c = Chain(dve, n["done"])
            link = c.link
            link(dve.memset(keep["plan"][:], 0))
            dve.wait_ge(n["iotas_ready"], seen(6))
            dve.wait_ge(n["starts_spread"], seen(1))
            for t in range(NT):
                link(dve.tensor_scalar(junk[:, 0:NC], starts[:], node[:, t:t + 1], 0.0, ALU.is_lt, ALU.add, accum_out=count1[:, t:t + 1]))
            link(dve.tensor_scalar(chunk_f[:], count1[:], -1.0, 0.0, ALU.add, ALU.max))
            dve.tensor_copy(chunk_i[:], chunk_f[:]).then_inc(n["chunks_ready"], 1)
            dve.wait_ge(n["edges_loaded"], seen(32))
            dve.wait_ge(n["ends_loaded"], seen(32))
            link(dve.memset(pen[:, 0:1], FAR))
            link(dve.tensor_tensor(pen[:, 1:EL], dst[:, 1:EL], dst[:, 0:EL - 1], ALU.is_equal))
            link(dve.tensor_scalar(pen[:, 1:EL], pen[:, 1:EL], -1.0, -FAR, ALU.add, ALU.mult))
            for h in range(HEADS):
                dve.tensor_tensor_scan(AE[:, :, h], pen[:], AE[:, :, h], FAR, ALU.add, ALU.max).then_inc(n["scanned"], 1)
            dve.wait_ge(n["rows_gathered"], 16 * NT)
            for t in range(NT):
                link(dve.tensor_scalar(junk[:], rows[:, t, :], node[:, t:t + 1], 0.0, ALU.is_lt, ALU.add, accum_out=count2[:, t:t + 1]))
            dve.scalar_tensor_tensor(out=r0[:], in0=chunk_f[:], scalar=float(CH), in1=count2[:], op0=ALU.mult, op1=ALU.add).then_inc(n["rowptr_ready"], 1)
            link(dve.tensor_tensor(joins[:, 1:P], firsts[:, 1:P], lasts[:, 0:P - 1], ALU.is_equal))
            link(dve.tensor_tensor(whole[:], firsts[:], lasts[:], ALU.is_equal))
            link(dve.tensor_tensor(pen8[:, 1:P], joins[:, 1:P], whole[:, 0:P - 1], ALU.mult))
            link(dve.tensor_scalar(pen8[:, 1:P], pen8[:, 1:P], -1.0, -FAR, ALU.add, ALU.mult))
            link(dve.tensor_scalar(joins[:, 1:P], joins[:, 1:P], -1.0, -FAR, ALU.add, ALU.mult))
            dve.wait_ge(n["ends_ready"], seen(16))
            link(dve.tensor_tensor(joins[:, 1:P], joins[:, 1:P], endT[:, 0:P - 1], ALU.add))
            link(dve.memset(carryT[:, 0:1], FAR))
            dve.tensor_tensor_scan(carryT[:, 1:P], pen8[:, 1:P], joins[:, 1:P], FAR, ALU.add, ALU.max).then_inc(n["carry_ready"], 1)
            dve.wait_ge(n["rowptr_loaded"], seen(48))
            link(dve.tensor_tensor(blk_row[:, 1, :], blk[:, 1:NT + 1], blk[:, 0:NT], ALU.subtract))
            link(dve.tensor_scalar(blk_i[:], blk_row[:, 1, :], 511.0, None, ALU.add))
            link(dve.tensor_scalar(blk_i[:], blk_i[:], 9, None, ALU.arith_shift_right))
            link(dve.tensor_copy(blk_row[:, 1, :], blk_i[:]))
            link(dve.tensor_tensor_scan(blk_row[:, 0, :], blk_row[:, 1, :], zero_row[:], 0.0, ALU.add, ALU.add))
            link(dve.tensor_tensor(blk_row[:, 1, :], blk_row[:, 0, :], blk_row[:, 1, :], ALU.subtract))
            dve.scalar_tensor_tensor(out=blk_row[:, 1, :], in0=blk_row[:, 1, :], scalar=-512.0, in1=blk[:, 0:NT],
                                     op0=ALU.mult, op1=ALU.add).then_inc(n["blk_ready"], 1)
            dve.wait_ge(n["blk_spread"], seen(1))

            def over(i):
                return blk_all[:, None, i * NT:(i + 1) * NT].broadcast_to([SP_, SC, NT])

            link(dve.tensor_tensor(hit[:], over(0), step[:, :, None].broadcast_to([SP_, SC, NT]), ALU.is_le))
            link(dve.tensor_reduce(st_b[:], hit[:], AX.X, ALU.add))
            link(dve.tensor_tensor(hit[:], over(2), st_b[:, :, None].broadcast_to([SP_, SC, NT]), ALU.is_equal))
            link(dve.tensor_tensor(hit[:], hit[:], over(1), ALU.mult))
            link(dve.tensor_reduce(st_e[:], hit[:], AX.X, ALU.add))
            link(dve.scalar_tensor_tensor(out=st_e[:], in0=step[:], scalar=512.0, in1=st_e[:], op0=ALU.mult, op1=ALU.add))
            link(dve.tensor_scalar(st_f[:], st_b[:], float(NT), float(E), ALU.is_ge, ALU.mult))
            link(dve.tensor_tensor(st_e[:], st_e[:], st_f[:], ALU.add))
            dve.tensor_scalar(plan[:, 0, :], st_b[:], float(NT - 1), None, ALU.min).then_inc(n["plan_ready"], 1)
            dve.tensor_scalar(plan[:, 1, :], st_e[:], float(E), None, ALU.min).then_inc(n["plan_ready"], 1)
            link(dve.tensor_scalar(last_f[:], r1[:], -1.0, 0.0, ALU.add, ALU.max))
            dve.tensor_copy(last_i[:], last_f[:]).then_inc(n["last_ready"], 1)
            flat = rows[:].rearrange("p a b -> p (a b)").bitcast(F32)[:, 0:NT * (P - 1)].rearrange("p (t k) -> p t k", t=NT)
            link(dve.tensor_tensor(flat, bounds[:, None, :].broadcast_to([P, NT, P - 1]), last_f[:, :, None].broadcast_to([P, NT, P - 1]), ALU.is_le))
            link(dve.tensor_reduce(part_f[:], flat, AX.X, ALU.add))
            dve.tensor_copy(part_i[:], part_f[:]).then_inc(n["last_ready"], 1)
            link(dve.tensor_scalar(part_f[:], part_f[:], float(EL), None, ALU.mult))
            link(dve.tensor_tensor(spans[:], r0[:], part_f[:], ALU.is_lt))
            link(dve.tensor_scalar(spans[:], spans[:], -1.0, -FAR, ALU.add, ALU.mult))
            link(dve.tensor_tensor(empty[:], r0[:], r1[:], ALU.is_equal))
            link(dve.tensor_scalar(empty[:], empty[:], FAR, None, ALU.mult))
            dve.wait_ge(n["m_gathered"], 16 * 2 * NT)

            def wide(ap):
                return ap[:, :, None].broadcast_to([P, NT, HEADS])

            a_node = keep["a_node"]
            link(dve.tensor_tensor(m_carry[:], m_carry[:], wide(spans), ALU.add))
            link(dve.tensor_tensor(m_scan[:], m_scan[:], m_carry[:], ALU.max))
            link(dve.tensor_tensor(m_scan[:], m_scan[:], wide(empty), ALU.add))
            link(dve.tensor_tensor(m_scan[:], m_scan[:], a_node[:, :, 0:HEADS], ALU.max))
            link(dve.tensor_tensor(m_scan[:], m_scan[:], a_node[:, :, HEADS:], ALU.add))
            link(dve.scalar_tensor_tensor(out=pair_v[:, :, HEADS:], in0=m_scan[:], scalar=0.2, in1=m_scan[:], op0=ALU.mult, op1=ALU.max))
            link(dve.tensor_copy(keep["m_node"][:], pair_v[:, :, HEADS:]))
            link(dve.tensor_copy(pair_v[:, :, 0:HEADS], a_node[:, :, HEADS:]))
            parts = keep["pair_parts"]
            for i in range(3):
                link(dve.tensor_copy(parts[:, :, i, :], pair_v[:]))
                if i < 2:
                    link(dve.tensor_tensor(pair_v[:], pair_v[:], parts[:, :, i, :], ALU.subtract))


def aggregate(nc, io, dram, keep, NT, plan_steps):
    W = D + HEADS
    R = 4
    with ExitStack() as ctx:
        k = Kit(nc, ctx, "agg")
        node_ids = k.sb("node_ids", [128, NT * P], U16)
        acc, own = keep["acc"], keep["self"]
        z_own = k.sb("z_own", [P, NT, HEADS])
        dst4 = k.sb("dst4", [128, R, 4], U16)
        feats = k.sb("feats", [128, R, 4, W])
        msg = k.sb("msg", [128, R, 4, W])
        sel = k.sb("sel", [128, R, 4, P])
        sel_bf = k.sb("sel_bf", [128, R, 4, P], BF16)
        selT = k.sb("selT", [P, R, 4, 128], BF16)
        z = k.sb("z", [128, 2, 4, HEADS])
        ident_bf = k.sb("ident_bf", [128, 128], BF16)
        ps_selT = [k.ps(f"ps_selT{b}", [P, 8, 128], BF16)[:, 0:4, :] for b in range(2)]
        ps_pair = [k.ps(f"ps_pair{b}", [128, 4, 128])[:, :, 0:2 * HEADS] for b in range(2)]
        ps_sum = [k.ps(f"ps_sum{b}", [P, 512]) for b in range(R)]
        ring = lambda name: [k.sem(f"{name}{b}") for b in range(R)]
        passed_sp = k.sem("passed_sp")
        iota_ready, zeros_ready = k.sem("iota_ready"), k.sem("zeros_ready")
        own_loaded, own_ready, z_own_done, p_own_ready = (k.sem(n) for n in ("own_loaded", "own_ready", "z_own_done", "p_own_ready"))
        ident_ready, dst_loaded, rows_loaded = k.sem("ident_ready"), ring("dst_loaded"), ring("rows_loaded")
        sel_bf_ready, sel_ready, selT_in_psum, selT_ready, pair_in_psum = ring("sel_bf_ready"), ring("sel_ready"), ring("selT_in_psum"), ring("selT_ready"), ring("pair_in_psum")
        z_added, z_leaked, z_below = ring("z_added"), ring("z_leaked"), ring("z_below")
        z_ready, p_ready, msg_ready, sum_in_psum, sum_added = ring("z_ready"), ring("p_ready"), ring("msg_ready"), ring("sum_in_psum"), ring("sum_added")
        block = k.start()
        plan = keep["plan"]
        TURNS = plan_steps // R

        BLOCK, FIRST = 0, 1
        limits = (NT - 1, io["src"].shape[0])

        def before(sems, r, b, back):
            return sems[(b - back) % R], seen(r + 1 + (b - back) // R)

        def in_turns(eng, parts):
            depth = max(lag for lag, _, _ in parts)
            first = -(-depth // R) * R
            regs = [[eng.alloc_register(name=f"{k.stage}_{f.__name__}{b}") for b in range(R)] if field is not None else None for _, f, field in parts]

            def turns(i, j, n):
                for (lag, _, field), to in zip(parts, regs):
                    if field is not None:
                        q = lag % R
                        eng.load(to, plan[q:q + 1, field, ds(R * j + max(i - lag + q, 0), R)])
                for b in range(n):
                    for (lag, f, field), to in zip(parts, regs):
                        step = i + b - lag
                        if not isinstance(j, int) or 0 <= step < plan_steps:
                            value = () if field is None else (eng.snap(to[b], min_val=0, max_val=limits[field]),)
                            f(j + step // R, step % R, *value)

            for i in range(0, first, R):
                turns(i, 0, R)
            with eng.Fori(0, (plan_steps - first) // R, 1) as j:
                turns(first, j, R)
            for i in range(plan_steps, plan_steps + depth, R):
                turns(i, 0, min(R, plan_steps + depth - i))

        @block.sync
        def _(sp):
            def load_dst(r, b, first):
                wait_apart(sp, sel_bf_ready[b], seen(r), passed_sp)
                sp.dma_start(dst4[:, b, :], dram["dst_pad"][ds(first, 512)].rearrange("(p c) -> p c", c=4)).then_inc(dst_loaded[b], 16)

            def load_rows(r, b, first):
                wait_apart(sp, msg_ready[b], seen(r), passed_sp)
                sp.dma_start(feats[:, b], dram["edge_rows"][ds(first, 512), :].rearrange("(p c) w -> p c w", c=4)).then_inc(rows_loaded[b], 16)

            sp.dma_start(own[:], dram["node_rows"].rearrange("(t p) w -> p t w", p=P)).then_inc(own_loaded, 16)
            in_turns(sp, [(0, load_dst, FIRST), (3, load_rows, FIRST)])
            for b in range(R):
                sp.wait_ge(sum_added[b], seen(TURNS))

        @block.gpsimd
        def _(pool):
            pool.iota(node_ids[:], pattern=[[1, NT * P]], base=0, channel_multiplier=0, allow_small_or_imprecise_dtypes=True).then_inc(iota_ready, 1)
            pool.wait_ge(p_own_ready, seen(1))
            pool.wait_ge(own_loaded, seen(16))
            pool.tensor_copy(own[:, :, D:W], z_own[:]).then_inc(own_ready, 1)
            pool.tensor_tensor(own[:, :, 0:D].rearrange("p t (h e) -> p t h e", e=DH), own[:, :, 0:D].rearrange("p t (h e) -> p t h e", e=DH),
                               z_own[:, :, :, None].broadcast_to([P, NT, HEADS, DH]), ALU.mult).then_inc(own_ready, 1)
            pool.wait_ge(own_ready, seen(2))

        @block.vector
        def _(dve):
            dve.tensor_tensor(z_own[:], keep["a_node"][:, :, 0:HEADS], keep["a_node"][:, :, HEADS:], ALU.add).then_inc(z_own_done, 1)
            dve.wait_ge(z_own_done, seen(1))
            dve.scalar_tensor_tensor(out=z_own[:], in0=z_own[:], scalar=0.2, in1=z_own[:], op0=ALU.mult, op1=ALU.max).then_inc(z_own_done, 1)
            dve.wait_ge(z_own_done, seen(2))
            dve.tensor_tensor(z_own[:], z_own[:], keep["m_node"][:], ALU.subtract).then_inc(z_own_done, 1)
            dve.memset(acc[:], 0.0).then_inc(zeros_ready, 1)
            dve.tensor_copy(ident_bf[:], keep["ident"][:]).then_inc(ident_ready, 1)
            dve.wait_ge(iota_ready, seen(1))
            dve.wait_ge(zeros_ready, seen(1))

            def one_hot(r, b, n):
                dve.wait_ge(dst_loaded[b], seen((r + 1) * 16))
                dve.wait_ge(sel_ready[b], seen(r))
                dve.wait_ge(selT_in_psum[b], seen(r))
                dve.tensor_tensor(sel_bf[:, b], node_ids[:, None, ds(n * P, P)].broadcast_to([128, 4, P]),
                                  dst4[:, b, :, None].broadcast_to([128, 4, P]), ALU.is_equal).then_inc(sel_bf_ready[b], 1)

            def logits(r, b):
                dve.wait_ge(rows_loaded[b], seen((r + 1) * 16))
                dve.wait_ge(pair_in_psum[b], seen(r + 1))
                dve.tensor_tensor(z[:, b % 2], feats[:, b, :, D:W], ps_pair[b % 2][:, :, 0:HEADS], ALU.add).then_inc(z_added[b], 1)

            def leak(r, b):
                dve.wait_ge(z_added[b], seen(r + 1))
                dve.scalar_tensor_tensor(out=z[:, b % 2], in0=z[:, b % 2], scalar=0.2, in1=z[:, b % 2], op0=ALU.mult, op1=ALU.max).then_inc(z_leaked[b], 1)

            def less_maximum(r, b):
                dve.wait_ge(z_leaked[b], seen(r + 1))
                dve.wait_ge(sum_in_psum[b], seen(r))
                dve.tensor_tensor(msg[:, b, :, D:W], z[:, b % 2], ps_pair[b % 2][:, :, HEADS:], ALU.subtract).then_inc(z_ready[b], 1)

            def messages(r, b):
                dve.wait_ge(p_ready[b], seen(r + 1))
                dve.tensor_tensor(msg[:, b, :, 0:D].rearrange("p c (h e) -> p c h e", e=DH), feats[:, b, :, 0:D].rearrange("p c (h e) -> p c h e", e=DH),
                                  msg[:, b, :, D:W, None].broadcast_to([128, 4, HEADS, DH]), ALU.mult).then_inc(msg_ready[b], 1)

            def add(r, b, n):
                dve.wait_ge(sum_in_psum[b], seen(r + 1))
                dve.wait_ge(*before(sum_added, r, b, 1))
                rows = acc[:, ds(n, 1), :]
                dve.tensor_tensor(rows, ps_sum[b][:, None, 0:W], rows, ALU.add).then_inc(sum_added[b], 1)

            in_turns(dve, [(3, logits, None), (0, one_hot, BLOCK), (3, leak, None), (4, messages, None), (3, less_maximum, None), (6, add, BLOCK)])

        @block.tensor
        def _(pe):
            def transposes(r, b):
                pe.wait_ge(sel_bf_ready[b], seen(r + 1))
                pe.wait_ge(*before(selT_ready, r, b, 2))
                for c in range(4):
                    last = pe.transpose(ps_selT[b % 2][:, c, :], sel_bf[:, b, c, :], ident_bf[:])
                last.then_inc(selT_in_psum[b], 1)

            def expand(r, b, n):
                pe.wait_ge(selT_ready[b], seen(r + 1))
                pe.wait_ge(*before(z_ready, r, b, 2))
                for c in range(4):
                    for i in range(3):
                        last = pe.matmul(ps_pair[b % 2][:, c, :], selT[:, b, c, :], keep["pair_parts"][:, ds(n, 1), i, :], start=(i == 0), stop=(i == 2))
                last.then_inc(pair_in_psum[b], 1)

            def product(r, b):
                pe.wait_ge(sel_ready[b], seen(r + 1))
                pe.wait_ge(msg_ready[b], seen(r + 1))
                pe.wait_ge(sum_added[b], seen(r))
                for c in range(4):
                    last = pe.matmul(ps_sum[b][:, 0:W], sel[:, b, c, :], msg[:, b, c, :], start=(c == 0), stop=(c == 3))
                last.then_inc(sum_in_psum[b], 1)

            pe.wait_ge(ident_ready, seen(1))
            in_turns(pe, [(2, expand, BLOCK), (1, transposes, None), (5, product, None)])

        @block.scalar
        def _(act):
            def turn_selT(r, b):
                act.wait_ge(selT_in_psum[b], seen(r + 1))
                act.wait_ge(pair_in_psum[b], seen(r))
                act.activation(selT[:, b], ps_selT[b % 2][:], ACT.Copy).then_inc(selT_ready[b], 1)

            def exps(r, b):
                act.wait_ge(z_ready[b], seen(r + 1))
                act.activation(msg[:, b, :, D:W], msg[:, b, :, D:W], ACT.Relu, scale=-1.0).then_inc(z_below[b], 1)
                act.wait_ge(z_below[b], seen(r + 1))
                act.activation(msg[:, b, :, D:W], msg[:, b, :, D:W], ACT.Exp, scale=-1.0).then_inc(p_ready[b], 1)

            def copy_sel(r, b):
                act.wait_ge(sum_in_psum[b], seen(r))
                act.wait_ge(sel_bf_ready[b], seen(r + 1))
                act.activation(sel[:, b], sel_bf[:, b], ACT.Copy).then_inc(sel_ready[b], 1)

            act.preload_act_table(ACT.Exp)
            act.wait_ge(z_own_done, seen(3))
            act.activation(z_own[:], z_own[:], ACT.Exp).then_inc(p_own_ready, 1)
            in_turns(act, [(1, turn_selT, None), (2, copy_sel, None), (3, exps, None)])


def combine_and_route(nc, io, dram, keep, NT, CAP, SLOTS):
    N = io["x"].shape[0]
    W = D + HEADS
    NX = io["L0_ffn_gate_w"].shape[1]
    BIG = float(1 << 20)
    PIECES = -(-NX * SLOTS * D // (128 * 2048))
    with ExitStack() as ctx:
        k = Kit(nc, ctx, "comb")
        acc = keep["acc"]
        rows = keep["self"]
        base = k.sb("base", [P, NT, D])
        den = k.sb("den", [P, NT, HEADS])
        vecs = k.sb("vecs", [P, 3, D])
        mean, gain, vtmp = k.sb("mean", [P, D]), k.sb("gain", [P, D]), k.sb("vtmp", [P, 2, D])
        ones = k.sb("ones", [P, P])
        upper = k.sb("upper", [P, P])
        gate_w, gate_b = k.sb("gate_w", [128, KC, NX]), k.sb("gate_b", [P, 1, NX])
        stats, ln_mean, ln_var, rstd, rtmp = k.sb("stats", [P, NT, 6]), k.sb("ln_mean", [P, NT, 1]), k.sb("ln_var", [P, NT]), k.sb("rstd", [P, NT, 1]), k.sb("rtmp", [P, 2, NT])
        h_tile, hT = k.sb("h_tile", [P, 2, D]), k.sb("hT", [128, 2, KC, P])
        zero_rows = k.sb("zero_rows", [128, 2048])
        logits, e, hot = k.sb("logits", [P, NT, NX]), k.sb("e", [P, NT, NX]), k.sb("hot", [P, NT, NX])
        expert_no = k.sb("expert_no", [P, 1, NX])
        total, upto = k.sb("total", [P, NT, NX]), k.sb("upto", [P, NT, NX])
        ones_row = k.sb("ones_row", [P, NT])
        col = {c: k.sb(f"col_{c}", [P, NT]) for c in ("top", "sum", "rec", "pick", "pos", "kept", "late", "slot")}
        slot_i = k.sb("slot_i", [P, NT], U32)
        ps_sum, ps_sq = k.ps("ps_sum", [P, 512]), k.ps("ps_sq", [P, 512])
        ps_t = [k.ps(f"ps_t{b}", [128, 4, 128])[:, 0:KC, 0:P] for b in range(2)]
        ps_gate, ps_pos, ps_tot = k.ps("ps_gate", [P, 512]), k.ps("ps_pos", [P, 512]), k.ps("ps_tot", [P, 512])
        n = {name: k.sem(name) for name in (
            "base_loaded", "vecs_loaded", "consts", "done", "out_ready", "sum_in_psum",
            "centred", "squared", "sq_in_psum", "x1_ready", "x1_stored", "stat_done", "h_ready", "e_in", "e_out",
            "hot_ready", "pos_in_psum", "slot_ready", "zeroed")}
        n["scattered"] = k.gather_sem("scattered")
        pair = lambda name: [k.sem(f"{name}{b}") for b in range(2)]
        h_copied, hT_in_psum, hT_ready, gate_done = pair("h_copied"), pair("hT_in_psum"), pair("hT_ready"), pair("gate_done")
        block = k.start()

        @block.sync
        def _(sp):
            sp.dma_start(base[:], dram["mix_out"].rearrange("(t p) d -> p t d", p=P)).then_inc(n["base_loaded"], 16)
            for i, name in enumerate(("L0_gnn_bias", "L0_gnn_gamma", "L0_gnn_beta")):
                sp.dma_start(vecs[:, i, :], row(io[name], P)).then_inc(n["vecs_loaded"], 16)
            sp.dma_start(gate_w[:], io["L0_ffn_gate_w"].rearrange("(k p) n -> p k n", p=128)).then_inc(n["vecs_loaded"], 16)
            sp.dma_start(gate_b[:, 0, :], row(io["L0_ffn_gate_b"], P)).then_inc(n["vecs_loaded"], 16)
            sp.wait_ge(n["consts"], seen(6))
            flat = dram["buf"].rearrange("s d -> (s d)")
            size = NX * SLOTS * D
            piece = 128 * 2048
            done, pieces = 0, 0
            while done < size:
                width = min(piece, size - done) // 128
                sp.dma_start(flat[done:done + 128 * width].rearrange("(p c) -> p c", p=128), zero_rows[:, 0:width]).then_inc(n["zeroed"], 16)
                done += 128 * width
                pieces += 1
            assert done == size and pieces == PIECES
            sp.wait_ge(n["x1_ready"], seen(1))
            sp.dma_start(dram["x1"].rearrange("(t p) d -> p t d", p=P), acc[:, :, 0:D]).then_inc(n["x1_stored"], 16)
            sp.wait_ge(n["x1_stored"], seen(16))

        @block.gpsimd
        def _(pool):
            pool.memset(ones[:], 1.0).then_inc(n["consts"], 1)
            pool.memset(upper[:], 1.0).then_inc(n["consts"], 1)
            pool.memset(zero_rows[:], 0.0).then_inc(n["consts"], 1)
            pool.memset(ones_row[:], 1.0).then_inc(n["consts"], 1)
            pool.iota(expert_no[:, 0, :], pattern=[[1, NX]], base=0, channel_multiplier=0, allow_small_or_imprecise_dtypes=True).then_inc(n["consts"], 1)
            pool.wait_ge(n["consts"], seen(5))
            pool.affine_select(out=upper[:], in_=upper[:], compare_op=ALU.is_ge, fill=0.0, base=0, pattern=[[1, P]],
                               channel_multiplier=-1).then_inc(n["consts"], 1)
            pool.wait_ge(n["zeroed"], seen(PIECES * 16))
            pool.wait_ge(n["h_ready"], seen(NT))
            pool.wait_ge(n["slot_ready"], seen(1))
            for t in range(NT):
                pool.indirect_dma_start(dram["buf"], bass.IndirectOffsetOnAxis(ap=slot_i[:, t:t + 1], axis=0), rows[:, t, 0:D], None,
                                        bounds_check=NX * SLOTS - 1, oob_is_err=False).then_inc(n["scattered"], 16)
            pool.wait_ge(n["scattered"], NT * 16)

        @block.vector
        def _(dve):
            c = Chain(dve, n["done"])
            link = c.link
            tt, ts, stt = dve.tensor_tensor, dve.tensor_scalar, dve.scalar_tensor_tensor

            def heads(ap):
                return ap.rearrange("p t (h e) -> p t h e", e=DH)

            def by_head(ap):
                return ap[:, :, :, None].broadcast_to([P, NT, HEADS, DH])

            def by_row(ap):
                return ap[:, None, :].broadcast_to([P, NT, D])

            dve.wait_ge(n["consts"], seen(6))
            link(tt(acc[:], acc[:], rows[:], ALU.add))
            link(dve.reciprocal(den[:], acc[:, :, D:W]))
            link(tt(heads(acc[:, :, 0:D]), heads(acc[:, :, 0:D]), by_head(den[:]), ALU.mult))
            dve.wait_ge(n["vecs_loaded"], seen(16 * 5))
            tt(acc[:, :, 0:D], acc[:, :, 0:D], by_row(vecs[:, 0, :]), ALU.add).then_inc(n["out_ready"], 1)
            dve.wait_ge(n["base_loaded"], seen(16))
            link(tt(base[:], base[:], by_row(vecs[:, 2, :]), ALU.add))
            dve.wait_ge(n["sum_in_psum"], seen(1))
            link(ts(mean[:], ps_sum[:, 0:D], 1.0 / N, None, ALU.mult))
            dve.wait_ge(n["out_ready"], seen(1))
            tt(acc[:, :, 0:D], acc[:, :, 0:D], by_row(mean[:]), ALU.subtract).then_inc(n["centred"], 1)
            dve.wait_ge(n["sq_in_psum"], seen(1))
            link(ts(gain[:], ps_sq[:, 0:D], 1.0 / N, None, ALU.mult))
            rsqrt_eps(dve, c, mean[:], gain[:], (vtmp[:, 0, :], vtmp[:, 1, :]))
            link(tt(gain[:], mean[:], vecs[:, 1, :], ALU.mult))
            dve.wait_ge(n["centred"], seen(1))
            link(tt(acc[:, :, 0:D], acc[:, :, 0:D], by_row(gain[:]), ALU.mult))
            tt(acc[:, :, 0:D], acc[:, :, 0:D], base[:], ALU.add).then_inc(n["x1_ready"], 1)
            dve.wait_ge(n["x1_ready"], seen(1))
            with dve.Fori(0, NT, 1) as t:
                dve.bn_stats(stats[:, ds(t, 1), :], acc[:, ds(t, 1), 0:D]).then_inc(n["stat_done"], 1)
            dve.wait_ge(n["stat_done"], seen(NT))
            aggregate_stats(dve, c, ln_mean[:, :, 0], ln_var[:], stats, D)
            rsqrt_eps(dve, c, rstd[:, :, 0], ln_var[:], (rtmp[:, 0, :], rtmp[:, 1, :]))
            with dve.Fori(0, NT, 1) as t:
                ts(rows[:, ds(t, 1), 0:D], acc[:, ds(t, 1), 0:D], ln_mean[:, ds(t, 1), 0], rstd[:, ds(t, 1), 0],
                   ALU.subtract, ALU.mult).then_inc(n["h_ready"], 1)
            for b in range(2):
                dve.wait_ge(gate_done[b], seen(NT // 2))

            def by_token(ap):
                return ap[:, :, None].broadcast_to([P, NT, NX])

            link(tt(logits[:], ps_gate[:, 0:NT * NX].rearrange("p (t x) -> p t x", x=NX), gate_b[:].broadcast_to([P, NT, NX]), ALU.add))
            link(dve.tensor_reduce(col["top"][:], logits[:], AX.X, ALU.max))
            tt(logits[:], logits[:], by_token(col["top"]), ALU.subtract).then_inc(n["e_in"], 1)
            dve.wait_ge(n["e_out"], seen(1))
            link(dve.tensor_reduce(col["sum"][:], e[:], AX.X, ALU.add))
            link(dve.tensor_reduce(col["top"][:], e[:], AX.X, ALU.max))
            link(dve.reciprocal(col["rec"][:], col["sum"][:]))
            link(tt(hot[:], e[:], by_token(col["top"]), ALU.is_lt))
            link(stt(out=hot[:], in0=hot[:], scalar=float(NX), in1=expert_no[:].broadcast_to([P, NT, NX]), op0=ALU.mult, op1=ALU.add))
            link(dve.tensor_reduce(col["pick"][:], hot[:], AX.X, ALU.min))
            tt(hot[:], expert_no[:].broadcast_to([P, NT, NX]), by_token(col["pick"]), ALU.is_equal).then_inc(n["hot_ready"], 1)
            link(tt(col["rec"][:], col["rec"][:], col["top"][:], ALU.mult))
            dve.wait_ge(n["pos_in_psum"], seen(1))
            link(dve.tensor_copy(total[:], ps_tot[:, 0:NT * NX].rearrange("p (t x) -> p t x", x=NX)))
            for x in range(NX):
                c.step(dve.tensor_tensor_scan(upto[:, :, x], ones_row[:], total[:, :, x], 0.0, ALU.mult, ALU.add))
            c.after()
            link(tt(upto[:], upto[:], total[:], ALU.subtract))
            link(tt(upto[:], upto[:], ps_pos[:, 0:NT * NX].rearrange("p (t x) -> p t x", x=NX), ALU.add))
            dve.wait_ge(n["hot_ready"], seen(1))
            link(tt(upto[:], upto[:], hot[:], ALU.mult))
            link(dve.tensor_reduce(col["pos"][:], upto[:], AX.X, ALU.add))
            link(ts(col["pos"][:], col["pos"][:], -1.0, None, ALU.add))
            link(ts(col["kept"][:], col["pos"][:], float(CAP), None, ALU.is_lt))
            link(ts(col["late"][:], col["pos"][:], float(CAP), BIG, ALU.is_ge, ALU.mult))
            link(ts(col["slot"][:], col["pick"][:], float(SLOTS), None, ALU.mult))
            link(tt(col["pos"][:], col["pos"][:], col["late"][:], ALU.add))
            link(tt(col["late"][:], col["slot"][:], col["pos"][:], ALU.add))
            dve.tensor_copy(slot_i[:], col["late"][:]).then_inc(n["slot_ready"], 1)
            link(ts(col["pos"][:], col["pos"][:], float(CAP - 1), None, ALU.min))
            link(tt(col["slot"][:], col["slot"][:], col["pos"][:], ALU.add))
            link(dve.tensor_copy(keep["slot"][:], col["slot"][:]))
            link(tt(keep["weight"][:], col["rec"][:], col["kept"][:], ALU.mult))

        @block.tensor
        def _(pe):
            pe.wait_ge(n["consts"], seen(6))
            pe.wait_ge(n["vecs_loaded"], seen(16 * 5))
            for ready, what, bank, done in (("out_ready", acc, ps_sum, "sum_in_psum"), ("squared", rows, ps_sq, "sq_in_psum")):
                pe.wait_ge(n[ready], seen(1))
                pe.matmul(bank[:, 0:D], ones[:], what[:, 0, 0:D], start=True, stop=False)
                with pe.Fori(1, NT - 1, 1) as t:
                    pe.matmul(bank[:, 0:D], ones[:], what[:, ds(t, 1), 0:D], start=False, stop=False, skip_group_check=True)
                pe.matmul(bank[:, 0:D], ones[:], what[:, NT - 1, 0:D], start=False, stop=True).then_inc(n[done], 1)
            with pe.Fori(0, NT // 2, 1) as g:
                for b in range(2):
                    pe.wait_ge(h_copied[b], seen(g + 1))
                    pe.wait_ge(hT_ready[b], seen(g))
                    for kc in range(KC):
                        last = pe.transpose(ps_t[b][:, kc, :], h_tile[:, b, kc * 128:(kc + 1) * 128], keep["ident"][0:P, 0:P])
                    last.then_inc(hT_in_psum[b], 1)
                for b in range(2):
                    pe.wait_ge(hT_ready[b], seen(g + 1))
                    for kc in range(KC):
                        last = pe.matmul(ps_gate[:, ds((2 * g + b) * NX, NX)], hT[:, b, kc, :], gate_w[:, kc, :], start=(kc == 0), stop=(kc == KC - 1))
                    last.then_inc(gate_done[b], 1)
            pe.wait_ge(n["hot_ready"], seen(1))
            flat = hot[:].rearrange("p t x -> p (t x)")
            pe.matmul(ps_pos[:, 0:NT * NX], upper[:], flat, start=True, stop=True)
            pe.matmul(ps_tot[:, 0:NT * NX], ones[:], flat, start=True, stop=True).then_inc(n["pos_in_psum"], 1)

        @block.scalar
        def _(act):
            act.wait_ge(n["centred"], seen(1))
            act.activation(rows[:, :, 0:D], acc[:, :, 0:D], ACT.Square).then_inc(n["squared"], 1)
            with act.Fori(0, NT // 2, 1) as g:
                for b in range(2):
                    act.wait_ge(n["h_ready"], seen(2 * g + b + 1))
                    act.wait_ge(hT_in_psum[b], seen(g))
                    act.activation(h_tile[:, b, None, :], rows[:, ds(2 * g + b, 1), 0:D], ACT.Copy).then_inc(h_copied[b], 1)
                for b in range(2):
                    act.wait_ge(hT_in_psum[b], seen(g + 1))
                    act.wait_ge(gate_done[b], seen(g))
                    act.activation(hT[:, b], ps_t[b], ACT.Copy).then_inc(hT_ready[b], 1)
            act.wait_ge(n["e_in"], seen(1))
            act.activation(e[:], logits[:], ACT.Exp).then_inc(n["e_out"], 1)


def experts(nc, io, dram, keep, TILE, SLOTS):
    NX, _, FF = io["L0_ffn_w1"].shape
    FC = FF // 128
    T2 = 2 * TILE
    CX = SLOTS // T2
    assert NX % 2 == 0 and CX % 2 == 0 and CX * T2 == SLOTS
    TURN = 2 * CX
    with ExitStack() as ctx:
        k = Kit(nc, ctx, "exp")
        w1, w2 = k.sb("w1", [128, 2, KC, FF]), k.sb("w2", [128, 2, FC, D])
        b1, b2 = k.sb("b1", [128, 2, FC]), k.sb("b2", [TILE, 2, 1, D])
        w1_high, w1_rest = (k.sb(n, [128, 2, KC, FF]) for n in ("w1_high", "w1_rest"))
        w2_high, w2_rest = (k.sb(n, [128, 2, FC, D]) for n in ("w2_high", "w2_rest"))
        tok, tokT = k.sb("tok", [TILE, 2, 2, D]), k.sb("tokT", [128, 2, KC, T2])
        tokT_high, tokT_rest = (k.sb(n, [128, 2, KC, T2]) for n in ("tokT_high", "tokT_rest"))
        u_raw = k.sb("u_raw", [128, 2, 2, T2])
        uT_high, uT_rest = (k.sb(n, [128, 2, FC, T2]) for n in ("uT_high", "uT_rest"))
        y = k.sb("y", [TILE, 2, 2, D])
        ps_t = [k.ps(f"ps_t{b}", [128, 512])[:, 0:KC * T2].rearrange("p (k n) -> p k n", k=KC) for b in range(2)]
        ps_u = [k.ps(f"ps_u{f}", [128, 512])[:, 0:KC * T2].rearrange("p (k n) -> p k n", k=2) for f in range(FC // 2)]
        ps_y = [k.ps(f"ps_y{b}", [128, 512])[0:TILE].rearrange("p (t d) -> p t d", t=2) for b in range(2)]
        pair = lambda name: [k.sem(f"{name}{b}") for b in range(2)]
        w_loaded, tok_loaded, tokT_in_psum, tokT_ready = pair("w_loaded"), pair("tok_loaded"), pair("tokT_in_psum"), pair("tokT_ready")
        u_in_psum, relu_done = ([k.sem(f"{n}{f}") for f in range(FC // 2)] for n in ("u_in_psum", "relu_done"))
        w_high_done, w_split, tok_high_done, tok_split = pair("w_high_done"), pair("w_split"), pair("tok_high_done"), pair("tok_split")
        u_high_done, u_split = ([k.sem(f"{n}{f}") for f in range(FC // 2)] for n in ("u_high_done", "u_split"))
        y_in_psum, y_ready, y_stored = pair("y_in_psum"), pair("y_ready"), pair("y_stored")
        block = k.start()
        buf = dram["buf"].rearrange("(c t p) d -> c p t d", t=2, p=TILE)
        ybuf = dram["ybuf"].rearrange("(c t p) d -> c p t d", t=2, p=TILE)

        class Chunk:

            def __init__(self, i, r):
                self.k, self.r = i, r
                self.i = TURN * r + i
                self.b, self.m = i % 2, (TURN // 2) * r + i // 2
                self.wb, self.wm = (i // CX) % 2, r + i // TURN

        def run(*steps):
            def turn(i, r):
                for lag, f in steps:
                    if r is None and not 0 <= i - lag < NX * CX:
                        continue
                    f(Chunk(i - lag, 0 if r is None else r))
            return turn

        def loop(eng, *steps):
            turn = run(*steps)
            depth = max(lag for lag, _ in steps)
            for i in range(depth):
                turn(i, None)
            with eng.Fori(0, NX // 2 - 1, 1) as r:
                for i in range(depth, TURN + depth):
                    turn(i, r)
            for i in range(NX * CX - TURN + depth, NX * CX + depth):
                turn(i, None)

        @block.sync
        def _(sp):
            def load_weights(x, slot, before):
                for b in range(2):
                    sp.wait_ge(y_ready[b], seen(before))
                one = ds(x, 1)
                sp.dma_start(w1[:, slot], io["L0_ffn_w1"][one].rearrange("x (k p) n -> p (x k) n", p=128)).then_inc(w_loaded[slot], 16)
                sp.dma_start(w2[:, slot], io["L0_ffn_w2"][one].rearrange("x (k p) n -> p (x k) n", p=128)).then_inc(w_loaded[slot], 16)
                sp.dma_start(b1[:, slot], io["L0_ffn_b1"][one].rearrange("x (k p) -> p (x k)", p=128),
                             allow_slow_non_contiguous=True).then_inc(w_loaded[slot], 16)
                sp.dma_start(b2[:, slot], io["L0_ffn_b2"][one][None].broadcast_to([TILE, 1, D])).then_inc(w_loaded[slot], 16)

            def load(c):
                if c.k == 0:
                    load_weights(0, 0, 0)
                if c.k % CX == 2 and c.k // CX != NX - 1:
                    e = c.k // CX
                    load_weights(e + 1 + 2 * c.r, (e + 1) % 2, e * (CX // 2) + CX * c.r)
                sp.wait_ge(tokT_in_psum[c.b], seen(c.m))
                sp.dma_start(tok[:, c.b], buf[ds(c.i, 1)].rearrange("c p t d -> p (c t) d")).then_inc(tok_loaded[c.b], 16)

            def store(c):
                sp.wait_ge(y_ready[c.b], seen(c.m + 1))
                sp.dma_start(ybuf[ds(c.i, 1)].rearrange("c p t d -> p (c t) d"), y[:, c.b]).then_inc(y_stored[c.b], 16)

            loop(sp, (0, load), (3, store))
            for b in range(2):
                sp.wait_ge(y_stored[b], seen(NX * CX // 2 * 16))

        @block.vector
        def _(dve):
            def take(c):
                dve.wait_ge(y_in_psum[c.b], seen(c.m + 1))
                dve.wait_ge(y_stored[c.b], seen(c.m * 16))
                dve.tensor_tensor(y[:, c.b], ps_y[c.b], b2[:, c.wb].broadcast_to([TILE, 2, D]), ALU.add).then_inc(y_ready[c.b], 1)

            def split_weights(x, r):
                slot, uses = x % 2, r + x // 2
                dve.wait_ge(w_loaded[slot], seen((uses + 1) * 64))
                split_high(dve, w1_high[:, slot], w1[:, slot]).then_inc(w_high_done[slot], 1)
                split_high(dve, w2_high[:, slot], w2[:, slot]).then_inc(w_high_done[slot], 1)
                dve.wait_ge(w_high_done[slot], seen(uses * 2 + 1))
                split_rest(dve, w1_rest[:, slot], w1[:, slot], w1_high[:, slot]).then_inc(w_split[slot], 1)
                dve.wait_ge(w_high_done[slot], seen(uses * 2 + 2))
                split_rest(dve, w2_rest[:, slot], w2[:, slot], w2_high[:, slot]).then_inc(w_split[slot], 1)

            def next_weights(c):
                if c.k % CX == CX - 1 and c.k // CX != NX - 1:
                    split_weights(c.k // CX + 1, c.r)

            def split_tok(c):
                dve.wait_ge(tokT_ready[c.b], seen(c.m + 1))
                split_high(dve, tokT_high[:, c.b], tokT[:, c.b]).then_inc(tok_high_done[c.b], 1)
                dve.wait_ge(tok_high_done[c.b], seen(c.m + 1))
                split_rest(dve, tokT_rest[:, c.b], tokT[:, c.b], tokT_high[:, c.b]).then_inc(tok_split[c.b], 1)

            def split_u(c):
                def high(f):
                    dve.wait_ge(relu_done[f], seen(c.i + 1))
                    split_high(dve, uT_high[:, c.b, 2 * f:2 * f + 2], u_raw[:, f % 2]).then_inc(u_high_done[f], 1)

                def rest(f):
                    dve.wait_ge(u_high_done[f], seen(c.i + 1))
                    quarter = slice(2 * f, 2 * f + 2)
                    split_rest(dve, uT_rest[:, c.b, quarter], u_raw[:, f % 2], uT_high[:, c.b, quarter]).then_inc(u_split[f], 1)

                dve.wait_ge(y_in_psum[c.b], seen(c.m))
                high(0)
                for f in range(1, FC // 2):
                    high(f)
                    rest(f - 1)
                rest(FC // 2 - 1)

            split_weights(0, 0)
            loop(dve, (3, take), (0, split_tok), (1, split_u), (0, next_weights))

        @block.tensor
        def _(pe):
            def transposes(c):
                pe.wait_ge(tok_loaded[c.b], seen((c.m + 1) * 16))
                pe.wait_ge(tokT_ready[c.b], seen(c.m))
                for kc in range(KC):
                    for t in range(2):
                        last = pe.transpose(ps_t[c.b][:, kc, t * TILE:(t + 1) * TILE], tok[:, c.b, t, kc * 128:(kc + 1) * 128], keep["ident"][0:TILE, 0:TILE])
                last.then_inc(tokT_in_psum[c.b], 1)

            def down(c):
                pe.wait_ge(y_ready[c.b], seen(c.m))
                for f in range(FC // 2):
                    pe.wait_ge(u_split[f], seen(c.i + 1))
                for t in range(2):
                    for f in range(FC):
                        lhs = [u[:, c.b, f, t * TILE:(t + 1) * TILE] for u in (uT_high, uT_rest)]
                        last = product_of_parts(pe, ps_y[c.b][:, t, :], lhs, [w[:, c.wb, f, :] for w in (w2_high, w2_rest)], f == 0, f == FC - 1)
                last.then_inc(y_in_psum[c.b], 1)

            def up(c):
                pe.wait_ge(w_split[c.wb], seen((c.wm + 1) * 2))
                pe.wait_ge(tok_split[c.b], seen(c.m + 1))
                for f in range(FC):
                    if f % 2 == 0:
                        pe.wait_ge(relu_done[f // 2], seen(c.i))
                    for kc in range(KC):
                        lhs = [w[:, c.wb, kc, f * 128:(f + 1) * 128] for w in (w1_high, w1_rest)]
                        last = product_of_parts(pe, ps_u[f // 2][:, f % 2, :], lhs, [x[:, c.b, kc, :] for x in (tokT_high, tokT_rest)], kc == 0, kc == KC - 1)
                    if f % 2:
                        last.then_inc(u_in_psum[f // 2], 1)

            loop(pe, (0, transposes), (1, up), (2, down))

        @block.scalar
        def _(act):
            def take_T(c):
                act.wait_ge(tokT_in_psum[c.b], seen(c.m + 1))
                act.activation(tokT[:, c.b], ps_t[c.b], ACT.Copy).then_inc(tokT_ready[c.b], 1)

            def relu(c):
                act.wait_ge(w_loaded[c.wb], seen((c.wm + 1) * 64))
                for f in range(FC // 2):
                    act.wait_ge(u_in_psum[f], seen(c.i + 1))
                    act.wait_ge(u_split[(f + 2) % (FC // 2)], seen(c.i + (f >= 2)))
                    for h in range(2):
                        last = act.activation(u_raw[:, f % 2, h, :], ps_u[f][:, h, :], ACT.Relu, bias=b1[:, c.wb, 2 * f + h:2 * f + h + 1])
                    last.then_inc(relu_done[f], 1)

            loop(act, (0, take_T), (1, relu))


def collect(nc, io, dram, keep, NT, out):
    LARGEST = 3.4028234663852886e38
    with ExitStack() as ctx:
        k = Kit(nc, ctx, "coll")
        x1, got = k.sb("x1", [P, NT, D]), k.sb("got", [P, NT, D])
        bound, real, finite, clean = (k.sb(n, [P, 2, D], dt) for n, dt in (("bound", F32), ("real", F32), ("finite", F32), ("clean", F32)))
        n = {name: k.sem(name) for name in ("x1_loaded", "stored")}
        gathered = [k.gather_sem(f"gathered{i}") for i in range(NT // 2)]
        done = k.sem("done")
        ready = k.sem("ready")
        block = k.start()
        x1_v = dram["x1"].rearrange("(t p) d -> p t d", p=P)
        out_v = out.rearrange("(t p) d -> p t d", p=P)

        @block.sync
        def _(sp):
            sp.dma_start(x1[:], x1_v).then_inc(n["x1_loaded"], 16)
            with sp.Fori(0, NT // 2, 1) as g:
                sp.wait_ge(ready, seen(g + 1))
                sp.dma_start(out_v[:, ds(2 * g, 2), :], x1[:, ds(2 * g, 2), :]).then_inc(n["stored"], 16)
            sp.wait_ge(n["stored"], seen(NT // 2 * 16))

        @block.gpsimd
        def _(pool):
            for t in range(NT):
                pool.indirect_dma_start(got[:, t, :], None, dram["ybuf"], bass.IndirectOffsetOnAxis(ap=keep["slot"][:, t:t + 1], axis=0)).then_inc(gathered[t // 2], 16)

        @block.vector
        def _(dve):
            c = Chain(dve, done)
            link = c.link
            dve.wait_ge(n["x1_loaded"], seen(16))
            for g in range(NT // 2):
                rows = got[:, 2 * g:2 * g + 2, :]
                dve.wait_ge(gathered[g], 32)
                link(dve.tensor_tensor(rows, rows, keep["weight"][:, 2 * g:2 * g + 2, None].broadcast_to([P, 2, D]), ALU.mult))
                c.step(dve.tensor_scalar(bound[:], rows, 1.0e4, -1.0e4, ALU.min, ALU.max))
                c.step(dve.tensor_tensor(real[:], rows, rows, ALU.is_equal))
                c.step(dve.tensor_scalar(finite[:], rows, 0.0, 0.0, ALU.mult, ALU.is_equal))
                link(dve.memset(clean[:], 0.0))
                link(dve.copy_predicated(clean[:], real[:].bitcast(U32), bound[:]))
                link(dve.copy_predicated(clean[:], finite[:].bitcast(U32), rows))
                link(dve.tensor_tensor(x1[:, 2 * g:2 * g + 2, :], x1[:, 2 * g:2 * g + 2, :], clean[:], ALU.add))
                dve.sem_inc(ready, 1)


def graph_block_kernel(nc, io, out):
    N = io["x"].shape[0]
    NT = N // P
    E = io["src"].shape[0]
    NX = io["L0_ffn_gate_w"].shape[1]
    CAP = max(1, -(-5 * N // (4 * NX)))
    TILE = -(-CAP // 8)
    SLOTS = 8 * TILE
    plan_steps = -(-(E // 512 + NT) // 110) * 110

    def scratch(name, shape, dt=F32):
        return nc.dram_tensor(name, shape, dt, kind="Internal").ap()

    dram = {
        "src": io["src"].bitcast(U32).rearrange("(p c) -> p c", p=P),
        "res": scratch("res_dram", (1, N, D)),
        "mix_out": scratch("mix_dram", (N, D)),
        "node_rows": scratch("node_rows_dram", (N, D + HEADS)),
        "a_edge": scratch("a_edge_dram", (P, E // P * HEADS)),
        "scan": scratch("scan_dram", (E, HEADS)),
        "carry": scratch("carry_dram", (P, HEADS)),
        "rowptr": scratch("rowptr_dram", (N + 1,)),
        "plan": scratch("plan_dram", (2, plan_steps), I32),
        "edge_rows": scratch("edge_rows_dram", (E + 512, D + HEADS)),
        "dst_pad": scratch("dst_pad_dram", (E + 512,), U16),
        "x_plus_xn": scratch("x_plus_xn_dram", (N, D)),
        "x1": scratch("x1_dram", (N, D)),
        "buf": scratch("buf_dram", (NX * SLOTS, D)),
        "ybuf": scratch("ybuf_dram", (NX * SLOTS, D)),
        "hT": scratch("hT_dram", (NT // 2, 128, KC, 2 * P)),
    }
    with ExitStack() as ctx:
        k = Kit(nc, ctx, "keep")
        keep = {
            "ident": k.sb("ident", [128, 128]),
            "a_node": k.sb("a_node", [P, NT, 2 * HEADS]),
            "m_node": k.sb("m_node", [P, NT, HEADS]),
            "pair_parts": k.sb("pair_parts", [P, NT, 3, 2 * HEADS], BF16),
            "plan": k.sb("plan", [4, 2, plan_steps + 8], I32),
            "slot": k.sb("slot", [P, NT], U32),
            "weight": k.sb("weight", [P, NT]),
        }
        prepare(nc, io, dram, keep, NT)
        mix(nc, io, dram, keep, NT)
        segments(nc, io, dram, keep, NT, plan_steps)
        with ExitStack() as span:
            held = Kit(nc, span, "graph")
            keep["acc"] = held.sb("acc", [P, NT, D + HEADS])
            keep["self"] = held.sb("self", [P, NT, D + HEADS])
            aggregate(nc, io, dram, keep, NT, plan_steps)
            combine_and_route(nc, io, dram, keep, NT, CAP, SLOTS)
        experts(nc, io, dram, keep, TILE, SLOTS)
        collect(nc, io, dram, keep, NT, out)


def kernel(**inputs):
    import numpy as _np
    import concourse.bacc as _bacc
    from concourse import mybir as _mybir
    from concourse.bass_utils import run_bass_kernel_spmd as _run

    nc = _bacc.Bacc("TRN2", target_bir_lowering=False, num_devices=1)
    arrays, args = {}, {}
    for name, a in inputs.items():
        a = _np.ascontiguousarray(a)
        arrays[f"in_{name}_dram"] = a
        args[name] = nc.dram_tensor(f"in_{name}_dram", a.shape, _mybir.dt.from_np(a.dtype), kind="ExternalInput").ap()
    out = nc.dram_tensor("out_0_dram", inputs["x"].shape, _mybir.dt.float32, kind="ExternalOutput").ap()
    graph_block_kernel(nc, args, out)
    r = _run(nc, [arrays], core_ids=[0])
    return r.results[0]["out_0_dram"]
```
